# Optimizing a Trainium2 kernel written in Bass

```python
import numpy as np
import jax
import jax.numpy as jnp

def _softmax(x, axis=-1):
    return jax.nn.softmax(x, axis=axis)

def _gelu(x):
    return jax.nn.gelu(x, approximate=True)

def _silu(x):
    return jax.nn.silu(x)

def _sigmoid(x):
    return jax.nn.sigmoid(x)

def _layernorm(x, axis=-1, eps=1e-05):
    m = jnp.mean(x, axis=axis, keepdims=True)
    v = jnp.var(x, axis=axis, keepdims=True)
    return (x - m) / jnp.sqrt(v + eps)

def _scatter_add(tgt, idx, src, axis=0):
    return tgt.at[idx].add(src)

def _segment_sum(src, seg, n):
    return jax.ops.segment_sum(src, seg, n)
kernel_name = 'mk_perceiver_d2_seqx_r2_3ed189'

def setup_inputs(seed: int=0):
    np.random.seed(seed)
    _w = jnp.asarray

    def _rec_inputs():
        import jax
        import jax.numpy as jnp
        _rk = jax.random.key(seed)
        x = -0.0005146 + 1 * jax.random.normal(jax.random.fold_in(_rk, 1), (8, 64, 512), jnp.float32)
        _lenS = 64 - jax.random.randint(jax.random.fold_in(_rk, 7), (8,), 0, max(1, 64 // 4) + 1, jnp.int32)
        _lenS2 = 1601 - jax.random.randint(jax.random.fold_in(_rk, 8), (8,), 0, max(1, 1601 // 4) + 1, jnp.int32)
        _ctx_768P = jax.random.normal(jax.random.fold_in(_rk, 11), (8, 16, 384), jnp.float32)
        _ctx_768c = jax.random.dirichlet(jax.random.fold_in(_rk, 511), 0.3 * jnp.ones((16,), jnp.float32), (8, 1601))
        _ctx_768t = jnp.einsum('bsk,bkd->bsd', _ctx_768c, _ctx_768P)
        _ctx_768t = _ctx_768t * jax.lax.rsqrt(jnp.mean(jnp.square(_ctx_768t)) + 1e-12) * 0.953939
        ctx_768 = -0.00040386 + 0.999972 * (_ctx_768t + 0.3 * jax.random.normal(jax.random.fold_in(_rk, 611), (8, 1601, 384), jnp.float32))
        _validS = jnp.arange(64)[None, :] < _lenS[:, None]
        _validS2 = jnp.arange(1601)[None, :] < _lenS2[:, None]
        _causal = jnp.tril(jnp.ones((64, 64), dtype=bool))
        mask_BxS2_bk0 = jnp.logical_not(jnp.broadcast_to(_validS2[:, :], (8, 1601)))
        mask_BxS_bf1 = jnp.ones((8, 64), dtype=bool)
        mask_BxS2_bf1 = jnp.ones((8, 1601), dtype=bool)
        return (x, ctx_768, mask_BxS2_bk0, mask_BxS_bf1, mask_BxS2_bf1)
    x, ctx_768, mask_BxS2_bk0, mask_BxS_bf1, mask_BxS2_bf1 = _rec_inputs()

    def _L0_xattn_setup():
        import jax, jax.numpy as jnp
        import numpy as np
        DIM_IN, DIM_LAT, DIM_HEAD = (384, 512, 64)
        INNER = max(DIM_LAT, DIM_IN)
        HEADS = INNER // DIM_HEAD
        SCALE = DIM_HEAD ** (-0.5)
        RMS_EPS = 1e-08
        LN_EPS = 1e-05

        def layernorm(x, g, b):
            mu = jnp.mean(x, axis=-1, keepdims=True)
            var = jnp.mean((x - mu) ** 2, axis=-1, keepdims=True)
            return (x - mu) * jax.lax.rsqrt(var + LN_EPS) * g + b

        def rmsnorm(x, gamma):
            norm = jnp.sqrt(jnp.sum(x * x, axis=-1, keepdims=True)) * x.shape[-1] ** (-0.5)
            return x / jnp.maximum(norm, RMS_EPS) * gamma
        key = jax.random.key(seed)
        ks = jax.random.split(key, 12)
        b, n, m = (4, 2048, 256)
        x = jax.random.normal(ks[0], (b, n, DIM_IN), jnp.float32)
        latents = jax.random.normal(ks[1], (b, m, DIM_LAT), jnp.float32)
        mask = jax.random.randint(ks[2], (b, n), 0, 2).astype(bool)
        s = lambda k, sh, fan: jax.random.normal(k, sh, jnp.float32) * fan ** (-0.5)
        return {'x': x, 'latents': latents, 'mask': mask, 'ln_x_g': jnp.ones((DIM_IN,), jnp.float32), 'ln_x_b': jnp.zeros((DIM_IN,), jnp.float32), 'ln_l_g': jnp.ones((DIM_LAT,), jnp.float32), 'ln_l_b': jnp.zeros((DIM_LAT,), jnp.float32), 'qn_g': jnp.ones((DIM_HEAD,), jnp.float32), 'kn_g': jnp.ones((DIM_HEAD,), jnp.float32), 'Wq': s(ks[3], (INNER, DIM_LAT), DIM_LAT), 'Wkv': s(ks[4], (2 * INNER, DIM_IN), DIM_IN), 'Wlkv': s(ks[5], (2 * INNER, DIM_LAT), DIM_LAT), 'Wo': s(ks[6], (DIM_LAT, INNER), INNER), 'bo': jnp.zeros((DIM_LAT,), jnp.float32)}
    _L0_xattn_all = _L0_xattn_setup()
    _L0_xattn_in = {k: v for k, v in _L0_xattn_all.items() if k in ('ln_x_g', 'ln_x_b', 'ln_l_g', 'ln_l_b', 'qn_g', 'kn_g', 'Wq', 'Wkv', 'Wlkv', 'Wo', 'bo')}
    del _L0_xattn_all

    def _L0_attn_setup():
        import jax, jax.numpy as jnp
        import numpy as np
        B, S, D, H = (2, 1024, 512, 16)
        HD = D // H
        key = jax.random.key(seed)
        k0, k1, k2 = jax.random.split(key, 3)
        return {'x': jax.random.normal(k0, (B, S, D), jnp.float32), 'qkv_w': jax.random.normal(k1, (D, 3 * D), jnp.float32) / np.sqrt(D).astype(np.float32), 'qkv_b': jnp.zeros((3 * D,), jnp.float32), 'out_w': jax.random.normal(k2, (D, D), jnp.float32) / np.sqrt(D).astype(np.float32), 'out_b': jnp.zeros((D,), jnp.float32)}
    _L0_attn_all = _L0_attn_setup()
    _L0_attn_in = {k: v for k, v in _L0_attn_all.items() if k in ('qkv_w', 'qkv_b', 'out_w', 'out_b')}
    del _L0_attn_all

    def _L0_ffn_setup():
        import jax, jax.numpy as jnp
        import numpy as np
        B, S, H, I, E_ROUTED, TOP_K = (8, 1024, 512, 1024, 8, 2)

        def _expert(x, Wg, Wu, Wd):
            return jax.nn.silu(x @ Wg.T) * (x @ Wu.T) @ Wd.T
        key = jax.random.key(seed)
        ks = jax.random.split(key, 9)
        s = 0.02
        return {'x': jax.random.normal(ks[0], (B, S, H), dtype=jnp.float32), 'Wg_s': jax.random.normal(ks[1], (I, H), dtype=jnp.float32) * s, 'Wu_s': jax.random.normal(ks[2], (I, H), dtype=jnp.float32) * s, 'Wd_s': jax.random.normal(ks[3], (H, I), dtype=jnp.float32) * s, 'Wg': jax.random.normal(ks[4], (E_ROUTED, I, H), dtype=jnp.float32) * s, 'Wu': jax.random.normal(ks[5], (E_ROUTED, I, H), dtype=jnp.float32) * s, 'Wd': jax.random.normal(ks[6], (E_ROUTED, H, I), dtype=jnp.float32) * s, 'Wr': jax.random.normal(ks[7], (E_ROUTED, H), dtype=jnp.float32) * s, 'rb': jnp.zeros((E_ROUTED,), dtype=jnp.float32)}
    _L0_ffn_all = _L0_ffn_setup()
    _L0_ffn_in = {k: v for k, v in _L0_ffn_all.items() if k in ('Wg_s', 'Wu_s', 'Wd_s', 'Wg', 'Wu', 'Wd', 'Wr', 'rb')}
    del _L0_ffn_all

    def _L1_xattn_setup():
        import jax, jax.numpy as jnp
        import numpy as np
        B, T, DT, G, DV = (16, 256, 512, 288, 384)
        H, DH = (4, 32)
        INNER = H * DH
        HID = 4 * DT
        N_STATE = 64
        K_TOP = 32

        def layernorm(x, g, b, eps=1e-05):
            m = x.mean(-1, keepdims=True)
            v = x.var(-1, keepdims=True)
            return (x - m) * jax.lax.rsqrt(v + eps) * g + b

        def s4d(x, log_dt, A_re, A_im, C_re, C_im, D_skip):
            Bb, L, D = x.shape
            dt = jnp.exp(log_dt)
            A = A_re + 1j * A_im
            C = C_re + 1j * C_im
            dtA = dt[:, None] * A
            dC = C * (jnp.exp(dtA) - 1.0) / A
            powers = jnp.exp(dtA[:, :, None] * jnp.arange(L))
            K = 2.0 * jnp.einsum('dn,dnl->dl', dC, powers).real
            n = 2 * L
            Kf = jnp.fft.rfft(K, n=n, axis=-1)
            xf = jnp.fft.rfft(x, n=n, axis=1)
            y = jnp.fft.irfft(xf * Kf.T[None], n=n, axis=1)[:, :L]
            return y + x * D_skip
        key = jax.random.key(seed)
        ks = jax.random.split(key, 16)
        s = 0.02
        inp = {'x_text': jax.random.normal(ks[0], (B, T, DT), jnp.float32), 'x_vision': jax.random.normal(ks[1], (B, G, DV), jnp.float32), 'text_mask': jnp.ones((B, T), bool), 'vision_mask': jnp.ones((B, G), bool), 'Wq': jax.random.normal(ks[2], (DT, INNER), jnp.float32) * s, 'Wk': jax.random.normal(ks[3], (DV, INNER), jnp.float32) * s, 'Wv': jax.random.normal(ks[4], (DV, DT), jnp.float32) * s, 'W_film_in': jax.random.normal(ks[5], (DT, 2 * DT), jnp.float32) * s, 'b_film_in': jnp.zeros((2 * DT,), jnp.float32), 'W_film_out': jax.random.normal(ks[6], (DT, 2 * DT), jnp.float32) * s, 'b_film_out': jnp.zeros((2 * DT,), jnp.float32), 'g_norm_in': jnp.ones((DT,), jnp.float32), 'b_norm_in': jnp.zeros((DT,), jnp.float32), 'g_norm_out': jnp.ones((DT,), jnp.float32), 'b_norm_out': jnp.zeros((DT,), jnp.float32), 'g_ffn': jnp.ones((DT,), jnp.float32), 'b_ffn': jnp.zeros((DT,), jnp.float32), 'W1': jax.random.normal(ks[7], (DT, HID), jnp.float32) * s, 'b1': jnp.zeros((HID,), jnp.float32), 'W2': jax.random.normal(ks[8], (HID, DT), jnp.float32) * s, 'b2': jnp.zeros((DT,), jnp.float32), 'log_dt': jnp.log(0.001) + jax.random.uniform(ks[9], (DT,), jnp.float32) * (jnp.log(0.1) - jnp.log(0.001)), 'A_re': -0.5 * jnp.ones((DT, N_STATE), jnp.float32), 'A_im': jnp.tile(jnp.pi * jnp.arange(N_STATE, dtype=jnp.float32), (DT, 1)), 'C_re': jax.random.normal(ks[10], (DT, N_STATE), jnp.float32) * 0.5 ** 0.5, 'C_im': jax.random.normal(ks[11], (DT, N_STATE), jnp.float32) * 0.5 ** 0.5, 'D_skip': jax.random.normal(ks[12], (DT,), jnp.float32), 'mod_gate': jnp.array(0.5, jnp.float32)}
        return inp
    _L1_xattn_all = _L1_xattn_setup()
    _L1_xattn_in = {k: v for k, v in _L1_xattn_all.items() if k in ('Wq', 'Wk', 'Wv', 'W_film_in', 'b_film_in', 'W_film_out', 'b_film_out', 'g_norm_in', 'b_norm_in', 'g_norm_out', 'b_norm_out', 'g_ffn', 'b_ffn', 'W1', 'b1', 'W2', 'b2', 'log_dt', 'A_re', 'A_im', 'C_re', 'C_im', 'D_skip', 'mod_gate')}
    del _L1_xattn_all

    def _L1_attn_setup():
        import jax, jax.numpy as jnp
        import numpy as np
        B, S, D = (2, 1024, 512)
        H = 16
        HD = D // H
        THETA = 1000.0
        SCALE = 0.02

        def _rope(t, cos, sin):
            even = t[..., ::2]
            odd = t[..., 1::2]
            return jnp.concatenate([even * cos - odd * sin, odd * cos + even * sin], axis=-1)
        key = jax.random.key(seed)
        k0, k1, k2, k3, k4 = jax.random.split(key, 5)
        x = jax.random.normal(k0, (B, S, D), dtype=jnp.float32)
        wq = SCALE * jax.random.normal(k1, (D, D), dtype=jnp.float32)
        wk = SCALE * jax.random.normal(k2, (D, HD), dtype=jnp.float32)
        wv = SCALE * jax.random.normal(k3, (D, HD), dtype=jnp.float32)
        wo = SCALE * jax.random.normal(k4, (D, D), dtype=jnp.float32)
        return {'x': x, 'wq': wq, 'wk': wk, 'wv': wv, 'wo': wo}
    _L1_attn_all = _L1_attn_setup()
    _L1_attn_in = {k: v for k, v in _L1_attn_all.items() if k in ('wq', 'wk', 'wv', 'wo')}
    del _L1_attn_all

    def _L1_ffn_setup():
        import jax, jax.numpy as jnp
        import numpy as np
        import math
        EMBED_DIM = 512
        FFN_DIM = 2048
        N_EXPERTS = 8
        TOP_K = 2
        CAP_FACTOR = 1.25
        key = jax.random.key(seed)
        k0, k1, k2, k3 = jax.random.split(key, 4)
        B, S = (4, 1024)
        x = jax.random.normal(k0, (B, S, EMBED_DIM), dtype=jnp.float32)
        Wr = jax.random.normal(k1, (EMBED_DIM, N_EXPERTS), dtype=jnp.float32) * 0.02
        W1 = jax.random.normal(k2, (N_EXPERTS, EMBED_DIM, FFN_DIM), dtype=jnp.float32) * 0.02
        W2 = jax.random.normal(k3, (N_EXPERTS, FFN_DIM, EMBED_DIM), dtype=jnp.float32) * 0.02
        return {'x': x, 'Wr': Wr, 'W1': W1, 'W2': W2}
    _L1_ffn_all = _L1_ffn_setup()
    _L1_ffn_in = {k: v for k, v in _L1_ffn_all.items() if k in ('Wr', 'W1', 'W2')}
    del _L1_ffn_all
    return {'x': x, 'ctx_768': ctx_768, 'mask_BxS2_bk0': mask_BxS2_bk0, 'mask_BxS_bf1': mask_BxS_bf1, 'mask_BxS2_bf1': mask_BxS2_bf1, 'L0_xattn_ln_x_g': _L0_xattn_in['ln_x_g'], 'L0_xattn_ln_x_b': _L0_xattn_in['ln_x_b'], 'L0_xattn_ln_l_g': _L0_xattn_in['ln_l_g'], 'L0_xattn_ln_l_b': _L0_xattn_in['ln_l_b'], 'L0_xattn_qn_g': _L0_xattn_in['qn_g'], 'L0_xattn_kn_g': _L0_xattn_in['kn_g'], 'L0_xattn_Wq': _L0_xattn_in['Wq'], 'L0_xattn_Wkv': _L0_xattn_in['Wkv'], 'L0_xattn_Wlkv': _L0_xattn_in['Wlkv'], 'L0_xattn_Wo': _L0_xattn_in['Wo'], 'L0_xattn_bo': _L0_xattn_in['bo'], 'L0_attn_qkv_w': _L0_attn_in['qkv_w'], 'L0_attn_qkv_b': _L0_attn_in['qkv_b'], 'L0_attn_out_w': _L0_attn_in['out_w'], 'L0_attn_out_b': _L0_attn_in['out_b'], 'L0_ffn_Wg_s': _L0_ffn_in['Wg_s'], 'L0_ffn_Wu_s': _L0_ffn_in['Wu_s'], 'L0_ffn_Wd_s': _L0_ffn_in['Wd_s'], 'L0_ffn_Wg': _L0_ffn_in['Wg'], 'L0_ffn_Wu': _L0_ffn_in['Wu'], 'L0_ffn_Wd': _L0_ffn_in['Wd'], 'L0_ffn_Wr': _L0_ffn_in['Wr'], 'L0_ffn_rb': _L0_ffn_in['rb'], 'L1_xattn_Wq': _L1_xattn_in['Wq'], 'L1_xattn_Wk': _L1_xattn_in['Wk'], 'L1_xattn_Wv': _L1_xattn_in['Wv'], 'L1_xattn_W_film_in': _L1_xattn_in['W_film_in'], 'L1_xattn_b_film_in': _L1_xattn_in['b_film_in'], 'L1_xattn_W_film_out': _L1_xattn_in['W_film_out'], 'L1_xattn_b_film_out': _L1_xattn_in['b_film_out'], 'L1_xattn_g_norm_in': _L1_xattn_in['g_norm_in'], 'L1_xattn_b_norm_in': _L1_xattn_in['b_norm_in'], 'L1_xattn_g_norm_out': _L1_xattn_in['g_norm_out'], 'L1_xattn_b_norm_out': _L1_xattn_in['b_norm_out'], 'L1_xattn_g_ffn': _L1_xattn_in['g_ffn'], 'L1_xattn_b_ffn': _L1_xattn_in['b_ffn'], 'L1_xattn_W1': _L1_xattn_in['W1'], 'L1_xattn_b1': _L1_xattn_in['b1'], 'L1_xattn_W2': _L1_xattn_in['W2'], 'L1_xattn_b2': _L1_xattn_in['b2'], 'L1_xattn_log_dt': _L1_xattn_in['log_dt'], 'L1_xattn_A_re': _L1_xattn_in['A_re'], 'L1_xattn_A_im': _L1_xattn_in['A_im'], 'L1_xattn_C_re': _L1_xattn_in['C_re'], 'L1_xattn_C_im': _L1_xattn_in['C_im'], 'L1_xattn_D_skip': _L1_xattn_in['D_skip'], 'L1_xattn_mod_gate': _L1_xattn_in['mod_gate'], 'L1_attn_wq': _L1_attn_in['wq'], 'L1_attn_wk': _L1_attn_in['wk'], 'L1_attn_wv': _L1_attn_in['wv'], 'L1_attn_wo': _L1_attn_in['wo'], 'L1_ffn_Wr': _L1_ffn_in['Wr'], 'L1_ffn_W1': _L1_ffn_in['W1'], 'L1_ffn_W2': _L1_ffn_in['W2']}

def reference(x, ctx_768, mask_BxS2_bk0, mask_BxS_bf1, mask_BxS2_bf1, L0_xattn_ln_x_g, L0_xattn_ln_x_b, L0_xattn_ln_l_g, L0_xattn_ln_l_b, L0_xattn_qn_g, L0_xattn_kn_g, L0_xattn_Wq, L0_xattn_Wkv, L0_xattn_Wlkv, L0_xattn_Wo, L0_xattn_bo, L0_attn_qkv_w, L0_attn_qkv_b, L0_attn_out_w, L0_attn_out_b, L0_ffn_Wg_s, L0_ffn_Wu_s, L0_ffn_Wd_s, L0_ffn_Wg, L0_ffn_Wu, L0_ffn_Wd, L0_ffn_Wr, L0_ffn_rb, L1_xattn_Wq, L1_xattn_Wk, L1_xattn_Wv, L1_xattn_W_film_in, L1_xattn_b_film_in, L1_xattn_W_film_out, L1_xattn_b_film_out, L1_xattn_g_norm_in, L1_xattn_b_norm_in, L1_xattn_g_norm_out, L1_xattn_b_norm_out, L1_xattn_g_ffn, L1_xattn_b_ffn, L1_xattn_W1, L1_xattn_b1, L1_xattn_W2, L1_xattn_b2, L1_xattn_log_dt, L1_xattn_A_re, L1_xattn_A_im, L1_xattn_C_re, L1_xattn_C_im, L1_xattn_D_skip, L1_xattn_mod_gate, L1_attn_wq, L1_attn_wk, L1_attn_wv, L1_attn_wo, L1_ffn_Wr, L1_ffn_W1, L1_ffn_W2):
    import jax
    import jax.numpy as jnp

    def _L0_xattn_ref(x, latents, mask, ln_x_g, ln_x_b, ln_l_g, ln_l_b, qn_g, kn_g, Wq, Wkv, Wlkv, Wo, bo):
        import jax, jax.numpy as jnp
        import numpy as np
        DIM_IN, DIM_LAT, DIM_HEAD = (384, 512, 64)
        INNER = max(DIM_LAT, DIM_IN)
        HEADS = INNER // DIM_HEAD
        SCALE = DIM_HEAD ** (-0.5)
        RMS_EPS = 1e-08
        LN_EPS = 1e-05

        def layernorm(x, g, b):
            mu = jnp.mean(x, axis=-1, keepdims=True)
            var = jnp.mean((x - mu) ** 2, axis=-1, keepdims=True)
            return (x - mu) * jax.lax.rsqrt(var + LN_EPS) * g + b

        def rmsnorm(x, gamma):
            norm = jnp.sqrt(jnp.sum(x * x, axis=-1, keepdims=True)) * x.shape[-1] ** (-0.5)
            return x / jnp.maximum(norm, RMS_EPS) * gamma
        b, n, _ = x.shape
        m = latents.shape[1]
        xn = layernorm(x, ln_x_g, ln_x_b)
        ln = layernorm(latents, ln_l_g, ln_l_b)
        q = ln @ Wq.T
        kv = jnp.concatenate([xn @ Wkv.T, ln @ Wlkv.T], axis=1)
        k, v = (kv[..., :INNER], kv[..., INNER:])
        split_heads = lambda t: t.reshape(t.shape[0], t.shape[1], HEADS, DIM_HEAD).transpose(0, 2, 1, 3)
        q, k, v = (split_heads(q), split_heads(k), split_heads(v))
        qn = rmsnorm(q, qn_g) * SCALE
        kn = rmsnorm(k, kn_g)
        attn = jnp.einsum('bhid,bhjd->bhij', qn, kn)
        full_mask = jnp.pad(mask, ((0, 0), (0, m)), constant_values=True)
        attn = jnp.where(full_mask[:, None, None, :], attn, -jnp.finfo(attn.dtype).max)
        attn = jax.nn.softmax(attn, axis=-1)
        out = jnp.einsum('bhij,bhjd->bhid', attn, v)
        out = out.transpose(0, 2, 1, 3).reshape(b, m, INNER)
        return out @ Wo.T + bo

    def _L0_attn_ref(x, qkv_w, qkv_b, out_w, out_b):
        import jax, jax.numpy as jnp
        import numpy as np
        B, S, D, H = (2, 1024, 512, 16)
        HD = D // H
        b, s, d = x.shape
        h, hd = (H, d // H)
        scale = 1.0 / np.sqrt(hd).astype(np.float32)
        qkv = (x @ qkv_w + qkv_b).reshape(b, s, 3, h, hd)
        q, k, v = (qkv[:, :, 0], qkv[:, :, 1], qkv[:, :, 2])
        logits = jnp.einsum('bqhd,bkhd->bhqk', q, k)
        causal_mask = jnp.triu(jnp.ones((s, s), bool), 1)
        logits = jnp.where(causal_mask, -jnp.inf, logits) * scale
        att = jax.nn.softmax(logits, axis=-1)
        out = jnp.einsum('bhqk,bkhd->bqhd', att, v).reshape(b, s, d)
        return out @ out_w + out_b

    def _L0_ffn_ref(x, Wg_s, Wu_s, Wd_s, Wg, Wu, Wd, Wr, rb):
        import jax, jax.numpy as jnp
        import numpy as np
        B, S, H, I, E_ROUTED, TOP_K = (8, 1024, 512, 1024, 8, 2)

        def _expert(x, Wg, Wu, Wd):
            return jax.nn.silu(x @ Wg.T) * (x @ Wu.T) @ Wd.T
        shared = _expert(x, Wg_s, Wu_s, Wd_s)
        logits = jnp.einsum('bsh,eh->bse', x, Wr) + rb
        probs = jax.nn.sigmoid(logits)
        scores, idx = jax.lax.top_k(probs, TOP_K)
        cw = (jax.nn.one_hot(idx, E_ROUTED, dtype=x.dtype) * scores[..., None]).sum(-2)
        out = shared
        for e in range(E_ROUTED):
            out = out + cw[..., e:e + 1] * _expert(x, Wg[e], Wu[e], Wd[e])
        return out

    def _L1_xattn_ref(x_text, x_vision, text_mask, vision_mask, Wq, Wk, Wv, W_film_in, b_film_in, W_film_out, b_film_out, g_norm_in, b_norm_in, g_norm_out, b_norm_out, g_ffn, b_ffn, W1, b1, W2, b2, log_dt, A_re, A_im, C_re, C_im, D_skip, mod_gate):
        import jax, jax.numpy as jnp
        import numpy as np
        B, T, DT, G, DV = (16, 256, 512, 288, 384)
        H, DH = (4, 32)
        INNER = H * DH
        HID = 4 * DT
        N_STATE = 64
        K_TOP = 32

        def layernorm(x, g, b, eps=1e-05):
            m = x.mean(-1, keepdims=True)
            v = x.var(-1, keepdims=True)
            return (x - m) * jax.lax.rsqrt(v + eps) * g + b

        def s4d(x, log_dt, A_re, A_im, C_re, C_im, D_skip):
            Bb, L, D = x.shape
            dt = jnp.exp(log_dt)
            A = A_re + 1j * A_im
            C = C_re + 1j * C_im
            dtA = dt[:, None] * A
            dC = C * (jnp.exp(dtA) - 1.0) / A
            powers = jnp.exp(dtA[:, :, None] * jnp.arange(L))
            K = 2.0 * jnp.einsum('dn,dnl->dl', dC, powers).real
            n = 2 * L
            Kf = jnp.fft.rfft(K, n=n, axis=-1)
            xf = jnp.fft.rfft(x, n=n, axis=1)
            y = jnp.fft.irfft(xf * Kf.T[None], n=n, axis=1)[:, :L]
            return y + x * D_skip
        Bb, Tt, D = x_text.shape
        Gg = x_vision.shape[1]
        Q = (x_text @ Wq).reshape(Bb, Tt, H, DH)
        K = (x_vision @ Wk).reshape(Bb, Gg, H, DH)
        scores = jnp.einsum('bthd,bghd->bhtg', Q, K) / np.sqrt(DH).astype(np.float32)
        scores = jnp.where(vision_mask[:, None, None, :], scores, -jnp.inf)
        topv, topi = jax.lax.top_k(scores, K_TOP)
        probs = jax.nn.softmax(topv, axis=-1)
        bi = jnp.arange(Bb)[:, None, None, None]
        hi = jnp.arange(H)[None, :, None, None]
        ti = jnp.arange(Tt)[None, None, :, None]
        attn = jnp.zeros_like(scores).at[bi, hi, ti, topi].set(probs)
        attn_mean = attn.mean(axis=1)
        V = x_vision @ Wv
        c_t = jnp.einsum('btg,bgd->btd', attn_mean, V)
        c_t = c_t * text_mask[..., None]
        x = layernorm(x_text, g_norm_in, b_norm_in)
        scale_in, shift_in = jnp.split(c_t @ W_film_in + b_film_in, 2, axis=-1)
        x = x * (1.0 + mod_gate * scale_in) + mod_gate * shift_in
        y = s4d(x, log_dt, A_re, A_im, C_re, C_im, D_skip)
        scale_out, shift_out = jnp.split(c_t @ W_film_out + b_film_out, 2, axis=-1)
        y = y * (1.0 + mod_gate * scale_out) + mod_gate * shift_out
        xt = x_text + y
        h = layernorm(xt, g_ffn, b_ffn)
        h = jax.nn.gelu(h @ W1 + b1, approximate=False) @ W2 + b2
        xt = xt + h
        return layernorm(xt, g_norm_out, b_norm_out)

    def _L1_attn_ref(x, wq, wk, wv, wo):
        import jax, jax.numpy as jnp
        import numpy as np
        B, S, D = (2, 1024, 512)
        H = 16
        HD = D // H
        THETA = 1000.0
        SCALE = 0.02

        def _rope(t, cos, sin):
            even = t[..., ::2]
            odd = t[..., 1::2]
            return jnp.concatenate([even * cos - odd * sin, odd * cos + even * sin], axis=-1)
        b, s, d = x.shape
        freqs = 1.0 / THETA ** (jnp.arange(0, HD, 2, dtype=jnp.float32) / HD)
        ang = jnp.arange(s, dtype=jnp.float32)[:, None] * freqs[None, :]
        cos, sin = (jnp.cos(ang), jnp.sin(ang))
        q = (x @ wq.T).reshape(b, s, H, HD).transpose(0, 2, 1, 3)
        k = x @ wk
        v = x @ wv
        q = _rope(q, cos[None, None], sin[None, None])
        k = _rope(k, cos[None], sin[None])
        scores = jnp.einsum('bhqd,bkd->bhqk', q, k) / np.float32(np.sqrt(HD))
        causal = jnp.triu(jnp.ones((s, s), dtype=bool), 1)
        scores = jnp.where(causal[None, None], -jnp.inf, scores)
        w = jax.nn.softmax(scores, axis=-1)
        out = jnp.einsum('bhqk,bkd->bhqd', w, v)
        out = out.transpose(0, 2, 1, 3).reshape(b, s, d)
        return out @ wo.T

    def _L1_ffn_ref(x, Wr, W1, W2):
        import jax, jax.numpy as jnp
        import numpy as np
        import math
        EMBED_DIM = 512
        FFN_DIM = 2048
        N_EXPERTS = 8
        TOP_K = 2
        CAP_FACTOR = 1.25
        B, S, D = x.shape
        t = B * S
        xf = x.reshape(t, D)
        probs = jax.nn.softmax(xf.astype(jnp.float32) @ Wr, axis=-1)
        topk_probs, topk_experts = jax.lax.top_k(probs, TOP_K)
        cap = max(math.ceil(t * TOP_K * CAP_FACTOR / N_EXPERTS), 1)
        y = jnp.zeros_like(xf)
        for e in range(N_EXPERTS):
            mask = topk_experts == e
            gate = jnp.sum(jnp.where(mask, topk_probs, 0.0), axis=-1)
            has = jnp.any(mask, axis=-1)
            g_masked = jnp.where(has, gate, -jnp.inf)
            vals, idx = jax.lax.top_k(g_masked, cap)
            g = jnp.where(jnp.isfinite(vals), vals, 0.0)
            xe = xf[idx]
            h = jax.nn.relu(xe @ W1[e]) @ W2[e]
            y = y.at[idx].add(g[:, None] * h)
        return y.reshape(B, S, D)
    x = x + _L0_xattn_ref(ctx_768, _layernorm(x, axis=-1), mask_BxS2_bk0, L0_xattn_ln_x_g, L0_xattn_ln_x_b, L0_xattn_ln_l_g, L0_xattn_ln_l_b, L0_xattn_qn_g, L0_xattn_kn_g, L0_xattn_Wq, L0_xattn_Wkv, L0_xattn_Wlkv, L0_xattn_Wo, L0_xattn_bo)
    x = x + _L0_attn_ref(_layernorm(x, axis=-1), L0_attn_qkv_w, L0_attn_qkv_b, L0_attn_out_w, L0_attn_out_b)
    x = x + _L0_ffn_ref(_layernorm(x, axis=-1), L0_ffn_Wg_s, L0_ffn_Wu_s, L0_ffn_Wd_s, L0_ffn_Wg, L0_ffn_Wu, L0_ffn_Wd, L0_ffn_Wr, L0_ffn_rb)
    x = x + _L1_xattn_ref(_layernorm(x, axis=-1), ctx_768, mask_BxS_bf1, mask_BxS2_bf1, L1_xattn_Wq, L1_xattn_Wk, L1_xattn_Wv, L1_xattn_W_film_in, L1_xattn_b_film_in, L1_xattn_W_film_out, L1_xattn_b_film_out, L1_xattn_g_norm_in, L1_xattn_b_norm_in, L1_xattn_g_norm_out, L1_xattn_b_norm_out, L1_xattn_g_ffn, L1_xattn_b_ffn, L1_xattn_W1, L1_xattn_b1, L1_xattn_W2, L1_xattn_b2, L1_xattn_log_dt, L1_xattn_A_re, L1_xattn_A_im, L1_xattn_C_re, L1_xattn_C_im, L1_xattn_D_skip, L1_xattn_mod_gate)
    x = x + _L1_attn_ref(_layernorm(x, axis=-1), L1_attn_wq, L1_attn_wk, L1_attn_wv, L1_attn_wo)
    x = x + _L1_ffn_ref(_layernorm(x, axis=-1), L1_ffn_Wr, L1_ffn_W1, L1_ffn_W2)
    return x

_drawn_inputs = setup_inputs


def setup_inputs(seed=0):
    import zlib

    import numpy as np

    out = dict(_drawn_inputs(seed))
    spreads = {'L0_xattn_ln_x_g': (1.0, 0.2),
     'L0_xattn_ln_x_b': (0.0, 0.1),
     'L0_xattn_ln_l_g': (1.0, 0.2),
     'L0_xattn_ln_l_b': (0.0, 0.1),
     'L0_xattn_qn_g': (1.0, 0.563),
     'L0_xattn_kn_g': (1.0, 0.587),
     'L0_xattn_bo': (0.0, 0.1),
     'L0_attn_qkv_b': (0.0, 0.1),
     'L0_attn_out_b': (0.0, 0.1),
     'L0_ffn_rb': (0.0, 0.353),
     'L1_xattn_b_film_in': (0.0, 0.282),
     'L1_xattn_b_film_out': (0.0, 0.307),
     'L1_xattn_g_norm_in': (1.0, 0.2),
     'L1_xattn_b_norm_in': (0.0, 0.1),
     'L1_xattn_g_norm_out': (1.0, 0.2),
     'L1_xattn_b_norm_out': (0.0, 0.1),
     'L1_xattn_g_ffn': (1.0, 0.6),
     'L1_xattn_b_ffn': (0.0, 0.8),
     'L1_xattn_b1': (0.0, 0.486),
     'L1_xattn_b2': (0.0, 0.1),
     'L1_xattn_A_re': (-0.5, 0.6)}
    factors = {'L1_attn_wq': 8.0, 'L1_attn_wk': 8.0}
    for name, (base, spread) in spreads.items():
        noise = np.random.default_rng([zlib.crc32(name.encode()), seed]).standard_normal(out[name].shape)
        drawn = base * np.exp(spread * noise) if base else spread * noise
        out[name] = jnp.asarray(drawn.astype(out[name].dtype))
    for name, factor in factors.items():
        out[name] = (out[name] * factor).astype(out[name].dtype)
    return out
```

```python
from contextlib import ExitStack

import numpy as np

import concourse.bass as bass
from concourse import mybir

ALU = mybir.AluOpType
ACT = mybir.ActivationFunctionType
AXX = mybir.AxisListType.X
F32 = mybir.dt.float32
BF16 = mybir.dt.bfloat16
U8 = mybir.dt.uint8

P = 128
NB, SEQ, D = 8, 64, 512
TOK = NB * SEQ
NT = TOK // P
KD = D // P
CTX, DC = 1601, 384
KC = DC // P
CFULL = CTX // P
CLAST = CTX - CFULL * P
CT = CFULL + 1
KEYS = CTX + SEQ
EPS = 1e-5
MASKED = -1e30
FIRST = 1


class Steps:

    def __init__(self, eng, sem, base=0):
        self.eng, self.sem, self.n, self.base = eng, sem, 0, base

    def did(self, ins):
        ins.then_inc(self.sem, 1)
        self.n += 1

    def wait(self):
        self.eng.wait_ge(self.sem, self.base + self.n)


def chunked(ap, k):
    return ap.rearrange("p (k n) -> p k n", k=k)


def rows(vec, n=None):
    return vec.partition_broadcast(P)


class Core:

    def __init__(self, nc, ctx, dram, out, debug):
        self.nc, self.dram, self.out, self.debug = nc, dram, out, debug
        self.ident = ctx.enter_context(nc.sbuf_tensor("ident", [P, P], F32))
        self.eps = ctx.enter_context(nc.sbuf_tensor("eps", [P, 1], F32))
        self.zero = ctx.enter_context(nc.sbuf_tensor("zero", [P, 1, 1], F32))
        self.kern = ctx.enter_context(nc.sbuf_tensor("kern", [P, KD, SEQ], F32))
        self.x = ctx.enter_context(nc.sbuf_tensor("x", [P, NT, D], F32))
        self.hT = ctx.enter_context(nc.sbuf_tensor("hT", [P, KD, TOK], F32))
        self.hn = ctx.enter_context(nc.sbuf_tensor("hn", [P, NT, D], F32))


def tokens(dram3):
    return dram3.rearrange("b s d -> (b s) d").rearrange("(t p) d -> p t d", p=P)


class Stage:

    def __init__(self, nc, name):
        self.nc, self.name, self.ctx, self.sems = nc, name, ExitStack(), []

    def __enter__(self):
        self.ctx.__enter__()
        return self

    def __exit__(self, *a):
        self.ctx.__exit__(*a)
        if self.sems and a[0] is None:
            self.nc.clear_and_free_semaphores(self.sems)
            self.nc.all_engine_barrier()

    def sb(self, name, shape, dt=F32):
        return self.ctx.enter_context(self.nc.sbuf_tensor(f"{self.name}_{name}", shape, dt))

    def ps(self, name, shape, dt=F32):
        return self.ctx.enter_context(self.nc.psum_tensor(f"{self.name}_{name}", shape, dt))

    def sem(self, name):
        self.sems.append(self.nc.alloc_semaphore(f"{self.name}_{name}"))
        return self.sems[-1]

    def block(self):
        return self.ctx.enter_context(self.nc.Block())


def restart(eng, sem):
    eng.nop(nofuse=True)
    eng.sem_clear(sem)


class Norm:

    def __init__(self, s, n=NT, name="norm"):
        self.n = n
        self.stats = s.sb(f"{name}_stats", [P, n, 6])
        self.mv = s.sb(f"{name}_mv", [P, n, 2])
        self.rstd = s.sb(f"{name}_rstd", [P, n])
        self.measured, self.rooted = s.sem(f"{name}_measured"), s.sem(f"{name}_rooted")
        self.normed = s.sem(f"{name}_normed")
        self.own, self.inverted = s.sem(f"{name}_own"), s.sem(f"{name}_inverted")

    def on_vector(self, dve, src, dst, turn=0):
        n = self.n
        for t in range(n):
            dve.bn_stats(self.stats[:, t, :], src[:, t, :]).then_inc(self.own, 1)
        dve.wait_ge(self.own, n * (turn + 1))
        for t in range(n):
            dve.bn_aggr(self.mv[:, t, :], self.stats[:, t, :]).then_inc(self.measured, 1)
        dve.wait_ge(self.rooted, turn + 1)
        dve.reciprocal(self.rstd[:], self.rstd[:]).then_inc(self.inverted, 1)
        dve.wait_ge(self.inverted, turn + 1)
        for t in range(n):
            dve.tensor_scalar(dst[:, t, :], src[:, t, :], self.mv[:, t, 0:1], self.rstd[:, t:t + 1],
                              ALU.subtract, ALU.mult).then_inc(self.normed, 1)
        dve.wait_ge(self.normed, n * (turn + 1))

    def on_scalar(self, act, eps, turn=0):
        act.wait_ge(self.measured, self.n * (turn + 1))
        act.activation(self.rstd[:], self.mv[:, :, 1], ACT.Sqrt, bias=eps).then_inc(self.rooted, 1)


def scale_by_length(dve, own, out, heads, length):
    own.did(dve.reciprocal(length, length))
    own.wait()
    m, n = length.shape
    return dve.scalar_tensor_tensor(out=out, in0=length.unsqueeze(2).to_broadcast([m, n, 64]), scalar=1 / 8e-8,
                                    in1=heads, op0=ALU.min, op1=ALU.mult)


def transpose_tokens(pe, turned_psum, src, ident, ready, filled, drained=None, n=NT):
    pe.wait_ge(*ready)
    for t in range(n):
        if drained is not None and t >= 2:
            pe.wait_ge(drained, t - 1)
        for k in range(KD):
            last = pe.transpose(turned_psum[t % 2][:, k, :], src[:, t, k * P:(k + 1) * P], ident)
        last.then_inc(filled, 1)


def xattn0_queries(g, q_T, kl_T):
    nc, d = g.nc, g.dram
    with Stage(nc, "a1") as s:
        wq = s.sb("wq", [P, KD, D])
        wk = s.sb("wk", [P, KD, D])
        gain = s.sb("gain", [P, KD])
        bias = s.sb("bias", [P, KD])
        qg = s.sb("qg", [P, SEQ])
        kg = s.sb("kg", [P, SEQ])
        qk = s.sb("qk", [P, SEQ])
        norm = Norm(s)
        sq = s.sb("sq", [P, 2, D])
        ss = s.sb("ss", [P, 2, 8])
        length = s.sb("length", [P, 2, 8])
        heads = s.sb("heads", [P, 2, D])
        turned = [s.ps(f"turned{i}", [P, KD, P]) for i in range(2)]
        proj = [s.ps(f"proj{i}", [P, D]) for i in range(2)]
        back = [s.ps(f"back{i}", [P, KD, P]) for i in range(2)]
        w_in = s.sem("w_in")
        dve_own, gains_made = s.sem("dve_own"), s.sem("gains_made")
        summed, rooted = s.sem("summed"), s.sem("rooted")
        turned_full, turned_out = s.sem("turned_full"), s.sem("turned_out")
        proj_full, squared, heads_made = s.sem("proj_full"), s.sem("squared"), s.sem("heads_made")
        back_full, back_out = s.sem("back_full"), s.sem("back_out")
        block = s.block()

        @block.sync
        def _(sp):
            for ap, name in ((wq, "L0_xattn_Wq"), (wk, "L0_xattn_Wlk")):
                sp.dma_start(ap[:], d[name]).then_inc(w_in, 16)
            sp.dma_start(gain[:], d["L0_xattn_ln_l_g"]).then_inc(w_in, 16)
            sp.dma_start(bias[:], d["L0_xattn_ln_l_b"]).then_inc(w_in, 16)
            sp.dma_start(qg[:], rows(d["L0_xattn_qn_g"])).then_inc(w_in, 16)
            sp.dma_start(kg[:], rows(d["L0_xattn_kn_g"])).then_inc(w_in, 16)

        @block.vector
        def _(dve):
            own = Steps(dve, dve_own)
            norm.on_vector(dve, g.x, g.hn)
            norm.on_vector(dve, g.hn, g.hn, 1)
            dve.wait_ge(w_in, 96)
            dve.scalar_tensor_tensor(out=qk[:], in0=qg[:], scalar=8.0, in1=kg[:], op0=ALU.mult,
                                     op1=ALU.mult).then_inc(gains_made, 1)
            dve.wait_ge(gains_made, 1)
            for t in range(NT):
                dve.wait_ge(turned_full, t + 1)
                for k in range(KD):
                    last = dve.tensor_scalar(g.hT[:, k, t * P:(t + 1) * P], turned[t % 2][:, k, :],
                                             gain[:, k:k + 1], bias[:, k:k + 1], ALU.mult, ALU.add)
                last.then_inc(turned_out, 1)
            for n in range(2 * NT):
                dve.wait_ge(squared, n + 1)
                if n >= 2:
                    dve.wait_ge(back_full, n - 1)
                dve.tensor_reduce(ss[:, n % 2, :], sq[:, n % 2, :].rearrange("p (h c) -> p h c", h=8),
                                  AXX, ALU.add).then_inc(summed, 1)
                dve.wait_ge(rooted, n + 1)
                h = heads[:, n % 2, :].rearrange("p (h c) -> p h c", h=8)
                ins = scale_by_length(dve, own, h, proj[n % 2][:].rearrange("p (h c) -> p h c", h=8),
                                      length[:, n % 2, :])
                if n < NT:
                    own.did(ins)
                    own.wait()
                    ins = dve.tensor_tensor(h, h, qk[:].unsqueeze(1).to_broadcast([P, 8, 64]), ALU.mult)
                ins.then_inc(heads_made, 1)

        def put_back(act, n):
            act.wait_ge(back_full, n + 1)
            dst = q_T if n < NT else kl_T
            t = n % NT
            act.activation(dst[:, :, t * P:(t + 1) * P], back[n % 2][:], ACT.Copy).then_inc(back_out, 1)

        @block.scalar
        def _(act):
            norm.on_scalar(act, g.eps[:])
            norm.on_scalar(act, g.eps[:], 1)
            for n in range(2 * NT):
                act.wait_ge(proj_full, n + 1)
                if n >= 2:
                    act.wait_ge(heads_made, n - 1)
                act.activation(sq[:, n % 2, :], proj[n % 2][:], ACT.Square).then_inc(squared, 1)
                act.wait_ge(summed, n + 1)
                act.activation(length[:, n % 2, :], ss[:, n % 2, :], ACT.Sqrt).then_inc(rooted, 1)
                if n >= 1:
                    put_back(act, n - 1)
            put_back(act, 2 * NT - 1)

        @block.tensor
        def _(pe):
            transpose_tokens(pe, turned, g.hn, g.ident[:], (norm.normed, 2 * NT), turned_full, turned_out)
            pe.wait_ge(turned_out, NT)
            for n in range(2 * NT + 1):
                if n < 2 * NT:
                    w, t = (wq, n) if n < NT else (wk, n - NT)
                    if n >= 2:
                        pe.wait_ge(heads_made, n - 1)
                    for k in range(KD):
                        last = pe.matmul(proj[n % 2][:], g.hT[:, k, t * P:(t + 1) * P], w[:, k, :],
                                         start=(k == 0), stop=(k == KD - 1))
                    last.then_inc(proj_full, 1)
                if n >= 1:
                    m = n - 1
                    pe.wait_ge(heads_made, m + 1)
                    if m >= 2:
                        pe.wait_ge(back_out, m - 1)
                    for k in range(KD):
                        last = pe.transpose(back[m % 2][:, k, :], heads[:, m % 2, k * P:(k + 1) * P], g.ident[:])
                    last.then_inc(back_full, 1)


def xattn0_context(g, q_T, kl_T, latent_probs):
    nc, d = g.nc, g.dram
    PAIRS = 4
    PER_RING = CT * 2 + PAIRS * 4
    PER_KS = CT + PAIRS * 4
    GROUPS = [(0, 4), (4, 8), (8, 12), (12, 13)]
    CHUNKS = [(0, 512), (512, 1024), (1024, 1536), (1536, KEYS)]

    def size(t):
        return P if t < CFULL else CLAST

    with Stage(nc, "a2") as s:
        xn = s.sb("xn", [P, 2, CT, DC])
        wk = s.sb("wk", [P, KC, D])
        gain = s.sb("gain", [P, DC])
        bias = s.sb("bias", [P, DC])
        mask8 = s.sb("mask8", [P, 2, CTX], U8)
        mask = s.sb("mask", [P, KEYS], BF16)
        stats = s.sb("stats", [P, CT, 6])
        mv = s.sb("mv", [P, CT, 2])
        rstd = s.sb("rstd", [P, CT])
        xn_T = s.sb("xn_T", [P, 2, KC, P])
        sq = s.sb("sq", [P, 2, D])
        ss = s.sb("ss", [P, 2, 8])
        length = s.sb("length", [P, 2, 8])
        keys = s.sb("keys", [P, 2, D])
        k_T = s.sb("k_T", [P, PAIRS, KEYS])
        q_diag = s.sb("q_diag", [P, PAIRS, P])
        probs = s.sb("probs", [P, 2, KEYS])
        top4 = s.sb("top4", [P, 2, 4])
        neg_top = s.sb("neg_top", [P, 2])
        total = s.sb("total", [P, 2])
        inv = s.sb("inv", [P, 2])
        probs_T = s.sb("probs_T", [P, CT, D])
        mixed = s.sb("mixed", [P, KC, D])
        ring = [s.ps(f"ring{i}", [P, 4, P]) for i in range(3)]
        ks = [s.ps(f"ks{i}", [P, D]) for i in range(2)]
        mix = [s.ps(f"mix{i}", [P, D]) for i in range(KC)]

        w_in = s.sem("w_in")
        ctx_in = [s.sem(f"ctx_in{i}") for i in range(2)]
        dve_own = s.sem("dve_own")
        pool_own = s.sem("pool_own")
        scaled = s.sem("scaled")
        context_ready = s.sem("context_ready")
        ring_full, ring_out = s.sem("ring_full"), s.sem("ring_out")
        ks_full, ks_out = s.sem("ks_full"), s.sem("ks_out")
        measured, rooted = s.sem("measured"), s.sem("rooted")
        squared, summed, lengths = s.sem("squared"), s.sem("summed"), s.sem("lengths")
        side_ready = s.sem("side_ready")
        row_top, exped, probs_ready = s.sem("row_top"), s.sem("exped"), s.sem("probs_ready")
        mix_full, mix_out, mix_stored = s.sem("mix_full"), s.sem("mix_out"), s.sem("mix_stored")
        block = s.block()

        def turn(t, what):
            n = 0
            for step in range(CT + 2):
                if step < CT:
                    if (step, 0) == (t, what):
                        return n
                    n += 1
                if step >= 2:
                    if (step - 2, 1) == (t, what):
                        return n
                    n += 1

        CTX_DMAS = 5

        def load(sp, b, par):
            src = d["ctx"][bass.ds(b, 1)].rearrange("a s d -> (a s) d")
            for lo, hi in GROUPS[:3]:
                sp.dma_start(xn[:, par, lo:hi, :],
                             src[lo * P:hi * P, :].rearrange("(t p) d -> p t d", p=P)).then_inc(ctx_in[par], 16)
            sp.dma_start(xn[0:CLAST, par, CFULL, :], src[CFULL * P:CTX, :]).then_inc(ctx_in[par], 16)
            sp.dma_start(mask8[:, par, :], d["mask_ctx0"][bass.ds(b, 1), :].rearrange("a s -> (a s)")
                         .partition_broadcast(P)).then_inc(ctx_in[par], 16)

        def store(sp, b):
            sp.wait_ge(mix_out, KC * b + KC + FIRST)
            for f in range(KC):
                sp.dma_start(g.mixed_dram[:, f, :, bass.ds(b * SEQ, SEQ)],
                             mixed[:, f, :].rearrange("p (h q) -> p h q", h=8)).then_inc(mix_stored, 16)

        @block.sync
        def _(sp):
            for signal in (mix_stored,):
                sp.sem_inc(signal, FIRST)
            sp.dma_start(wk[:], d["L0_xattn_Wk"]).then_inc(w_in, 16)
            sp.dma_start(gain[:], rows(d["L0_xattn_ln_x_g"])).then_inc(w_in, 16)
            sp.dma_start(bias[:], rows(d["L0_xattn_ln_x_b"])).then_inc(w_in, 16)
            for par in range(2):
                load(sp, par, par)
            with sp.Fori(0, NB // 2 - 1) as i:
                for par in range(2):
                    b = i * 2 + par
                    store(sp, b)
                    sp.wait_ge(mix_full, KC * b + KC)
                    load(sp, b + 2, par)
            for par in range(2):
                store(sp, NB - 2 + par)
            sp.wait_ge(mix_stored, 16 * KC * NB + FIRST)

        @block.gpsimd
        def _(pool):
            for signal in (side_ready,):
                pool.sem_inc(signal, FIRST)
            pool.memset(mask[:, CTX:KEYS], 0.0).then_inc(pool_own, 1)
            pool.wait_ge(pool_own, 1)
            pool.memset(q_diag[:], 0.0).then_inc(pool_own, 1)
            pool.wait_ge(pool_own, 2)
            pool.wait_ge(w_in, 48)
            PER = len(GROUPS)
            with pool.Fori(0, NB // 2) as i:
                for par in range(2):
                    b = i * 2 + par
                    for n, (lo, hi) in enumerate(GROUPS):
                        m = size(hi - 1)
                        if n == 0:
                            pool.wait_ge(side_ready, b * 4 + FIRST)
                        else:
                            pool.wait_ge(context_ready, b * PER + n)
                        pool.wait_ge(scaled, b * PER + (n + 1))
                        part = xn[0:m, par, lo:hi, :]
                        pool.tensor_tensor(part, part, gain[0:m].unsqueeze(1).to_broadcast([m, hi - lo, DC]),
                                           ALU.mult).then_inc(pool_own, 1)
                        pool.wait_ge(pool_own, b * PER + (n + 3))
                        pool.tensor_tensor(part, part, bias[0:m].unsqueeze(1).to_broadcast([m, hi - lo, DC]),
                                           ALU.add).then_inc(context_ready, 1)
                    pool.wait_ge(ks_out, b * PER_KS + 2)
                    pool.wait_ge(context_ready, b * PER + PER)
                    pool.nop(nofuse=True)
                    pool.tensor_scalar(mask[:, 0:CTX], mask8[:, par, :], -MASKED, MASKED, ALU.mult,
                                       ALU.add).then_inc(side_ready, 1)
                    for h in range(2):
                        pool.wait_ge(side_ready, b * 4 + (1 + h) + FIRST)
                        pool.tensor_copy(q_diag[h * 64:(h + 1) * 64, :, h * 64:(h + 1) * 64],
                                         q_T[h * 64:(h + 1) * 64, :, bass.ds(b * SEQ, SEQ)]).then_inc(side_ready, 1)
                    pool.wait_ge(side_ready, b * 4 + 3 + FIRST)
                    pool.tensor_copy(k_T[:, :, CTX:KEYS], kl_T[:, :, bass.ds(b * SEQ, SEQ)]).then_inc(side_ready, 1)

        @block.vector
        def _(dve):
            dve.sem_inc(ks_out, 2)

            def measure_group(own, par, n):
                lo, hi = GROUPS[n]
                m = size(hi - 1)
                for t in range(lo, hi):
                    own.did(dve.bn_stats(stats[0:m, t, :], xn[0:m, par, t, :]))
                own.wait()
                for t in range(lo, hi):
                    last = dve.bn_aggr(mv[0:m, t, :], stats[0:m, t, :])
                last.then_inc(measured, 1)

            def normalise_group(own, b, par, n):
                lo, hi = GROUPS[n]
                m = size(hi - 1)
                dve.wait_ge(rooted, b * len(GROUPS) + (n + 1))
                own.did(dve.reciprocal(rstd[0:m, lo:hi], rstd[0:m, lo:hi]))
                own.wait()
                for t in range(lo, hi):
                    last = dve.tensor_scalar(xn[0:m, par, t, :], xn[0:m, par, t, :], mv[0:m, t, 0:1],
                                             rstd[0:m, t:t + 1], ALU.subtract, ALU.mult)
                last.then_inc(scaled, 1)

            def sum_squares(b, par, t):
                m, i = size(t), (par * CT + t) % 2
                dve.wait_ge(squared, b * CT + (t + 1))
                dve.tensor_reduce(ss[0:m, i, :], sq[0:m, i, :].rearrange("p (h c) -> p h c", h=8),
                                  AXX, ALU.add).then_inc(summed, 1)

            def normalise_keys(own, b, par, t):
                m, i = size(t), (par * CT + t) % 2
                use = (par * PER_KS + t) % 2
                dve.wait_ge(ring_full, b * PER_RING + (turn(t - 2, 1) + 1 if t >= 2 else 0) + FIRST)
                dve.wait_ge(lengths, b * CT + (t + 1))
                scale_by_length(dve, own, keys[0:m, i, :].rearrange("p (h c) -> p h c", h=8),
                                ks[use][0:m, :].rearrange("p (h c) -> p h c", h=8),
                                length[0:m, i, :]).then_inc(ks_out, 1)

            def take_scores(own, b, par, pair, c):
                lo, hi = CHUNKS[c]
                n = CT + pair * 4 + c
                dve.wait_ge(ks_full, b * PER_KS + (n + 1) + FIRST)
                dve.nop(nofuse=True)
                dve.tensor_tensor_reduce(out=probs[:, pair % 2, lo:hi], in0=ks[(par * PER_KS + n) % 2][:, 0:hi - lo],
                                         in1=mask[:, lo:hi], scale=1.0, scalar=-3e38, op0=ALU.add, op1=ALU.max,
                                         accum_out=top4[:, pair % 2, c:c + 1]).then_inc(ks_out, 1)

            def scale_probs(own, b, pair):
                dve.wait_ge(exped, b * PAIRS + (pair + 1))
                own.did(dve.reciprocal(inv[:, pair % 2:pair % 2 + 1], total[:, pair % 2:pair % 2 + 1]))
                own.wait()
                dve.tensor_scalar(probs[:, pair % 2, :], probs[:, pair % 2, :], inv[:, pair % 2:pair % 2 + 1], None,
                                  ALU.mult).then_inc(probs_ready, 1)

            with dve.Fori(0, NB // 2) as i:
                for par in range(2):
                    b = i * 2 + par
                    restart(dve, dve_own)
                    own = Steps(dve, dve_own)
                    dve.wait_ge(ctx_in[par], (i + 1) * (16 * CTX_DMAS))
                    measure_group(own, par, 0)
                    measure_group(own, par, 1)
                    normalise_group(own, b, par, 0)
                    for t in range(CT):
                        sum_squares(b, par, t)
                        if t % 4 == 0 and t // 4 + 1 < len(GROUPS):
                            normalise_group(own, b, par, t // 4 + 1)
                        if t % 4 == 0 and t // 4 + 2 < len(GROUPS):
                            measure_group(own, par, t // 4 + 2)
                        normalise_keys(own, b, par, t)
                    dve.wait_ge(side_ready, b * 4 + 4 + FIRST)
                    for pair in range(PAIRS):
                        for c in range(4):
                            take_scores(own, b, par, pair, c)
                            if c == 2 and pair >= 1:
                                scale_probs(own, b, pair - 1)
                        dve.wait_ge(ks_out, b * PER_KS + (CT + pair * 4 + 4 + 2))
                        dve.tensor_reduce(neg_top[:, pair % 2:pair % 2 + 1], top4[:, pair % 2, :], AXX, ALU.max,
                                          negate=True).then_inc(row_top, 1)
                    scale_probs(own, b, PAIRS - 1)
                    own.wait()

        @block.scalar
        def _(act):
            for signal in (mix_out,):
                act.sem_inc(signal, FIRST)
            act.sem_inc(ring_out, 3)

            def put_context(b, par, t):
                m, n = size(t), turn(t, 0)
                act.wait_ge(ring_full, b * PER_RING + (n + 1) + FIRST)
                if t < 2:
                    act.wait_ge(ks_full, b * PER_KS + FIRST)
                else:
                    act.wait_ge(ks_full, b * PER_KS + (t - 1) + FIRST)
                act.activation(xn_T[:, (par * CT + t) % 2, :, 0:m], ring[(par * PER_RING + n) % 3][:, 0:KC, 0:m],
                               ACT.Copy).then_inc(ring_out, 1)

            def square_keys(b, par, t):
                m, i = size(t), (par * CT + t) % 2
                act.wait_ge(ks_full, b * PER_KS + (t + 1) + FIRST)
                if t < 2:
                    act.wait_ge(ks_out, b * PER_KS + 2)
                else:
                    act.wait_ge(ks_out, b * PER_KS + (t - 2 + 1 + 2))
                act.activation(sq[0:m, i, :], ks[(par * PER_KS + t) % 2][0:m, :], ACT.Square).then_inc(squared, 1)

            def root_group(b, n):
                lo, hi = GROUPS[n]
                m = size(hi - 1)
                act.wait_ge(measured, b * len(GROUPS) + (n + 1))
                act.activation(rstd[0:m, lo:hi], mv[0:m, lo:hi, 1], ACT.Sqrt, bias=g.eps[0:m]).then_inc(rooted, 1)

            def root_lengths(b, par, t):
                m, i = size(t), (par * CT + t) % 2
                act.wait_ge(summed, b * CT + (t + 1))
                act.activation(length[0:m, i, :], ss[0:m, i, :], ACT.Sqrt).then_inc(lengths, 1)

            def put_keys(b, par, t):
                m, n = size(t), turn(t, 1)
                act.wait_ge(ring_full, b * PER_RING + (n + 1) + FIRST)
                act.activation(k_T[:, :, t * P:t * P + m], ring[(par * PER_RING + n) % 3][:, :, 0:m],
                               ACT.Copy).then_inc(ring_out, 1)

            def exponentials(b, pair):
                act.wait_ge(row_top, b * PAIRS + (pair + 1))
                act.activation(probs[:, pair % 2, :], probs[:, pair % 2, :], ACT.Exp,
                               bias=neg_top[:, pair % 2:pair % 2 + 1],
                               accum_out=total[:, pair % 2:pair % 2 + 1]).then_inc(exped, 1)

            def put_probs(b, par, pair):
                for q in range(4):
                    n = 2 * CT + pair * 4 + q
                    bank = ring[(par * PER_RING + n) % 3]
                    act.wait_ge(ring_full, b * PER_RING + (n + 1) + FIRST)
                    cols = slice(pair * P, (pair + 1) * P)
                    if q < 3:
                        act.activation(probs_T[:, 4 * q:4 * q + 4, cols], bank[:], ACT.Copy).then_inc(ring_out, 1)
                    else:
                        act.activation(probs_T[0:CLAST, CFULL, cols], bank[0:CLAST, 0, :], ACT.Copy)
                        act.activation(latent_probs[:, bass.ds(b, 1), cols], bank[0:SEQ, 1, :].unsqueeze(1),
                                       ACT.Copy).then_inc(ring_out, 1)

            with act.Fori(0, NB // 2) as i:
                for par in range(2):
                    b = i * 2 + par
                    root_group(b, 0)
                    root_group(b, 1)
                    for t in range(CT + 2):
                        if t < CT:
                            put_context(b, par, t)
                        if 1 <= t <= CT:
                            square_keys(b, par, t - 1)
                        if t >= 2:
                            put_keys(b, par, t - 2)
                        if 1 <= t <= CT:
                            root_lengths(b, par, t - 1)
                        if t in (2, 6):
                            root_group(b, t // 4 + 2)
                    for pair in range(PAIRS):
                        exponentials(b, pair)
                        put_probs(b, par, pair)
                    act.wait_ge(mix_stored, b * (16 * KC) + FIRST)
                    for f in range(KC):
                        act.wait_ge(mix_full, b * KC + (f + 1))
                        act.activation(mixed[:, f, :], mix[f][:], ACT.Copy).then_inc(mix_out, 1)

        @block.tensor
        def _(pe):
            for signal in (ring_full, ks_full,):
                pe.sem_inc(signal, FIRST)
            pe.wait_ge(w_in, 48)

            def turn_context(b, par, t):
                m, n = size(t), turn(t, 0)
                if t % 4 == 0:
                    pe.wait_ge(context_ready, b * len(GROUPS) + (t // 4 + 1))
                pe.wait_ge(ring_out, b * PER_RING + (n + 1))
                for k in range(KC):
                    last = pe.transpose(ring[(par * PER_RING + n) % 3][:, k, 0:m], xn[0:m, par, t, k * P:(k + 1) * P],
                                        g.ident[0:m, 0:m])
                last.then_inc(ring_full, 1)

            def project(b, par, t):
                m = size(t)
                pe.wait_ge(ring_out, b * PER_RING + (turn(t, 0) + 1 + 3))
                pe.wait_ge(ks_out, b * PER_KS + (t + 1))
                for k in range(KC):
                    last = pe.matmul(ks[(par * PER_KS + t) % 2][0:m, :], xn_T[:, (par * CT + t) % 2, k, 0:m],
                                     wk[:, k, :], start=(k == 0), stop=(k == KC - 1))
                last.then_inc(ks_full, 1)

            def turn_keys(b, par, t):
                m, n = size(t), turn(t, 1)
                pe.wait_ge(ks_out, b * PER_KS + (t + 1 + 2))
                pe.wait_ge(ring_out, b * PER_RING + (n + 1))
                for k in range(4):
                    last = pe.transpose(ring[(par * PER_RING + n) % 3][:, k, 0:m],
                                        keys[0:m, (par * CT + t) % 2, k * P:(k + 1) * P], g.ident[0:m, 0:m])
                last.then_inc(ring_full, 1)

            def scores(b, par, pair):
                for c, (lo, hi) in enumerate(CHUNKS):
                    n = CT + pair * 4 + c
                    pe.wait_ge(ks_out, b * PER_KS + (n + 1))
                    pe.matmul(ks[(par * PER_KS + n) % 2][:, 0:hi - lo], q_diag[:, pair, :], k_T[:, pair, lo:hi],
                              start=True, stop=True).then_inc(ks_full, 1)

            def turn_probs(b, par, pair):
                pe.wait_ge(probs_ready, b * PAIRS + (pair + 1))
                for q in range(4):
                    n = 2 * CT + pair * 4 + q
                    bank = ring[(par * PER_RING + n) % 3]
                    pe.wait_ge(ring_out, b * PER_RING + (n + 1))
                    if q < 3:
                        for j in range(4):
                            t = 4 * q + j
                            last = pe.transpose(bank[:, j, :], probs[:, pair % 2, t * P:(t + 1) * P], g.ident[:])
                    else:
                        pe.transpose(bank[0:CLAST, 0, :], probs[:, pair % 2, CFULL * P:CTX], g.ident[:])
                        last = pe.transpose(bank[0:SEQ, 1, :], probs[:, pair % 2, CTX:KEYS], g.ident[:])
                    last.then_inc(ring_full, 1)

            with pe.Fori(0, NB // 2) as i:
                for par in range(2):
                    b = i * 2 + par
                    for t in range(CT + 2):
                        if t < CT:
                            turn_context(b, par, t)
                        if 1 <= t <= CT:
                            project(b, par, t - 1)
                        if t >= 2:
                            turn_keys(b, par, t - 2)
                    pe.wait_ge(ring_out, b * PER_RING + (2 * CT + 3))
                    pe.wait_ge(side_ready, b * 4 + 4 + FIRST)
                    scores(b, par, 0)
                    for pair in range(PAIRS):
                        if pair + 1 < PAIRS:
                            scores(b, par, pair + 1)
                        turn_probs(b, par, pair)
                    pe.wait_ge(ring_out, b * PER_RING + (PER_RING + 3))
                    for f in range(KC):
                        pe.wait_ge(mix_out, b * KC + FIRST)
                        for t in range(CT):
                            m = size(t)
                            last = pe.matmul(mix[f][:], xn[0:m, par, t, f * P:(f + 1) * P], probs_T[0:m, t, :],
                                             start=(t == 0), stop=(t == CT - 1))
                        last.then_inc(mix_full, 1)


def xattn0_output(g, latent_probs):
    nc, d = g.nc, g.dram
    with Stage(nc, "a3") as s:
        mixed = s.sb("mixed", [P, KC, 8, TOK])
        wv = s.sb("wv", [P, KC, D])
        wlv = s.sb("wlv", [P, KD, D])
        wo = s.sb("wo", [P, KD, D])
        bo = s.sb("bo", [P, D])
        lat_v = s.sb("lat_v", [SEQ, NB, D])
        o_T = s.sb("o_T", [P, 4, TOK])
        proj = [s.ps(f"proj{i}", [P, D]) for i in range(2)]
        heads = [s.ps(f"heads{i}", [P, TOK]) for i in range(2)]
        w_in, mixed_in = s.sem("w_in"), s.sem("mixed_in")
        v_full, v_out = s.sem("v_full"), s.sem("v_out")
        heads_full, heads_out = s.sem("heads_full"), s.sem("heads_out")
        y_full, biased, y_out = s.sem("y_full"), s.sem("biased"), s.sem("y_out")
        block = s.block()

        @block.sync
        def _(sp):
            sp.dma_start(wlv[:], d["L0_xattn_Wlv"]).then_inc(w_in, 16)
            sp.dma_start(wv[:], d["L0_xattn_Wv"]).then_inc(w_in, 16)
            sp.dma_start(wo[:], d["L0_xattn_Wo"]).then_inc(w_in, 16)
            sp.dma_start(bo[:], rows(d["L0_xattn_bo"])).then_inc(w_in, 16)
            sp.dma_start(mixed[:], g.mixed_dram).then_inc(mixed_in, 16)

        @block.gpsimd
        def _(pool):
            pool.wait_ge(w_in, 64)
            pool.tensor_tensor(g.x[:], g.x[:], bo[:].unsqueeze(1).to_broadcast([P, NT, D]),
                               ALU.add).then_inc(biased, 1)

        @block.tensor
        def _(pe):
            pe.wait_ge(w_in, 64)
            for b in range(NB):
                if b >= 2:
                    pe.wait_ge(v_out, b - 1)
                for k in range(KD):
                    last = pe.matmul(proj[b % 2][0:SEQ, :], g.hT[:, k, b * SEQ:(b + 1) * SEQ], wlv[:, k, :],
                                     start=(k == 0), stop=(k == KD - 1))
                last.then_inc(v_full, 1)
            pe.wait_ge(mixed_in, 16)
            pe.wait_ge(v_out, NB)
            for pair in range(4):
                if pair >= 2:
                    pe.wait_ge(heads_out, pair - 1)
                for half in range(2):
                    h = pair * 2 + half
                    out = heads[pair % 2][half * 64:(half + 1) * 64, :]
                    for k in range(KC):
                        pe.matmul(out, wv[:, k, h * 64:(h + 1) * 64], mixed[:, k, h, :], start=(k == 0), stop=False,
                                  skip_group_check=True)
                    for b in range(NB):
                        last = pe.matmul(out[:, b * SEQ:(b + 1) * SEQ], lat_v[:, b, h * 64:(h + 1) * 64],
                                         latent_probs[:, b, h * SEQ:(h + 1) * SEQ], start=False,
                                         stop=(b == NB - 1), skip_group_check=True)
                last.then_inc(heads_full, 1)
            pe.wait_ge(heads_out, 4)
            for t in range(NT):
                if t >= 2:
                    pe.wait_ge(y_out, t - 1)
                for k in range(KD):
                    last = pe.matmul(proj[t % 2][:], o_T[:, k, t * P:(t + 1) * P], wo[:, k, :],
                                     start=(k == 0), stop=(k == KD - 1))
                last.then_inc(y_full, 1)

        @block.scalar
        def _(act):
            for b in range(NB):
                act.wait_ge(v_full, b + 1)
                act.activation(lat_v[:, b, :], proj[b % 2][0:SEQ, :], ACT.Copy).then_inc(v_out, 1)
            for pair in range(4):
                act.wait_ge(heads_full, pair + 1)
                act.activation(o_T[:, pair, :], heads[pair % 2][:], ACT.Copy).then_inc(heads_out, 1)

        @block.vector
        def _(dve):
            dve.wait_ge(biased, 1)
            for t in range(NT):
                dve.wait_ge(y_full, t + 1)
                dve.tensor_tensor(g.x[:, t, :], proj[t % 2][:], g.x[:, t, :], ALU.add).then_inc(y_out, 1)


def causal_attention(g, name, w_dram, n_k, rope, v_dram, v_cols, wo_dram, bias_dram, scale):
    nc, d = g.nc, g.dram
    H, HD = 16, 32
    NQK = 4 + n_k
    NPROJ = NQK * (2 if rope else 1)
    with Stage(nc, name) as s:
        w = s.sb("w", [P, KD, NPROJ * P])
        wv = s.sb("wv", [P, KD, v_cols])
        wo = s.sb("wo", [P, KD, D])
        norm = Norm(s)
        causal = s.sb("causal", [P, P])
        qk_T = s.sb("qk_T", [P, NQK, TOK])
        v = s.sb("v", [P, NT, v_cols])
        scores = s.sb("scores", [P, 4, 4, P])
        top = s.sb("top", [P, H])
        total = s.sb("total", [P, H])
        probs_T = s.sb("probs_T", [P, H, P])
        o_T = s.sb("o_T", [P, 4, TOK])
        if rope:
            half = s.sb("half", [P, TOK])
            cos = s.sb("cos", [P, TOK])
            sin = s.sb("sin", [P, TOK])
        else:
            bias = s.sb("bias", [P, NQK])
            bias_v = s.sb("bias_v", [P, v_cols])
            bias_o = s.sb("bias_o", [P, D])
        bank = [s.ps(f"bank{i}", [P, 4, P]) for i in range(4)]
        ring = [s.ps(f"ring{i}", [P, 4, P]) for i in range(4)]
        w_in = s.sem("w_in")
        mask_made = s.sem("mask_made")
        ring_full, ring_out = s.sem("ring_full"), s.sem("ring_out")
        heads_ready = s.sem("heads_ready")
        v_ready = s.sem("v_ready")
        scores_full, masked, centred = s.sem("scores_full"), s.sem("masked"), s.sem("centred")
        exped, probs_ready, probs_turned = s.sem("exped"), s.sem("probs_ready"), s.sem("probs_turned")
        o_full, o_out, biased, x_out = s.sem("o_full"), s.sem("o_out"), s.sem("biased"), s.sem("x_out")
        dve_own = s.sem("dve_own")
        block = s.block()
        R_PROJ = NT
        R_V = R_PROJ + NPROJ
        R_TILE = R_V + NT
        R_Y = R_TILE + 5 * NT
        W_IN = 16 * (5 if rope else 6)

        @block.sync
        def _(sp):
            sp.dma_start(w[:], d[w_dram]).then_inc(w_in, 16)
            sp.dma_start(wv[:], d[v_dram]).then_inc(w_in, 16)
            sp.dma_start(wo[:], d[wo_dram]).then_inc(w_in, 16)
            if rope:
                sp.dma_start(cos[:], d["rope_cos"]).then_inc(w_in, 16)
                sp.dma_start(sin[:], d["rope_sin"]).then_inc(w_in, 16)
            else:
                sp.dma_start(bias[:], d[bias_dram + "_qk"]).then_inc(w_in, 16)
                sp.dma_start(bias_v[:], rows(d[bias_dram + "_v"])).then_inc(w_in, 16)
                sp.dma_start(bias_o[:], rows(d[bias_dram + "_o"])).then_inc(w_in, 16)

        @block.gpsimd
        def _(pool):
            pool.memset(causal[:], 0.0).then_inc(mask_made, 1)
            pool.wait_ge(mask_made, 1)
            pool.affine_select(out=causal[:], in_=causal[:], compare_op=ALU.is_ge, fill=MASKED, base=0,
                               pattern=[[-1, P]], channel_multiplier=1).then_inc(mask_made, 1)
            pool.wait_ge(mask_made, 2)
            pool.memset(causal[SEQ:P, 0:SEQ], MASKED).then_inc(mask_made, 1)
            if not rope:
                pool.wait_ge(mask_made, 3)
                pool.wait_ge(norm.normed, NT)
                pool.wait_ge(w_in, W_IN)
                pool.tensor_tensor(g.x[:], g.x[:], bias_o[:].unsqueeze(1).to_broadcast([P, NT, D]),
                                   ALU.add).then_inc(biased, 1)

        @block.vector
        def _(dve):
            own = Steps(dve, dve_own)
            norm.on_vector(dve, g.x, g.hn)
            dve.wait_ge(w_in, W_IN)
            if rope:
                for n in range(NQK):
                    u = R_PROJ + 2 * n
                    dve.wait_ge(ring_full, u + 1)
                    own.did(dve.tensor_tensor(qk_T[:, n, :], flat(ring[u % 4]), cos[:], ALU.mult))
                    own.wait()
                    dve.sem_inc(ring_out, 1)
                    dve.wait_ge(ring_full, u + 2)
                    own.did(dve.tensor_tensor(half[:], flat(ring[(u + 1) % 4]), sin[:], ALU.mult))
                    own.wait()
                    dve.sem_inc(ring_out, 1)
                    dve.tensor_tensor(qk_T[:, n, :], qk_T[:, n, :], half[:], ALU.add).then_inc(heads_ready, 1)
                    dve.wait_ge(heads_ready, n + 1)
            else:
                for n in range(NQK):
                    u = R_PROJ + n
                    dve.wait_ge(ring_full, u + 1)
                    own.did(dve.tensor_scalar(qk_T[:, n, :], flat(ring[u % 4]), bias[:, n:n + 1], None, ALU.add))
                    own.wait()
                    dve.sem_inc(ring_out, 1)
            for t in range(NT):
                u = R_V + t
                dve.wait_ge(ring_full, u + 1)
                part = flat(ring[u % 4])[:, 0:v_cols]
                if rope:
                    own.did(dve.tensor_copy(v[:, t, :], part))
                else:
                    own.did(dve.tensor_tensor(v[:, t, :], part, bias_v[:], ALU.add))
                own.wait()
                dve.sem_inc(ring_out, 1)
            dve.sem_inc(v_ready, 1)
            dve.wait_ge(mask_made, 3)
            for t in range(NT):
                if t >= 1:
                    dve.wait_ge(ring_full, R_TILE + 5 * (t - 1) + 4)
                for i in range(4):
                    dve.wait_ge(scores_full, 4 * t + i + 1)
                    dve.tensor_tensor(scores[:, i, :, :], bank[i][:], causal[:].unsqueeze(1).to_broadcast([P, 4, P]),
                                      ALU.add).then_inc(masked, 1)
                dve.wait_ge(masked, 4 * t + 4)
                by_head = scores[:].rearrange("p i c k -> p (i c) k")
                own.did(dve.tensor_reduce(top[:], by_head, AXX, ALU.max))
                own.wait()
                dve.tensor_tensor(by_head, by_head, top[:].unsqueeze(2).to_broadcast([P, H, P]),
                                  ALU.subtract).then_inc(centred, 1)
                dve.wait_ge(exped, t + 1)
                own.did(dve.tensor_reduce(total[:], by_head, AXX, ALU.add))
                own.wait()
                own.did(dve.reciprocal(total[:], total[:]))
                own.wait()
                dve.tensor_tensor(by_head, by_head, total[:].unsqueeze(2).to_broadcast([P, H, P]),
                                  ALU.mult).then_inc(probs_ready, 1)
            if not rope:
                dve.wait_ge(biased, 1)
            for t in range(NT):
                dve.wait_ge(ring_full, R_Y + t + 1)
                dve.tensor_tensor(g.x[:, t, :], flat(ring[(R_Y + t) % 4]), g.x[:, t, :], ALU.add).then_inc(x_out, 1)

        @block.scalar
        def _(act):
            norm.on_scalar(act, g.eps[:])
            for t in range(NT):
                act.wait_ge(ring_full, t + 1)
                act.activation(g.hT[:, :, t * P:(t + 1) * P], ring[t % 4][:], ACT.Copy).then_inc(ring_out, 1)
            for t in range(NT):
                act.wait_ge(centred, t + 1)
                act.activation(scores[:], scores[:], ACT.Exp, scale=scale).then_inc(exped, 1)
                if t >= 1:
                    act.wait_ge(ring_full, R_TILE + 5 * t)
                for i in range(4):
                    u = R_TILE + 5 * t + i
                    act.wait_ge(ring_full, u + 1)
                    act.activation(probs_T[:, 4 * i:4 * i + 4, :], ring[u % 4][:], ACT.Copy).then_inc(ring_out, 1)
                u = R_TILE + 5 * t + 4
                act.wait_ge(ring_full, u + 1)
                act.activation(o_T[:, :, t * P:(t + 1) * P], ring[u % 4][:], ACT.Copy).then_inc(ring_out, 1)

        @block.tensor
        def _(pe):
            pe.wait_ge(norm.normed, NT)
            for t in range(NT):
                for k in range(KD):
                    last = pe.transpose(ring[t][:, k, :], g.hn[:, t, k * P:(k + 1) * P], g.ident[:])
                last.then_inc(ring_full, 1)
            pe.wait_ge(w_in, W_IN)
            for n in range(NPROJ):
                u = R_PROJ + n
                pe.wait_ge(ring_out, max(u - 3, NT))
                col = (n // 2 + n % 2 * NQK) if rope else n
                for k in range(KD):
                    last = pe.matmul(flat(ring[u % 4]), w[:, k, col * P:(col + 1) * P], g.hT[:, k, :],
                                     start=(k == 0), stop=(k == KD - 1))
                last.then_inc(ring_full, 1)
            for t in range(NT):
                u = R_V + t
                pe.wait_ge(ring_out, u - 3)
                for k in range(KD):
                    last = pe.matmul(flat(ring[u % 4])[:, 0:v_cols], g.hT[:, k, t * P:(t + 1) * P], wv[:, k, :],
                                     start=(k == 0), stop=(k == KD - 1))
                last.then_inc(ring_full, 1)
            pe.wait_ge(ring_out, R_TILE)
            if rope:
                pe.wait_ge(heads_ready, NQK)

            def tile_scores(t):
                tok = slice(t * P, (t + 1) * P)
                for i in range(4):
                    if t >= 1:
                        pe.wait_ge(masked, 4 * (t - 1) + i + 1)
                    r = slice(HD * i, HD * i + HD)
                    for c in range(4):
                        key = 4 + (c if n_k == 4 else 0)
                        last = pe.matmul(bank[i][:, c, :], qk_T[r, c, tok], qk_T[r, key, tok], start=True, stop=True)
                    last.then_inc(scores_full, 1)

            tile_scores(0)
            for t in range(NT):
                if t + 1 < NT:
                    tile_scores(t + 1)
                pe.wait_ge(probs_ready, t + 1)
                for i in range(4):
                    u = R_TILE + 5 * t + i
                    pe.wait_ge(ring_out, u - 3)
                    for c in range(4):
                        last = pe.transpose(ring[u % 4][:, c, :], scores[:, i, c, :], g.ident[:])
                    last.then_inc(ring_full, 1)
                u = R_TILE + 5 * t + 4
                pe.wait_ge(ring_out, u)
                for c in range(4):
                    for i in range(4):
                        h = c * 4 + i
                        vh = v[:, t, h * HD:(h + 1) * HD] if v_cols > HD else v[:, t, :]
                        last = pe.matmul(ring[u % 4][i * HD:(i + 1) * HD, c, :], vh, probs_T[:, i * 4 + c, :],
                                         start=True, stop=True)
                last.then_inc(ring_full, 1)
            pe.wait_ge(ring_out, R_Y)
            for t in range(NT):
                u = R_Y + t
                for k in range(KD):
                    last = pe.matmul(flat(ring[u % 4]), o_T[:, k, t * P:(t + 1) * P], wo[:, k, :],
                                     start=(k == 0), stop=(k == KD - 1))
                last.then_inc(ring_full, 1)


def flat(bank):
    return bank[:].rearrange("p k n -> p (k n)")


E_N = 8
TOP = 2


def choose(dve, own, probs, above, equal, before, rank, chosen):
    mine = probs[:].unsqueeze(3).to_broadcast([P, NT, E_N, E_N])
    other = probs[:].unsqueeze(2).to_broadcast([P, NT, E_N, E_N])
    own.did(dve.tensor_tensor(above[:], other, mine, ALU.is_gt))
    own.did(dve.tensor_tensor(equal[:], other, mine, ALU.is_equal))
    own.wait()
    flat_equal = equal[:].rearrange("p t e f -> p t (e f)")
    own.did(dve.tensor_tensor(flat_equal, flat_equal, before[:].unsqueeze(1).to_broadcast([P, NT, E_N * E_N]),
                              ALU.mult))
    own.wait()
    own.did(dve.tensor_tensor(above[:], above[:], equal[:], ALU.add))
    own.wait()
    own.did(dve.tensor_reduce(rank[:], above[:], AXX, ALU.add))
    own.wait()
    own.did(dve.tensor_scalar(rank[:], rank[:], TOP - 0.5, None, ALU.is_lt))
    own.wait()
    own.did(dve.tensor_tensor(chosen, probs[:], rank[:], ALU.mult))
    own.wait()


def shared_and_routed_experts(g):
    nc, d = g.nc, g.dram
    F = 1024
    FC = F // P
    NE = E_N + 1
    with Stage(nc, "c") as s:
        w_gate = s.sb("w_gate", [P, KD, F])
        w_up = s.sb("w_up", [P, KD, F])
        w_down = s.sb("w_down", [P, FC, D])
        w_route = s.sb("w_route", [P, KD, E_N])
        bias = s.sb("bias", [P, E_N])
        before = s.sb("before", [P, E_N * E_N])
        norm = Norm(s)
        probs = s.sb("probs", [P, NT, E_N])
        above = s.sb("above", [P, NT, E_N, E_N])
        equal = s.sb("equal", [P, NT, E_N, E_N])
        rank = s.sb("rank", [P, NT, E_N])
        weight = s.sb("weight", [P, NT, NE])
        silu = s.sb("silu", [P, 2, TOK])
        hidden = s.sb("hidden", [P, FC, TOK])
        up = [s.ps(f"up{i}", [P, TOK]) for i in range(4)]
        y = [s.ps(f"y{i}", [P, D]) for i in range(NT)]
        r_in, gate_in, up_in, down_in = s.sem("r_in"), s.sem("gate_in"), s.sem("up_in"), s.sem("down_in")
        turned_full, turned_out = s.sem("turned_full"), s.sem("turned_out")
        routed, biased, probs_ready, weights_ready = (s.sem("routed"), s.sem("biased"), s.sem("probs_ready"),
                                                      s.sem("weights_ready"))
        gate_full, up_full, silu_ready, hidden_ready = (s.sem("gate_full"), s.sem("up_full"), s.sem("silu_ready"),
                                                        s.sem("hidden_ready"))
        y_full, y_out = s.sem("y_full"), s.sem("y_out")
        dve_own = s.sem("dve_own")
        ss = StateSpace(s, g)
        block = s.block()

        @block.gpsimd
        def _(pool):
            ss.on_gpsimd(pool)

        def load_wide(sp, e):
            sp.dma_start(w_gate[:], d["L0_ffn_Wg"][bass.ds(e, 1)].rearrange("a p k n -> p (a k) n")).then_inc(gate_in, 16)
            sp.dma_start(w_up[:], d["L0_ffn_Wu"][bass.ds(e, 1)].rearrange("a p k n -> p (a k) n")).then_inc(up_in, 16)

        def load_down(sp, e):
            sp.dma_start(w_down[:], d["L0_ffn_Wd"][bass.ds(e, 1)].rearrange("a p k n -> p (a k) n")).then_inc(down_in, 16)

        @block.sync
        def _(sp):
            sp.dma_start(w_route[:], d["L0_ffn_Wr"]).then_inc(r_in, 16)
            sp.dma_start(bias[:], rows(d["L0_ffn_rb"])).then_inc(r_in, 16)
            sp.dma_start(before[:], rows(d["before"])).then_inc(r_in, 16)
            load_wide(sp, 0)
            ss.on_sync(sp)
            load_down(sp, 0)
            with sp.Fori(0, NE - 1) as e:
                sp.wait_ge(up_full, e * FC + FC)
                load_wide(sp, e + 1)
                sp.wait_ge(y_full, e * NT + NT + FIRST)
                load_down(sp, e + 1)

        @block.vector
        def _(dve):
            for signal in (y_out, hidden_ready,):
                dve.sem_inc(signal, FIRST)
            own = Steps(dve, dve_own)
            norm.on_vector(dve, g.x, g.hn)
            dve.wait_ge(r_in, 48)
            own.did(dve.memset(weight[:], 1.0))
            dve.wait_ge(routed, 1)
            dve.tensor_tensor(probs[:], up[3][:, 0:NT * E_N].rearrange("p (t e) -> p t e", t=NT),
                              bias[:].unsqueeze(1).to_broadcast([P, NT, E_N]), ALU.add).then_inc(biased, 1)
            dve.wait_ge(probs_ready, 1)
            choose(dve, own, probs, above, equal, before, rank, weight[:, :, 1:NE])
            ss.on_vector(dve)
            with dve.Fori(0, NE) as e:
                dve.wait_ge(y_full, e * NT + FIRST)
                for m in range(FC):
                    dve.wait_ge(silu_ready, e * FC + (m + 1))
                    dve.wait_ge(up_full, e * FC + (m + 1))
                    dve.tensor_tensor(hidden[:, m, :], silu[:, m % 2, :], up[2 + m % 2][:],
                                      ALU.mult).then_inc(hidden_ready, 1)
                for t in range(NT):
                    dve.wait_ge(y_full, e * NT + (t + 1) + FIRST)
                    dve.wait_ge(y_out, e * NT + FIRST)
                    dve.scalar_tensor_tensor(out=g.x[:, t, :], in0=y[t][:], scalar=weight[:, t, bass.ds(e, 1)],
                                             in1=g.x[:, t, :], op0=ALU.mult, op1=ALU.add).then_inc(y_out, 1)

        @block.scalar
        def _(act):
            norm.on_scalar(act, g.eps[:])
            for t in range(NT):
                act.wait_ge(turned_full, t + 1)
                act.activation(g.hT[:, :, t * P:(t + 1) * P], y[t][:].rearrange("p (k n) -> p k n", k=KD),
                               ACT.Copy).then_inc(turned_out, 1)
            act.wait_ge(biased, 1)
            act.activation(probs[:], probs[:], ACT.Sigmoid).then_inc(probs_ready, 1)
            ss.on_scalar(act)
            with act.Fori(0, NE) as e:
                for m in range(FC):
                    act.wait_ge(gate_full, e * FC + (m + 1))
                    act.wait_ge(hidden_ready, e * FC + (m - 1 if m >= 2 else 0) + FIRST)
                    act.activation(silu[:, m % 2, :], up[m % 2][:], ACT.Silu).then_inc(silu_ready, 1)

        @block.tensor
        def _(pe):
            for signal in (y_full,):
                pe.sem_inc(signal, FIRST)
            pe.wait_ge(norm.normed, NT)
            for t in range(NT):
                for k in range(KD):
                    last = pe.transpose(y[t][:, k * P:(k + 1) * P], g.hn[:, t, k * P:(k + 1) * P], g.ident[:])
                last.then_inc(turned_full, 1)
            pe.wait_ge(turned_out, NT)
            pe.wait_ge(r_in, 48)
            for t in range(NT):
                for k in range(KD):
                    last = pe.matmul(up[3][:, t * E_N:(t + 1) * E_N], g.hT[:, k, t * P:(t + 1) * P], w_route[:, k, :],
                                     start=(k == 0), stop=(k == KD - 1))
            last.then_inc(routed, 1)
            pe.wait_ge(biased, 1)
            with pe.Fori(0, NE) as e:
                for m in range(FC):
                    pe.wait_ge(hidden_ready, e * FC + (m - 1 if m >= 2 else 0) + FIRST)
                    if m == 0:
                        pe.wait_ge(gate_in, e * 16 + 16)
                    for k in range(KD):
                        last = pe.matmul(up[m % 2][:], w_gate[:, k, m * P:(m + 1) * P], g.hT[:, k, :],
                                         start=(k == 0), stop=(k == KD - 1))
                    last.then_inc(gate_full, 1)
                    if m == 0:
                        pe.wait_ge(up_in, e * 16 + 16)
                    for k in range(KD):
                        last = pe.matmul(up[2 + m % 2][:], w_up[:, k, m * P:(m + 1) * P], g.hT[:, k, :],
                                         start=(k == 0), stop=(k == KD - 1))
                    last.then_inc(up_full, 1)
                pe.wait_ge(down_in, e * 16 + 16)
                pe.wait_ge(hidden_ready, e * FC + FC + FIRST)
                pe.wait_ge(y_out, e * NT + FIRST)
                for t in range(NT):
                    for k in range(FC):
                        last = pe.matmul(y[t][:], hidden[:, k, t * P:(t + 1) * P], w_down[:, k, :],
                                         start=(k == 0), stop=(k == FC - 1))
                    last.then_inc(y_full, 1)


def capacity_experts(g):
    nc, d = g.nc, g.dram
    F = 2048
    FC = F // P
    CAP = -(-TOK * TOP * 5 // (4 * E_N))
    REST = CAP - P
    TRIPLES = [(m, min(m + 3, FC)) for m in range(0, FC, 3)]
    assert 0 < REST <= 32 and 3 * CAP <= 512 < 4 * CAP
    with Stage(nc, "f") as s:
        w1 = s.sb("w1", [P, KD, F])
        w2 = s.sb("w2", [P, FC, D])
        w_route = s.sb("w_route", [P, KD, E_N])
        before = s.sb("before", [P, E_N * E_N])
        slots = s.sb("slots", [P, CAP])
        earlier = s.sb("earlier", [P, NT, TOK])
        norm = Norm(s)
        probs = s.sb("probs", [P, NT, E_N])
        above = s.sb("above", [P, NT, E_N, E_N])
        equal = s.sb("equal", [P, NT, E_N, E_N])
        rank8 = s.sb("rank8", [P, NT, E_N])
        stat = s.sb("stat", [P, NT])
        gate = s.sb("gate", [P, NT, E_N + 1])
        gate_rows = s.sb("gate_rows", [P, E_N + 1, TOK])
        compared = s.sb("compared", [P, TOK])
        better = s.sb("better", [P, NT])
        level = s.sb("level", [P, NT])
        place = s.sb("place", [P, NT])
        pick = s.sb("pick", [P, NT, CAP])
        pick_gate = s.sb("pick_gate", [P, NT, CAP])
        picked_T = s.sb("picked_T", [P, KD, CAP])
        put_back = s.sb("put_back", [P, 2, NT, P])
        hidden = s.sb("hidden", [P, FC, CAP])
        y_T = s.sb("y_T", [P, KD, CAP])
        y = s.sb("y", [P, 2, D])
        zero = s.sb("zero", [1, D])
        acc = [s.ps(f"acc{t}", [P, D]) for t in range(NT)]
        ring = [s.ps(f"ring{i}", [P, 512]) for i in range(2)]
        side = [s.ps(f"side{i}", [P, 512]) for i in range(2)]
        r_in, w1_in, w2_in = s.sem("r_in"), s.sem("w1_in"), s.sem("w2_in")
        pool_own, dve_own = s.sem("pool_own"), s.sem("dve_own")
        turned_full, turned_out, routed, centred = (s.sem("turned_full"), s.sem("turned_out"), s.sem("routed"),
                                                    s.sem("centred"))
        exped, gates_ready, rows_full, rows_out = (s.sem("exped"), s.sem("gates_ready"), s.sem("rows_full"),
                                                   s.sem("rows_out"))
        picks_ready = s.sem("picks_ready")
        side_full, side_out = s.sem("side_full"), s.sem("side_out")
        ring_full, ring_out = s.sem("ring_full"), s.sem("ring_out")
        acc_full = s.sem("acc_full")
        N_SIDE = 6
        N_RING = len(TRIPLES) + 2
        block = s.block()

        def load(sp, w, name, e, sem):
            sp.dma_start(w[:], d[name][bass.ds(e, 1)].rearrange("a p k n -> p (a k) n")).then_inc(sem, 16)

        @block.sync
        def _(sp):
            sp.dma_start(w_route[:], d["L1_ffn_Wr"]).then_inc(r_in, 16)
            sp.dma_start(before[:], rows(d["before"])).then_inc(r_in, 16)
            sp.dma_start(slots[:], rows(d["slots"])).then_inc(r_in, 16)
            load(sp, w1, "L1_ffn_W1", 0, w1_in)
            load(sp, w2, "L1_ffn_W2", 0, w2_in)
            with sp.Fori(0, E_N - 1) as e:
                sp.wait_ge(ring_full, e * N_RING + len(TRIPLES))
                load(sp, w1, "L1_ffn_W1", e + 1, w1_in)
                sp.wait_ge(ring_full, e * N_RING + N_RING)
                load(sp, w2, "L1_ffn_W2", e + 1, w2_in)

        @block.gpsimd
        def _(pool):
            pool.memset(zero[:], 0.0).then_inc(pool_own, 1)
            pool.wait_ge(pool_own, 1)
            pool.memset(gate[:], 0.0).then_inc(pool_own, 1)
            pool.wait_ge(pool_own, 2)
            pool.memset(gate_rows[:, E_N, :], 0.0).then_inc(pool_own, 1)
            pool.wait_ge(pool_own, 3)
            pool.memset(earlier[:], 1.0).then_inc(pool_own, 1)
            pool.wait_ge(pool_own, 4)
            pool.affine_select(out=earlier[:], in_=earlier[:], compare_op=ALU.is_gt, fill=0.0, base=0,
                               pattern=[[P, NT], [-1, TOK]], channel_multiplier=1).then_inc(pool_own, 1)

        @block.vector
        def _(dve):
            for signal in (side_out,):
                dve.sem_inc(signal, FIRST)
            own = Steps(dve, dve_own)
            norm.on_vector(dve, g.x, g.hn)
            dve.wait_ge(r_in, 48)
            dve.wait_ge(pool_own, 5)
            dve.wait_ge(routed, 1)
            logits = side[0][:, 0:NT * E_N].rearrange("p (t e) -> p t e", t=NT)
            own.did(dve.tensor_reduce(stat[:], logits, AXX, ALU.max))
            own.wait()
            dve.tensor_tensor(probs[:], logits, stat[:].unsqueeze(2).to_broadcast([P, NT, E_N]),
                              ALU.subtract).then_inc(centred, 1)
            dve.wait_ge(exped, 1)
            own.did(dve.tensor_reduce(stat[:], probs[:], AXX, ALU.add))
            own.wait()
            own.did(dve.reciprocal(stat[:], stat[:]))
            own.wait()
            own.did(dve.tensor_tensor(probs[:], probs[:], stat[:].unsqueeze(2).to_broadcast([P, NT, E_N]), ALU.mult))
            own.wait()
            choose(dve, own, probs, above, equal, before, rank8, gate[:, :, 0:E_N])
            dve.sem_inc(gates_ready, 1)

            def place_tokens(e, own, turned=None):
                row = gate_rows[:, bass.ds(e, 1), :].rearrange("p a n -> p (a n)")
                for t in range(NT):
                    mine = gate[:, t, bass.ds(e, 1)]
                    own.did(dve.tensor_scalar(compared[:], row, mine, 0.0, ALU.is_gt, ALU.add,
                                              accum_out=better[:, t:t + 1]))
                    own.wait()
                    own.did(dve.scalar_tensor_tensor(out=compared[:], in0=row, scalar=mine, in1=earlier[:, t, :],
                                                     op0=ALU.is_equal, op1=ALU.mult,
                                                     accum_out=level[:, t:t + 1]))
                    own.wait()
                own.did(dve.tensor_tensor(place[:], better[:], level[:], ALU.add))
                own.wait()
                if turned:
                    dve.wait_ge(*turned)
                for t in range(NT):
                    dve.tensor_scalar(pick[:, t, :], slots[:], place[:, t:t + 1], None,
                                      ALU.is_equal).then_inc(picks_ready, 1)
                    dve.tensor_scalar(pick_gate[:, t, :], slots[:], place[:, t:t + 1], gate[:, t, bass.ds(e, 1)],
                                      ALU.is_equal, ALU.mult).then_inc(picks_ready, 1)

            dve.wait_ge(rows_out, E_N)
            place_tokens(0, own)
            with dve.Fori(0, E_N) as e:
                restart(dve, dve_own)
                own = Steps(dve, dve_own)
                dve.wait_ge(side_full, e * N_SIDE + 1)
                dve.tensor_copy(picked_T[:, 0:3, :], side[0][:, 0:3 * CAP].rearrange("p (k n) -> p k n", k=3)
                                ).then_inc(side_out, 1)
                dve.wait_ge(side_full, e * N_SIDE + 2)
                dve.tensor_copy(picked_T[:, 3, :], side[1][:, 0:CAP]).then_inc(side_out, 1)
                dve.wait_ge(acc_full, e + FIRST)
                for j in range(2):
                    m = P if j == 0 else REST
                    dve.wait_ge(side_full, e * N_SIDE + (3 + j))
                    dve.tensor_copy(put_back[0:m, j, :, :], side[j][0:m, :].rearrange("p (t n) -> p t n", t=NT)
                                    ).then_inc(side_out, 1)
                place_tokens(e + 1, own, (side_full, e * N_SIDE + 4))
                for j in range(2):
                    m = P if j == 0 else REST
                    dve.wait_ge(side_full, e * N_SIDE + (5 + j))
                    dve.tensor_copy(y[0:m, j, :], side[j][0:m, :]).then_inc(side_out, 1)
                own.wait()
            for t in range(NT):
                dve.wait_ge(acc_full, E_N + FIRST)
                dve.tensor_tensor(g.x[:, t, :], acc[t][:], g.x[:, t, :], ALU.add).then_inc(side_out, 1)

        @block.scalar
        def _(act):
            for signal in (ring_out,):
                act.sem_inc(signal, FIRST)
            norm.on_scalar(act, g.eps[:])
            for t in range(NT):
                act.wait_ge(turned_full, t + 1)
                act.activation(g.hT[:, :, t * P:(t + 1) * P], acc[t][:].rearrange("p (k n) -> p k n", k=KD),
                               ACT.Copy).then_inc(turned_out, 1)
            act.wait_ge(centred, 1)
            act.activation(probs[:], probs[:], ACT.Exp).then_inc(exped, 1)
            act.wait_ge(pool_own, 5)
            for e in range(E_N):
                act.wait_ge(rows_full, e + 1)
                act.activation(gate_rows[:, e, :], acc[e % NT][:], ACT.Copy).then_inc(rows_out, 1)
            with act.Fori(0, E_N) as e:
                for n, (lo, hi) in enumerate(TRIPLES):
                    act.wait_ge(ring_full, e * N_RING + (n + 1))
                    act.activation(hidden[:, lo:hi, :], ring[n % 2][:, 0:(hi - lo) * CAP]
                                   .rearrange("p (m n) -> p m n", m=hi - lo), ACT.Relu).then_inc(ring_out, 1)
                for j, (lo, hi) in enumerate(((0, 3), (3, 4))):
                    n = len(TRIPLES) + j
                    act.wait_ge(ring_full, e * N_RING + (n + 1))
                    act.activation(y_T[:, lo:hi, :], ring[n % 2][:, 0:(hi - lo) * CAP]
                                   .rearrange("p (m n) -> p m n", m=hi - lo), ACT.Copy).then_inc(ring_out, 1)

        @block.tensor
        def _(pe):
            for signal in (acc_full,):
                pe.sem_inc(signal, FIRST)
            pe.wait_ge(norm.normed, NT)
            for t in range(NT):
                for k in range(KD):
                    last = pe.transpose(acc[t][:, k * P:(k + 1) * P], g.hn[:, t, k * P:(k + 1) * P], g.ident[:])
                last.then_inc(turned_full, 1)
            pe.wait_ge(turned_out, NT)
            pe.wait_ge(r_in, 48)
            for t in range(NT):
                for k in range(KD):
                    last = pe.matmul(side[0][:, t * E_N:(t + 1) * E_N], g.hT[:, k, t * P:(t + 1) * P],
                                     w_route[:, k, :], start=(k == 0), stop=(k == KD - 1))
            last.then_inc(routed, 1)
            pe.wait_ge(gates_ready, 1)
            for e in range(E_N):
                if e >= NT:
                    pe.wait_ge(rows_out, e - NT + 1)
                for t in range(NT):
                    last = pe.transpose(acc[e % NT][:, t * P:(t + 1) * P], gate[:, t, e:e + 1].to_broadcast([P, P]),
                                        g.ident[:])
                last.then_inc(rows_full, 1)
            pe.wait_ge(rows_out, E_N)
            for t in range(NT):
                pe.matmul(acc[t][:], zero[:, 0:P], zero[:], start=True, stop=False, skip_group_check=True)
            assert N_RING % 2 == 0 and N_SIDE % 2 == 0
            with pe.Fori(0, E_N) as e:
                pe.wait_ge(picks_ready, e * 2 * NT + 2 * NT)
                for k in range(KD):
                    if k == 0:
                        pe.wait_ge(side_out, e * N_SIDE + FIRST)
                    out = side[0][:, k * CAP:(k + 1) * CAP] if k < 3 else side[1][:, 0:CAP]
                    for t in range(NT):
                        last = pe.matmul(out, g.hn[:, t, k * P:(k + 1) * P], pick[:, t, :], start=(t == 0),
                                         stop=(t == NT - 1))
                    if k >= 2:
                        last.then_inc(side_full, 1)
                for j in range(2):
                    m = P if j == 0 else REST
                    pe.wait_ge(side_out, e * N_SIDE + (1 + j) + FIRST)
                    for t in range(NT):
                        last = pe.transpose(side[j][0:m, t * P:(t + 1) * P], pick_gate[:, t, j * P:j * P + m],
                                            g.ident[:])
                    last.then_inc(side_full, 1)
                pe.wait_ge(side_out, e * N_SIDE + 2 + FIRST)
                pe.wait_ge(w1_in, e * 16 + 16)
                for n, (lo, hi) in enumerate(TRIPLES):
                    pe.wait_ge(ring_out, e * N_RING + (n - 1 if n >= 2 else 0) + FIRST)
                    for m in range(lo, hi):
                        for k in range(KD):
                            last = pe.matmul(ring[n % 2][:, (m - lo) * CAP:(m - lo + 1) * CAP],
                                             w1[:, k, m * P:(m + 1) * P], picked_T[:, k, :], start=(k == 0),
                                             stop=(k == KD - 1))
                    last.then_inc(ring_full, 1)
                pe.wait_ge(w2_in, e * 16 + 16)
                for j, (lo, hi) in enumerate(((0, 3), (3, 4))):
                    n = len(TRIPLES) + j
                    pe.wait_ge(ring_out, e * N_RING + len(TRIPLES) + FIRST)
                    for m in range(lo, hi):
                        for k in range(FC):
                            last = pe.matmul(ring[n % 2][:, (m - lo) * CAP:(m - lo + 1) * CAP],
                                             w2[:, k, m * P:(m + 1) * P], hidden[:, k, :], start=(k == 0),
                                             stop=(k == FC - 1))
                    last.then_inc(ring_full, 1)
                pe.wait_ge(ring_out, e * N_RING + N_RING + FIRST)
                for j in range(2):
                    m = P if j == 0 else REST
                    pe.wait_ge(side_out, e * N_SIDE + (3 + j) + FIRST)
                    for k in range(KD):
                        last = pe.transpose(side[j][0:m, k * P:(k + 1) * P], y_T[:, k, j * P:j * P + m], g.ident[:])
                    last.then_inc(side_full, 1)
                pe.wait_ge(side_out, e * N_SIDE + 6 + FIRST)
                for t in range(NT):
                    for j in range(2):
                        m = P if j == 0 else REST
                        last = pe.matmul(acc[t][:], put_back[0:m, j, t, :], y[0:m, j, :], start=False,
                                         stop=(j == 1), skip_group_check=True)
                last.then_inc(acc_full, 1)


S4 = 64
MAGIC = 1.5 * 2.0 ** 23
TWO_PI = (6.28125, 0.0019350051879882812, 3.019916e-07)
PI_BELOW = 3.1415925


class StateSpace:

    SMALL = ("ar", "ai", "er", "rs", "rc", "wr", "wi", "nr", "ni", "t0", "t1", "t2")

    def __init__(self, s, g):
        self.g, self.s = g, s
        n = [P, KD, S4]
        self.inp = {k: s.sb(f"ss_{k}", n) for k in ("A_re", "A_im", "C_re", "C_im")}
        self.dt = s.sb("ss_dt", [P, KD])
        self.skip = s.sb("ss_skip", [P, KD])
        self.v = {k: s.sb(f"ss_{k}", n) for k in self.SMALL}
        self.re = s.sb("ss_re", [P, SEQ, S4])
        self.im = s.sb("ss_im", [P, SEQ // 2, S4])
        self.tmp = s.sb("ss_tmp", [P, SEQ // 2, S4])
        self.loaded, self.own = s.sem("ss_loaded"), s.sem("ss_own")
        self.dt_ready, self.phased, self.waved, self.dt_used = (s.sem("ss_dt_ready"), s.sem("ss_phased"),
                                                                s.sem("ss_waved"), s.sem("ss_dt_used"))
        self.inverse_in, self.inverse_out = s.sem("ss_inverse_in"), s.sem("ss_inverse_out")

    def on_sync(self, sp):
        d = self.g.dram
        for k, t in self.inp.items():
            sp.dma_start(t[:], d[f"L1_xattn_{k}"]).then_inc(self.loaded, 16)
        sp.dma_start(self.dt[:], d["L1_xattn_log_dt"]).then_inc(self.loaded, 16)
        sp.dma_start(self.skip[:], d["L1_xattn_D_skip"]).then_inc(self.loaded, 16)

    def on_scalar(self, act):
        v = self.v
        act.wait_ge(self.loaded, 96)
        act.activation(self.dt[:], self.dt[:], ACT.Exp).then_inc(self.dt_ready, 1)
        act.wait_ge(self.phased, 1)
        act.activation(v["er"][:], v["ar"][:], ACT.Exp).then_inc(self.waved, 1)
        act.activation(v["rs"][:], v["rs"][:], ACT.Sin).then_inc(self.waved, 1)
        act.activation(v["rc"][:], v["rc"][:], ACT.Sin).then_inc(self.waved, 1)

    def on_vector(self, dve):
        dve.wait_ge(self.inverse_in, 1)
        dve.reciprocal(self.v["t2"][:], self.v["t2"][:]).then_inc(self.inverse_out, 1)

    def on_gpsimd(self, pool):
        v, inp, own = self.v, self.inp, Steps(pool, self.own)

        def tt(out, a, b, op):
            own.did(pool.tensor_tensor(out, a, b, op))
            own.wait()

        def ts(out, a, s1, s2, op0, op1):
            own.did(pool.tensor_scalar(out, a, s1, s2, op0, op1))
            own.wait()

        a = {k: t[:] for k, t in v.items()}
        a.update({k: t[:] for k, t in inp.items()})
        pool.wait_ge(self.dt_ready, 1)
        dt = self.dt[:].unsqueeze(2).to_broadcast([P, KD, S4])
        tt(a["ar"], a["A_re"], dt, ALU.mult)
        tt(a["ai"], a["A_im"], dt, ALU.mult)
        for out, shift in (("rs", 0.0), ("rc", 0.25)):
            ts(a["t0"], a["ai"], 1 / (2 * np.pi), shift, ALU.mult, ALU.add)
            ts(a["t0"], a["t0"], MAGIC, -MAGIC, ALU.add, ALU.add)
            src = a["ai"]
            for part in TWO_PI:
                ts(a["t1"], a["t0"], -part, 0.0, ALU.mult, ALU.add)
                tt(a[out], src, a["t1"], ALU.add)
                src = a[out]
            if shift:
                ts(a[out], a[out], np.pi / 2, 0.0, ALU.add, ALU.add)
            ts(a[out], a[out], PI_BELOW, -PI_BELOW, ALU.min, ALU.max)
        pool.sem_inc(self.phased, 1)
        tt(a["t0"], a["A_re"], a["A_re"], ALU.mult)
        tt(a["t1"], a["A_im"], a["A_im"], ALU.mult)
        tt(a["t2"], a["t0"], a["t1"], ALU.add)
        pool.sem_inc(self.inverse_in, 1)
        pool.wait_ge(self.waved, 3)
        tt(a["wr"], a["er"], a["rc"], ALU.mult)
        tt(a["wi"], a["er"], a["rs"], ALU.mult)
        ts(a["er"], a["wr"], -1.0, 0.0, ALU.add, ALU.add)
        tt(a["t0"], a["er"], a["A_re"], ALU.mult)
        tt(a["t1"], a["wi"], a["A_im"], ALU.mult)
        tt(a["nr"], a["t0"], a["t1"], ALU.add)
        tt(a["t0"], a["wi"], a["A_re"], ALU.mult)
        tt(a["t1"], a["er"], a["A_im"], ALU.mult)
        tt(a["ni"], a["t0"], a["t1"], ALU.subtract)
        pool.wait_ge(self.inverse_out, 1)
        ts(a["t2"], a["t2"], 2.0, 0.0, ALU.mult, ALU.add)
        tt(a["nr"], a["nr"], a["t2"], ALU.mult)
        tt(a["ni"], a["ni"], a["t2"], ALU.mult)
        tt(a["t0"], a["nr"], a["C_re"], ALU.mult)
        tt(a["t1"], a["ni"], a["C_im"], ALU.mult)
        tt(a["rs"], a["t0"], a["t1"], ALU.subtract)
        tt(a["t0"], a["nr"], a["C_im"], ALU.mult)
        tt(a["t1"], a["ni"], a["C_re"], ALU.mult)
        tt(a["rc"], a["t0"], a["t1"], ALU.add)
        re, im, tmp = self.re, self.im, self.tmp
        for c in range(KD):
            one = [P, 1, S4]
            wr, wi = v["wr"][:, c:c + 1, :], v["wi"][:, c:c + 1, :]
            tt(re[:, 0:1, :], v["rs"][:, c:c + 1, :], self.g.zero[:].to_broadcast(one), ALU.add)
            tt(im[:, 0:1, :], v["rc"][:, c:c + 1, :], self.g.zero[:].to_broadcast(one), ALU.add)
            h = 1
            while h < SEQ:
                br, bi = wr.to_broadcast([P, h, S4]), wi.to_broadcast([P, h, S4])
                tt(re[:, h:2 * h, :], re[:, 0:h, :], br, ALU.mult)
                tt(tmp[:, 0:h, :], im[:, 0:h, :], bi, ALU.mult)
                tt(re[:, h:2 * h, :], re[:, h:2 * h, :], tmp[:, 0:h, :], ALU.subtract)
                if 2 * h < SEQ:
                    tt(im[:, h:2 * h, :], im[:, 0:h, :], br, ALU.mult)
                    tt(tmp[:, 0:h, :], re[:, 0:h, :], bi, ALU.mult)
                    tt(im[:, h:2 * h, :], im[:, h:2 * h, :], tmp[:, 0:h, :], ALU.add)
                    t0, t1 = v["t0"][:, c:c + 1, :], v["t1"][:, c:c + 1, :]
                    tt(t0, wr, wr, ALU.mult)
                    tt(t1, wi, wi, ALU.mult)
                    tt(wi, wr, wi, ALU.mult)
                    ts(wi, wi, 2.0, 0.0, ALU.mult, ALU.add)
                    tt(wr, t0, t1, ALU.subtract)
                h *= 2
            n = S4 // 2
            while n:
                out = re[:, :, 0:n] if n > 1 else self.g.kern[:, c, :].unsqueeze(2)
                tt(out, re[:, :, 0:n], re[:, :, n:2 * n], ALU.add)
                n //= 2
        tt(self.g.kern[:, :, 0], self.g.kern[:, :, 0], self.skip[:], ALU.add)


def xattn1_context(g, c_T):
    nc, d = g.nc, g.dram
    HD, HEADS, ROUNDS = 32, 4, 4
    SCALE = 1.0 / float(np.sqrt(32.0))
    CHUNKS = [(0, 512), (512, 1024), (1024, 1536), (1536, CTX)]
    PER_KS = 4 + 2 * 4

    def size(t):
        return P if t < CFULL else CLAST

    with Stage(nc, "d2") as s:
        wq = s.sb("wq", [P, KD, P])
        wk = s.sb("wk", [P, KC, P])
        norm = Norm(s)
        q_T = s.sb("q_T", [P, TOK])
        q_diag = s.sb("q_diag", [P, 2, P])
        ones = s.sb("ones", [1, P])
        stack = s.sb("stack", [P, SEQ])
        context = s.sb("context", [P, 2, CT, DC])
        mask8 = s.sb("mask8", [1, 2, CTX], U8)
        mask = s.sb("mask", [1, CTX])
        context_T = s.sb("context_T", [P, KC, CTX])
        k_T = s.sb("k_T", [P, CTX])
        scores = s.sb("scores", [P, 4, CTX])
        left = s.sb("left", [P, 2, CTX])
        best = s.sb("best", [P, 4, ROUNDS * 8])
        neg_top = s.sb("neg_top", [P, 4])
        best_exp = s.sb("best_exp", [P, ROUNDS * 8])
        total = s.sb("total", [P, 4])
        share = s.sb("share", [P, 2, SEQ])
        mean_T = s.sb("mean_T", [P, CT, SEQ])
        ring = [s.ps(f"ring{i}", [P, 4, P]) for i in range(2)]
        ks = [s.ps(f"ks{i}", [P, 512]) for i in range(3)]
        mean = [s.ps(f"mean{i}", [P, 8, SEQ]) for i in range(2)]
        mix = s.ps("mix", [P, KC, SEQ])
        w_in = s.sem("w_in")
        ctx_in = [s.sem(f"ctx_in{i}") for i in range(2)]
        pool_own, dve_own, act_own = s.sem("pool_own"), s.sem("dve_own"), s.sem("act_own")
        q_full, q_out = s.sem("q_full"), s.sem("q_out")
        side_ready = s.sem("side_ready")
        ring_full, ring_out = s.sem("ring_full"), s.sem("ring_out")
        ks_full, ks_out = s.sem("ks_full"), s.sem("ks_out")
        picked, exped, probs_ready, share_ready = (s.sem("picked"), s.sem("exped"), s.sem("probs_ready"),
                                                   s.sem("share_ready"))
        mean_full, mean_out, mix_full, mix_out = (s.sem("mean_full"), s.sem("mean_out"), s.sem("mix_full"),
                                                  s.sem("mix_out"))
        block = s.block()

        def in_turn(eng, step):
            with eng.Fori(0, NB // 2 - 1) as i:
                for par in range(2):
                    step(i * 2 + par, par, False)
            for par in range(2):
                step(NB - 2 + par, par, par == 1)

        @block.sync
        def _(sp):
            sp.dma_start(wq[:], d["L1_xattn_Wq"]).then_inc(w_in, 16)
            sp.dma_start(wk[:], d["L1_xattn_Wk"]).then_inc(w_in, 16)

            def load(b, par):
                src = d["ctx"][bass.ds(b, 1)].rearrange("a s d -> (a s) d")
                for lo in range(0, CFULL, 4):
                    sp.dma_start(context[:, par, lo:lo + 4, :],
                                 src[lo * P:(lo + 4) * P, :].rearrange("(t p) d -> p t d", p=P)
                                 ).then_inc(ctx_in[par], 16)
                sp.dma_start(context[0:CLAST, par, CFULL, :], src[CFULL * P:CTX, :]).then_inc(ctx_in[par], 16)
                sp.dma_start(mask8[:, par, :], d["mask_ctx1"][bass.ds(b, 1), :]).then_inc(ctx_in[par], 16)

            for par in range(2):
                load(par, par)
            with sp.Fori(0, NB // 2 - 1) as i:
                for par in range(2):
                    b = i * 2 + par
                    sp.wait_ge(mix_full, b + 1)
                    load(b + 2, par)

        @block.gpsimd
        def _(pool):
            pool.memset(q_diag[:], 0.0).then_inc(pool_own, 1)
            pool.wait_ge(pool_own, 1)
            pool.memset(ones[:], 1.0).then_inc(pool_own, 1)
            pool.wait_ge(pool_own, 2)
            pool.tensor_tensor(stack[:], g.ident[:, 0:SEQ], g.ident[:, SEQ:P], ALU.add).then_inc(pool_own, 1)
            pool.wait_ge(pool_own, 3)
            pool.wait_ge(q_out, 1)
            SIDE = 1 + HEADS

            def prepare(b, par):
                pool.wait_ge(ctx_in[par], (b - par) * (16 * 5 // 2) + 16 * 5)
                pool.wait_ge(ks_full, b * PER_KS)
                pool.nop(nofuse=True)
                pool.tensor_scalar(mask[:], mask8[:, par, :], -MASKED, MASKED, ALU.mult,
                                   ALU.add).then_inc(side_ready, 1)
                for h in range(HEADS):
                    pool.wait_ge(side_ready, b * SIDE + (1 + h))
                    r = slice(h * HD, (h + 1) * HD)
                    pool.tensor_copy(q_diag[r, h // 2, (h % 2) * SEQ:(h % 2 + 1) * SEQ],
                                     q_T[r, bass.ds(b * SEQ, SEQ)]).then_inc(side_ready, 1)
                pool.wait_ge(side_ready, b * SIDE + SIDE)

            def step(b, par, last):
                if not last:
                    prepare(b + 1, 1 - par)
                for r in range(2):
                    pool.wait_ge(exped, b * 2 + (r + 1))
                    sc = scores[:, 2 * par + r, :]
                    pool.tensor_tensor(sc, sc, left[:, r, :], ALU.subtract).then_inc(probs_ready, 1)
                    pool.wait_ge(probs_ready, b * 2 + (r + 1))

            prepare(0, 0)
            in_turn(pool, step)

        @block.vector
        def _(dve):
            norm.on_vector(dve, g.x, g.hn)

            def pick(par, r, rounds, after=None):
                own = Steps(dve, dve_own, rounds[0] * 2)
                sc = scores[:, 2 * par + r, :]
                for n in rounds:
                    src = sc if n == 0 else left[:, r, :]
                    eight = best[:, 2 * par + r, 8 * n:8 * n + 8]
                    own.did(dve.max(eight, src))
                    own.wait()
                    if n == 0:
                        if after is not None:
                            dve.wait_ge(probs_ready, after)
                            dve.nop(nofuse=True)
                    ins = dve.match_replace(left[:, r, :], eight, src, MASKED)
                    if n < ROUNDS - 1:
                        own.did(ins)
                        own.wait()
                    else:
                        ins.then_inc(picked, 1)

            def shares(b, par):
                own = Steps(dve, dve_own, 2)
                dve.wait_ge(exped, b * 2 + 2)
                own.did(dve.reciprocal(total[:, 2 * par:2 * par + 2], total[:, 2 * par:2 * par + 2]))
                own.wait()
                dve.wait_ge(mean_full, b * 2 + FIRST)
                for r in range(2):
                    dve.tensor_scalar(share[:, r, :], stack[:], total[:, 2 * par + r:2 * par + r + 1], 1.0 / HEADS,
                                      ALU.mult, ALU.mult).then_inc(share_ready, 1)

            def first(b, par):
                dve.wait_ge(ks_out, b * PER_KS + (8 + 3))
                restart(dve, dve_own)
                pick(par, 0, range(ROUNDS))
                dve.wait_ge(ks_out, b * PER_KS + (12 + 3))
                restart(dve, dve_own)
                pick(par, 1, range(ROUNDS))

            def step(b, par, last):
                if last:
                    restart(dve, dve_own)
                    dve.sem_inc(dve_own, 2)
                    shares(b, par)
                    return
                q = 1 - par
                dve.wait_ge(ks_out, (b + 1) * PER_KS + (8 + 3))
                restart(dve, dve_own)
                pick(q, 0, range(0, 1), b * 2 + 1)
                shares(b, par)
                pick_rest(q)
                dve.wait_ge(picked, (b + 1) * 2 + 1)
                dve.wait_ge(ks_out, (b + 1) * PER_KS + (12 + 3))
                restart(dve, dve_own)
                pick(q, 1, range(ROUNDS), b * 2 + 2)
                dve.wait_ge(picked, (b + 1) * 2 + 2)

            def pick_rest(par):
                own = Steps(dve, dve_own, 3)
                for n in range(1, ROUNDS):
                    eight = best[:, 2 * par, 8 * n:8 * n + 8]
                    own.did(dve.max(eight, left[:, 0, :]))
                    own.wait()
                    ins = dve.match_replace(left[:, 0, :], eight, left[:, 0, :], MASKED)
                    if n < ROUNDS - 1:
                        own.did(ins)
                        own.wait()
                    else:
                        ins.then_inc(picked, 1)

            first(0, 0)
            dve.wait_ge(picked, 2)
            in_turn(dve, step)

        @block.scalar
        def _(act):
            for signal in (mean_out, mix_out,):
                act.sem_inc(signal, FIRST)
            norm.on_scalar(act, g.eps[:])
            for t in range(NT):
                act.wait_ge(ring_full, t + 1)
                act.activation(g.hT[:, :, t * P:(t + 1) * P], ring[t % 2][:], ACT.Copy).then_inc(ring_out, 1)
            act.wait_ge(q_full, 1)
            act.activation(q_T[:], ks[0][:], ACT.Copy).then_inc(q_out, 1)
            act.wait_ge(ring_out, NT)
            act.wait_ge(q_out, 1)
            act.sem_inc(ks_out, 3)

            def put_context(b, par):
                for t in range(CT):
                    m = size(t)
                    act.wait_ge(ring_full, b * CT + (t + 1 + NT))
                    act.activation(context_T[:, :, t * P:t * P + m], ring[(par * CT + t) % 2][:, 0:KC, 0:m],
                                   ACT.Copy).then_inc(ring_out, 1)
                    if t % 4 == 3:
                        put_keys(b, t // 4)
                put_keys(b, 3)

            def put_keys(b, c):
                lo, hi = CHUNKS[c]
                act.wait_ge(ks_full, b * PER_KS + (c + 1))
                act.activation(k_T[:, lo:hi], ks[c % 3][:, 0:hi - lo], ACT.Copy).then_inc(ks_out, 1)

            def put_scores(b, par):
                if not (isinstance(b, int) and b < 2):
                    act.wait_ge(mean_full, (b - 2) * 2 + 2 + FIRST)
                for n in range(8):
                    r, c = n // 4, n % 4
                    lo, hi = CHUNKS[c]
                    act.wait_ge(ks_full, b * PER_KS + (4 + n + 1))
                    act.activation(scores[:, 2 * par + r, lo:hi], ks[(4 + n) % 3][:, 0:hi - lo],
                                   ACT.Copy).then_inc(ks_out, 1)

            def exponentials(b, par, r):
                i = 2 * par + r
                act.wait_ge(picked, b * 2 + (r + 1))
                restart(act, act_own)
                act.activation(neg_top[:, i:i + 1], best[:, i, 0:1], ACT.Copy, scale=-SCALE).then_inc(act_own, 1)
                act.wait_ge(act_own, 1)
                top = neg_top[:, i:i + 1]
                act.activation(best_exp[:], best[:, i, :], ACT.Exp, bias=top, scale=SCALE,
                               accum_out=total[:, i:i + 1]).then_inc(act_own, 1)
                act.activation(scores[:, i, :], scores[:, i, :], ACT.Exp, bias=top, scale=SCALE).then_inc(act_own, 1)
                act.activation(left[:, r, :], left[:, r, :], ACT.Exp, bias=top, scale=SCALE).then_inc(act_own, 1)
                act.wait_ge(act_own, 4)
                act.sem_inc(exped, 1)

            def step(b, par, last):
                if not last:
                    put_context(b + 1, 1 - par)
                exponentials(b, par, 0)
                if not last:
                    put_scores(b + 1, 1 - par)
                exponentials(b, par, 1)
                for j in range(2):
                    act.wait_ge(mean_full, b * 2 + (j + 1) + FIRST)
                    if j == 0:
                        act.activation(mean_T[:, 0:8, :], mean[0][:], ACT.Copy).then_inc(mean_out, 1)
                    else:
                        act.activation(mean_T[:, 8:CFULL, :], mean[1][:, 0:CFULL - 8, :],
                                       ACT.Copy).then_inc(mean_out, 1)
                        act.activation(mean_T[0:CLAST, CFULL, :], mean[1][0:CLAST, CFULL - 8, :],
                                       ACT.Copy).then_inc(mean_out, 1)
                act.wait_ge(mix_full, b + 1)
                act.activation(c_T[:, :, bass.ds(b * SEQ, SEQ)], mix[:], ACT.Copy).then_inc(mix_out, 1)

            put_context(0, 0)
            put_scores(0, 0)
            in_turn(act, step)

        @block.tensor
        def _(pe):
            for signal in (mean_full,):
                pe.sem_inc(signal, FIRST)
            pe.wait_ge(norm.normed, NT)
            for t in range(NT):
                if t >= 2:
                    pe.wait_ge(ring_out, t - 1)
                for k in range(KD):
                    last = pe.transpose(ring[t % 2][:, k, :], g.hn[:, t, k * P:(k + 1) * P], g.ident[:])
                last.then_inc(ring_full, 1)
            pe.wait_ge(ring_out, NT)
            pe.wait_ge(w_in, 32)
            for k in range(KD):
                last = pe.matmul(ks[0][:], wq[:, k, :], g.hT[:, k, :], start=(k == 0), stop=(k == KD - 1))
            last.then_inc(q_full, 1)
            pe.wait_ge(q_out, 1)
            pe.wait_ge(pool_own, 3)

            def prepare(b, par):
                pe.wait_ge(ctx_in[par], (b - par) * (16 * 5 // 2) + 16 * 5)
                for t in range(CT):
                    m = size(t)
                    pe.wait_ge(ring_out, b * CT + (t - 1 + NT))
                    for k in range(KC):
                        last = pe.transpose(ring[(par * CT + t) % 2][:, k, 0:m],
                                            context[0:m, par, t, k * P:(k + 1) * P], g.ident[0:m, 0:m])
                    last.then_inc(ring_full, 1)
                    if t % 4 == 0 and t:
                        keys(b, t // 4 - 1)
                keys(b, 3)
                pe.wait_ge(side_ready, b * 5 + 5)
                for n in range(8):
                    r, c = n // 4, n % 4
                    lo, hi = CHUNKS[c]
                    if n == 0:
                        pe.wait_ge(ks_out, b * PER_KS + (4 + 3))
                    pe.wait_ge(ks_out, b * PER_KS + (4 + n + 1))
                    out = ks[(4 + n) % 3][:, 0:hi - lo]
                    pe.matmul(out, q_diag[:, r, :], k_T[:, lo:hi], start=True, stop=False)
                    pe.matmul(out, ones[:], mask[:, lo:hi], start=False, stop=True).then_inc(ks_full, 1)

            def keys(b, c):
                lo, hi = CHUNKS[c]
                pe.wait_ge(ring_out, b * CT + (min(4 * c + 4, CT) + NT))
                pe.wait_ge(ks_out, b * PER_KS + (c + 1))
                for k in range(KC):
                    last = pe.matmul(ks[c % 3][:, 0:hi - lo], wk[:, k, :], context_T[:, k, lo:hi], start=(k == 0),
                                     stop=(k == KC - 1))
                last.then_inc(ks_full, 1)

            def step(b, par, last):
                if not last:
                    prepare(b + 1, 1 - par)
                pe.wait_ge(share_ready, b * 2 + 2)
                pe.wait_ge(probs_ready, b * 2 + 2)
                pe.wait_ge(mean_out, b * 3 + FIRST)
                for t in range(CT):
                    m = size(t)
                    for r in range(2):
                        ins = pe.matmul(mean[t // 8][0:m, t % 8, :], scores[:, 2 * par + r, t * P:t * P + m],
                                        share[:, r, :], start=(r == 0), stop=(r == 1))
                    if t in (7, CFULL):
                        ins.then_inc(mean_full, 1)
                pe.wait_ge(mean_out, b * 3 + 3 + FIRST)
                pe.wait_ge(mix_out, b + FIRST)
                for f in range(KC):
                    for t in range(CT):
                        m = size(t)
                        ins = pe.matmul(mix[:, f, :], context[0:m, par, t, f * P:(f + 1) * P], mean_T[0:m, t, :],
                                        start=(t == 0), stop=(t == CT - 1))
                ins.then_inc(mix_full, 1)

            prepare(0, 0)
            in_turn(pe, step)


def film_and_mlp(g, c_T):
    nc, d = g.nc, g.dram
    F = 2048
    FC = F // P
    with Stage(nc, "d3") as s:
        w_v = s.sb("w_v", [P, KC, D])
        w_in_film = s.sb("w_in_film", [P, KD, 2 * D])
        w_out_film = s.sb("w_out_film", [P, KD, 2 * D])
        w_wide = s.sb("w_wide", [P, KD, F])
        w_down = s.sb("w_down", [P, KD, D])
        vecs = {n: s.sb(f"v_{n}", [P, k]) for n, k in (("g_norm_in", KD), ("b_norm_in", KD), ("g_ffn", KD),
                                                       ("b_ffn", KD), ("b_film_in", 2 * KD), ("b_film_out", 2 * KD),
                                                       ("b1", FC), ("mod_gate", 1))}
        long = {n: s.sb(f"r_{n}", [P, D]) for n in ("b2", "g_norm_out", "b_norm_out")}
        mask8 = s.sb("mask8", [P, TOK], U8)
        value_T = s.sb("value_T", [P, KD, TOK])
        film = s.sb("film", [P, 2, 2, TOK])
        xin = s.sb("xin", [P, KD, TOK])
        conv = s.sb("conv", [P, KD, TOK])
        hidden = s.sb("hidden", [P, FC, TOK])
        xt = s.sb("xt", [P, NT, D])
        norm = Norm(s)
        ring = [s.ps(f"ring{i}", [P, TOK]) for i in range(4)]
        y = [s.ps(f"y{i}", [P, D]) for i in range(NT)]
        v_in, w_in, down_in = s.sem("v_in"), s.sem("w_in"), s.sem("down_in")
        own_dve = s.sem("own_dve")
        masked, gates_ready = s.sem("masked"), s.sem("gates_ready")
        ring_full, ring_out = s.sem("ring_full"), s.sem("ring_out")
        film_used, turned_full, turned_out = s.sem("film_used"), s.sem("turned_full"), s.sem("turned_out")
        conv_done, y_full, normed_T = s.sem("conv_done"), s.sem("y_full"), s.sem("normed_T")
        block = s.block()
        R_IN = KD
        R_OUT = R_IN + 2 * KD
        R_WIDE = R_OUT + 2 * KD
        V_IN = 16 * (len(vecs) + len(long) + 1)

        @block.sync
        def _(sp):
            sp.dma_start(w_v[:], d["L1_xattn_Wv"]).then_inc(w_in, 16)
            sp.dma_start(w_in_film[:], d["L1_xattn_W_film_in"]).then_inc(w_in, 16)
            sp.dma_start(w_out_film[:], d["L1_xattn_W_film_out"]).then_inc(w_in, 16)
            sp.dma_start(w_wide[:], d["L1_xattn_W1"]).then_inc(w_in, 16)
            for q in range(4):
                if q:
                    sp.wait_ge(y_full, q)
                sp.dma_start(w_down[:], d["L1_xattn_W2"][:, q * KD:(q + 1) * KD, :]).then_inc(down_in, 16)

        @block.gpsimd
        def _(pool):
            for n, t in vecs.items():
                src = rows(d[f"L1_xattn_{n}"]) if n == "mod_gate" else d[f"L1_xattn_{n}"]
                pool.dma_start(t[:], src).then_inc(v_in, 16)
            for n, t in long.items():
                pool.dma_start(t[:], rows(d[f"L1_xattn_{n}"])).then_inc(v_in, 16)
            pool.dma_start(mask8[:], rows(d["mask_text"])).then_inc(v_in, 16)

        @block.vector
        def _(dve):
            own = Steps(dve, own_dve)
            dve.wait_ge(v_in, V_IN)
            for k in range(KC):
                dve.tensor_tensor(c_T[:, k, :], c_T[:, k, :], mask8[:], ALU.mult).then_inc(masked, 1)
            for n in ("b_film_in", "b_film_out"):
                t = vecs[n]
                own.did(dve.tensor_scalar(t[:], t[:], vecs["mod_gate"][:, 0:1], None, ALU.mult))
                own.wait()
                dve.tensor_scalar(t[:, 0:KD], t[:, 0:KD], 1.0, None, ALU.add).then_inc(gates_ready, 1)
            norm.on_vector(dve, g.hn, xt)
            for t in range(NT):
                dve.wait_ge(turned_full, t + 1)
                for k in range(KD):
                    last = dve.tensor_scalar(xin[:, k, t * P:(t + 1) * P], y[t][:, k * P:(k + 1) * P],
                                             vecs["g_norm_in"][:, k:k + 1], vecs["b_norm_in"][:, k:k + 1],
                                             ALU.mult, ALU.add)
                last.then_inc(turned_out, 1)
            dve.wait_ge(turned_out, NT)

            def modulate(t, n):
                dve.wait_ge(ring_out, R_IN + 2 * n + 2)
                own.did(dve.tensor_tensor(t, t, film[:, n % 2, 0, :], ALU.mult))
                own.wait()
                dve.tensor_tensor(t, t, film[:, n % 2, 1, :], ALU.add).then_inc(film_used, 1)
                dve.wait_ge(film_used, n + 1)

            for k in range(KD):
                modulate(xin[:, k, :], k)
            for k in range(KD):
                out = conv[:, k, :].rearrange("p (b s) -> p b s", b=NB)
                src = xin[:, k, :].rearrange("p (b s) -> p b s", b=NB)
                own.did(dve.tensor_scalar(conv[:, k, :], xin[:, k, :], g.kern[:, k, 0:1], None, ALU.mult))
                for l in range(1, SEQ):
                    own.wait()
                    own.did(dve.scalar_tensor_tensor(out=out[:, :, l:SEQ], in0=src[:, :, 0:SEQ - l],
                                                     scalar=g.kern[:, k, l:l + 1], in1=out[:, :, l:SEQ],
                                                     op0=ALU.mult, op1=ALU.add))
                own.wait()
                modulate(conv[:, k, :], KD + k)
                dve.tensor_tensor(conv[:, k, :], conv[:, k, :], g.hT[:, k, :], ALU.add).then_inc(conv_done, 1)
            for t in range(NT):
                dve.wait_ge(turned_full, NT + t + 1)
                own.did(dve.tensor_copy(xt[:, t, :], y[t][:]))
            own.wait()
            norm.on_vector(dve, xt, g.hn, 1)
            for t in range(NT):
                dve.wait_ge(turned_full, 2 * NT + t + 1)
                for k in range(KD):
                    last = dve.tensor_scalar(xin[:, k, t * P:(t + 1) * P], y[t][:, k * P:(k + 1) * P],
                                             vecs["g_ffn"][:, k:k + 1], vecs["b_ffn"][:, k:k + 1],
                                             ALU.mult, ALU.add)
                last.then_inc(normed_T, 1)
            for t in range(NT):
                own.did(dve.tensor_tensor(xt[:, t, :], xt[:, t, :], long["b2"][:], ALU.add))
            own.wait()
            dve.wait_ge(y_full, 4)
            for t in range(NT):
                own.did(dve.tensor_tensor(xt[:, t, :], xt[:, t, :], y[t][:], ALU.add))
            own.wait()
            norm.on_vector(dve, xt, g.hn, 2)
            for t in range(NT):
                own.did(dve.tensor_tensor(g.hn[:, t, :], g.hn[:, t, :], long["g_norm_out"][:], ALU.mult))
                own.did(dve.tensor_tensor(g.x[:, t, :], g.x[:, t, :], long["b_norm_out"][:], ALU.add))
            own.wait()
            for t in range(NT):
                own.did(dve.tensor_tensor(g.x[:, t, :], g.x[:, t, :], g.hn[:, t, :], ALU.add))

        @block.scalar
        def _(act):
            norm.on_scalar(act, g.eps[:])
            for m in range(KD):
                act.wait_ge(ring_full, m + 1)
                act.activation(value_T[:, m, :], ring[m % 4][:], ACT.Copy).then_inc(ring_out, 1)
            act.wait_ge(gates_ready, 2)
            for n in range(2 * KD):
                bias = vecs["b_film_in" if n < KD else "b_film_out"]
                if n >= 2:
                    act.wait_ge(film_used, n - 1)
                for j in range(2):
                    u = R_IN + 2 * n + j
                    act.wait_ge(ring_full, u + 1)
                    act.activation(film[:, n % 2, j, :], ring[u % 4][:], ACT.Identity,
                                   bias=bias[:, j * KD + n % KD:j * KD + n % KD + 1],
                                   scale=vecs["mod_gate"][:, 0:1]).then_inc(ring_out, 1)
            norm.on_scalar(act, g.eps[:], 1)
            for m in range(FC):
                u = R_WIDE + m
                act.wait_ge(ring_full, u + 1)
                act.activation(hidden[:, m, :], ring[u % 4][:], ACT.Gelu,
                               bias=vecs["b1"][:, m:m + 1]).then_inc(ring_out, 1)
            norm.on_scalar(act, g.eps[:], 2)

        @block.tensor
        def _(pe):
            pe.wait_ge(w_in, 64)
            pe.wait_ge(masked, KC)
            for m in range(KD):
                for k in range(KC):
                    last = pe.matmul(ring[m % 4][:], w_v[:, k, m * P:(m + 1) * P], c_T[:, k, :], start=(k == 0),
                                     stop=(k == KC - 1))
                last.then_inc(ring_full, 1)
            pe.wait_ge(norm.normed, NT)
            for t in range(NT):
                for k in range(KD):
                    last = pe.transpose(y[t][:, k * P:(k + 1) * P], xt[:, t, k * P:(k + 1) * P], g.ident[:])
                last.then_inc(turned_full, 1)
            pe.wait_ge(ring_out, KD)
            for n in range(2 * KD):
                w = w_in_film if n < KD else w_out_film
                for j in range(2):
                    u = R_IN + 2 * n + j
                    pe.wait_ge(ring_out, max(u - 3, KD))
                    m = j * KD + n % KD
                    for k in range(KD):
                        last = pe.matmul(ring[u % 4][:], w[:, k, m * P:(m + 1) * P], value_T[:, k, :],
                                         start=(k == 0), stop=(k == KD - 1))
                    last.then_inc(ring_full, 1)
            pe.wait_ge(conv_done, KD)
            for t in range(NT):
                for k in range(KD):
                    last = pe.transpose(y[t][:, k * P:(k + 1) * P], conv[:, k, t * P:(t + 1) * P], g.ident[:])
                last.then_inc(turned_full, 1)
            pe.wait_ge(norm.normed, 2 * NT)
            for t in range(NT):
                for k in range(KD):
                    last = pe.transpose(y[t][:, k * P:(k + 1) * P], g.hn[:, t, k * P:(k + 1) * P], g.ident[:])
                last.then_inc(turned_full, 1)
            pe.wait_ge(normed_T, NT)
            for m in range(FC):
                u = R_WIDE + m
                pe.wait_ge(ring_out, u - 3)
                for k in range(KD):
                    last = pe.matmul(ring[u % 4][:], w_wide[:, k, m * P:(m + 1) * P], xin[:, k, :],
                                     start=(k == 0), stop=(k == KD - 1))
                last.then_inc(ring_full, 1)
            for q in range(4):
                pe.wait_ge(down_in, 16 * (q + 1))
                pe.wait_ge(ring_out, R_WIDE + (q + 1) * KD)
                for t in range(NT):
                    for k in range(KD):
                        m = q * KD + k
                        last = pe.matmul(y[t][:], hidden[:, m, t * P:(t + 1) * P], w_down[:, k, :],
                                         start=(m == 0), stop=(m == FC - 1))
                last.then_inc(y_full, 1)


def state_space_alone(g):
    with Stage(g.nc, "y") as s:
        ss = StateSpace(s, g)
        block = s.block()

        @block.sync
        def _(sp):
            ss.on_sync(sp)

        @block.scalar
        def _(act):
            ss.on_scalar(act)

        @block.vector
        def _(dve):
            ss.on_vector(dve)

        @block.gpsimd
        def _(pool):
            ss.on_gpsimd(pool)


def write_out(g):
    nc = g.nc
    with Stage(nc, "z") as s:
        stored = s.sem("stored")
        block = s.block()

        @block.sync
        def _(sp):
            sp.dma_start(tokens(g.out), g.x[:]).then_inc(stored, 16)
            sp.wait_ge(stored, 16)


def load_x(g):
    nc = g.nc
    with Stage(nc, "i") as s:
        loaded, cleared, made = s.sem("loaded"), s.sem("cleared"), s.sem("made")
        block = s.block()

        @block.sync
        def _(sp):
            sp.dma_start(g.x[:], tokens(g.dram["x"])).then_inc(loaded, 16)
            sp.wait_ge(loaded, 16)

        @block.gpsimd
        def _(pool):
            pool.memset(g.eps[:], EPS).then_inc(cleared, 1)
            pool.wait_ge(cleared, 1)
            pool.memset(g.zero[:], 0.0).then_inc(cleared, 1)
            pool.wait_ge(cleared, 2)
            pool.memset(g.ident[:], 0.0).then_inc(cleared, 1)
            pool.wait_ge(cleared, 3)
            pool.affine_select(out=g.ident[:], in_=g.ident[:], compare_op=ALU.not_equal, fill=1.0, base=0,
                               pattern=[[-1, P]], channel_multiplier=1).then_inc(made, 1)
            pool.wait_ge(made, 1)


def build(nc, dram, out, stages=range(6)):
    with ExitStack() as ctx:
        g = Core(nc, ctx, dram, out, None)
        load_x(g)
        if 0 in stages:
            g.mixed_dram = nc.dram_tensor("mixed_context", [P, KC, 8, TOK], F32, kind="Internal").ap()
            with Stage(nc, "a") as s:
                q_T = s.sb("q_T", [P, 4, TOK])
                kl_T = s.sb("kl_T", [P, 4, TOK])
                latent_probs = s.sb("latent_probs", [SEQ, NB, D])
                xattn0_queries(g, q_T, kl_T)
                xattn0_context(g, q_T, kl_T, latent_probs)
                xattn0_output(g, latent_probs)
        if 1 in stages:
            causal_attention(g, "b", "L0_attn_qk", 4, False, "L0_attn_v", D, "L0_attn_out_w", "L0_attn_b",
                             1.0 / float(np.sqrt(32.0)))
        if 2 in stages:
            shared_and_routed_experts(g)
        if 3 in stages:
            if 2 not in stages:
                state_space_alone(g)
            with Stage(nc, "d") as s:
                c_T = s.sb("c_T", [P, KC, TOK])
                xattn1_context(g, c_T)
                film_and_mlp(g, c_T)
        if 4 in stages:
            causal_attention(g, "e", "L1_attn_qk", 1, True, "L1_attn_wv", 32, "L1_attn_wo", None,
                             1.0 / float(np.sqrt(32.0)))
        if 5 in stages:
            capacity_experts(g)
        write_out(g)


def lay(w):
    k, n = w.shape
    return np.ascontiguousarray(w.reshape(k // P, P, n).transpose(1, 0, 2))


def layout(inputs):
    a = {k: np.asarray(v) for k, v in inputs.items()}
    o = {}
    o["x"] = a["x"]
    o["ctx"] = a["ctx_768"]
    o["mask_ctx0"] = a["mask_BxS2_bk0"]
    o["L0_xattn_Wq"] = lay(a["L0_xattn_Wq"].T)
    o["L0_xattn_Wk"] = lay(a["L0_xattn_Wkv"][:D].T)
    o["L0_xattn_Wv"] = lay(a["L0_xattn_Wkv"][D:].T)
    o["L0_xattn_Wlk"] = lay(a["L0_xattn_Wlkv"][:D].T)
    o["L0_xattn_Wlv"] = lay(a["L0_xattn_Wlkv"][D:].T)
    o["L0_xattn_Wo"] = lay(a["L0_xattn_Wo"].T)
    for n in ("L0_xattn_ln_l_g", "L0_xattn_ln_l_b"):
        o[n] = np.ascontiguousarray(a[n].reshape(KD, P).T)
    for n in ("L0_xattn_qn_g", "L0_xattn_kn_g", "L0_xattn_ln_x_g", "L0_xattn_ln_x_b", "L0_xattn_bo"):
        o[n] = a[n]
    qkv = a["L0_attn_qkv_w"]
    o["L0_attn_qk"] = lay(qkv[:, :2 * D])
    o["L0_attn_v"] = lay(qkv[:, 2 * D:])
    o["L0_attn_out_w"] = lay(a["L0_attn_out_w"])
    o["L0_attn_b_qk"] = np.ascontiguousarray(a["L0_attn_qkv_b"][:2 * D].reshape(8, P).T)
    o["L0_attn_b_v"] = a["L0_attn_qkv_b"][2 * D:]
    o["L0_attn_b_o"] = a["L0_attn_out_b"]
    for n in ("Wg", "Wu", "Wd"):
        w = np.concatenate([a[f"L0_ffn_{n}_s"][None], a[f"L0_ffn_{n}"]])
        o[f"L0_ffn_{n}"] = np.stack([lay(m.T) for m in w])
    o["L0_ffn_Wr"] = lay(a["L0_ffn_Wr"].T)
    o["L0_ffn_rb"] = a["L0_ffn_rb"]
    o["mask_ctx1"] = a["mask_BxS2_bf1"]
    o["mask_text"] = a["mask_BxS_bf1"].reshape(-1)
    for n in ("Wq", "Wk", "Wv", "W_film_in", "W_film_out", "W1", "W2"):
        o[f"L1_xattn_{n}"] = lay(a[f"L1_xattn_{n}"])
    for n in ("g_norm_in", "b_norm_in", "g_ffn", "b_ffn", "b_film_in", "b_film_out", "b1", "log_dt", "D_skip"):
        o[f"L1_xattn_{n}"] = np.ascontiguousarray(a[f"L1_xattn_{n}"].reshape(-1, P).T)
    for n in ("A_re", "A_im", "C_re", "C_im"):
        o[f"L1_xattn_{n}"] = lay(a[f"L1_xattn_{n}"])
    for n in ("b2", "g_norm_out", "b_norm_out"):
        o[f"L1_xattn_{n}"] = a[f"L1_xattn_{n}"]
    o["L1_xattn_mod_gate"] = a["L1_xattn_mod_gate"].reshape(1)
    o["L1_ffn_Wr"] = lay(a["L1_ffn_Wr"])
    o["L1_ffn_W1"] = np.stack([lay(m) for m in a["L1_ffn_W1"]])
    o["L1_ffn_W2"] = np.stack([lay(m) for m in a["L1_ffn_W2"]])
    o["slots"] = np.arange(160, dtype=np.float32)
    o["before"] = (np.arange(E_N)[None, :] < np.arange(E_N)[:, None]).astype(np.float32).reshape(-1)
    even_odd = np.concatenate([np.arange(0, 32, 2), np.arange(1, 32, 2)])
    odd_even = np.concatenate([np.arange(1, 32, 2), np.arange(0, 32, 2)])
    wq, wk = a["L1_attn_wq"].T.reshape(D, 16, 32), a["L1_attn_wk"]
    cols = []
    for order in (even_odd, odd_even):
        cols += [wq[:, :, order].reshape(D, D)] + [wk[:, order]] * 4
    o["L1_attn_qk"] = lay(np.concatenate(cols, axis=1))
    o["L1_attn_wv"] = lay(a["L1_attn_wv"])
    o["L1_attn_wo"] = lay(a["L1_attn_wo"].T)
    freqs = (np.float32(1.0) / np.float32(1000.0) ** (np.arange(0, 32, 2, dtype=np.float32) / np.float32(32)))
    ang = np.arange(SEQ, dtype=np.float32)[:, None] * freqs[None, :].astype(np.float32)
    cos, sin = np.cos(ang).T, np.sin(ang).T
    o["rope_cos"] = np.ascontiguousarray(np.tile(np.concatenate([cos, cos]), (4, NB)))
    o["rope_sin"] = np.ascontiguousarray(np.tile(np.concatenate([-sin, sin]), (4, NB)))
    return o


def kernel(**inputs):
    import concourse.bacc as bacc
    from concourse.bass_utils import run_bass_kernel_spmd

    nc = bacc.Bacc("TRN2", target_bir_lowering=False, num_devices=1)
    arrays = layout(inputs)
    dram = {n: nc.dram_tensor(f"in_{n}", v.shape, mybir.dt.from_np(v.dtype), kind="ExternalInput").ap()
            for n, v in arrays.items()}
    out = nc.dram_tensor("out", [NB, SEQ, D], F32, kind="ExternalOutput").ap()
    build(nc, dram, out)
    r = run_bass_kernel_spmd(nc, [{f"in_{n}": v for n, v in arrays.items()}], core_ids=[0])
    return r.results[0]["out"]
```

```python
from contextlib import ExitStack

import numpy as np

import concourse.bass as bass
from concourse import mybir

ALU = mybir.AluOpType
ACT = mybir.ActivationFunctionType
AXX = mybir.AxisListType.X
F32 = mybir.dt.float32
F32R = mybir.dt.float32r
BF16 = mybir.dt.bfloat16
U8 = mybir.dt.uint8

P = 128
NB, SEQ, D = 8, 64, 512
TOK = NB * SEQ
NT = TOK // P
KD = D // P
CTX, DC = 1601, 384
KC = DC // P
CFULL = CTX // P
CLAST = CTX - CFULL * P
CT = CFULL + 1
KEYS = CTX + SEQ
EPS = 1e-5
MASKED = -1e30
FIRST = 1


class Steps:

    def __init__(self, eng, sem, base=0):
        self.eng, self.sem, self.n, self.base = eng, sem, 0, base

    def did(self, ins):
        ins.then_inc(self.sem, 1)
        self.n += 1

    def wait(self):
        self.eng.wait_ge(self.sem, self.base + self.n)


def chunked(ap, k):
    return ap.rearrange("p (k n) -> p k n", k=k)


def rows(vec, n=None):
    return vec.partition_broadcast(P)


class Core:

    def __init__(self, nc, ctx, dram, out, debug):
        self.nc, self.dram, self.out, self.debug = nc, dram, out, debug
        self.ident = ctx.enter_context(nc.sbuf_tensor("ident", [P, P], F32))
        self.eps = ctx.enter_context(nc.sbuf_tensor("eps", [P, 1], F32))
        self.zero = ctx.enter_context(nc.sbuf_tensor("zero", [P, 1, 1], F32))
        self.kern = ctx.enter_context(nc.sbuf_tensor("kern", [P, KD, SEQ], F32))
        self.x = ctx.enter_context(nc.sbuf_tensor("x", [P, NT, D], F32))
        self.hT = ctx.enter_context(nc.sbuf_tensor("hT", [P, KD, TOK], F32))
        self.hn = ctx.enter_context(nc.sbuf_tensor("hn", [P, NT, D], F32))


def tokens(dram3):
    return dram3.rearrange("b s d -> (b s) d").rearrange("(t p) d -> p t d", p=P)


class Stage:

    def __init__(self, nc, name):
        self.nc, self.name, self.ctx, self.sems = nc, name, ExitStack(), []

    def __enter__(self):
        self.ctx.__enter__()
        return self

    def __exit__(self, *a):
        self.ctx.__exit__(*a)
        if self.sems and a[0] is None:
            self.nc.clear_and_free_semaphores(self.sems)
            self.nc.all_engine_barrier()

    def sb(self, name, shape, dt=F32):
        return self.ctx.enter_context(self.nc.sbuf_tensor(f"{self.name}_{name}", shape, dt))

    def ps(self, name, shape, dt=F32):
        return self.ctx.enter_context(self.nc.psum_tensor(f"{self.name}_{name}", shape, dt))

    def sem(self, name):
        self.sems.append(self.nc.alloc_semaphore(f"{self.name}_{name}"))
        return self.sems[-1]

    def block(self):
        return self.ctx.enter_context(self.nc.Block())


def product(pe, out, left, right, k, last_k):
    pe.matmul(out, left[0], right[0], start=(k == 0), stop=False)
    pe.matmul(out, left[0], right[1], start=False, stop=False)
    return pe.matmul(out, left[1], right[0], start=False, stop=(k == last_k))


def restart(eng, sem):
    eng.nop(nofuse=True)
    eng.sem_clear(sem)


class Norm:

    def __init__(self, s, n=NT, name="norm"):
        self.n = n
        self.stats = s.sb(f"{name}_stats", [P, n, 6])
        self.mv = s.sb(f"{name}_mv", [P, n, 2])
        self.rstd = s.sb(f"{name}_rstd", [P, n])
        self.measured, self.rooted = s.sem(f"{name}_measured"), s.sem(f"{name}_rooted")
        self.normed = s.sem(f"{name}_normed")
        self.own, self.inverted = s.sem(f"{name}_own"), s.sem(f"{name}_inverted")

    def on_vector(self, dve, src, dst, turn=0):
        n = self.n
        for t in range(n):
            dve.bn_stats(self.stats[:, t, :], src[:, t, :]).then_inc(self.own, 1)
        dve.wait_ge(self.own, n * (turn + 1))
        for t in range(n):
            dve.bn_aggr(self.mv[:, t, :], self.stats[:, t, :]).then_inc(self.measured, 1)
        dve.wait_ge(self.rooted, turn + 1)
        dve.reciprocal(self.rstd[:], self.rstd[:]).then_inc(self.inverted, 1)
        dve.wait_ge(self.inverted, turn + 1)
        for t in range(n):
            dve.tensor_scalar(dst[:, t, :], src[:, t, :], self.mv[:, t, 0:1], self.rstd[:, t:t + 1],
                              ALU.subtract, ALU.mult).then_inc(self.normed, 1)
        dve.wait_ge(self.normed, n * (turn + 1))

    def on_scalar(self, act, eps, turn=0):
        act.wait_ge(self.measured, self.n * (turn + 1))
        act.activation(self.rstd[:], self.mv[:, :, 1], ACT.Sqrt, bias=eps).then_inc(self.rooted, 1)


def scale_by_length(dve, own, out, heads, length):
    own.did(dve.reciprocal(length, length))
    own.wait()
    m, n = length.shape
    return dve.scalar_tensor_tensor(out=out, in0=length.unsqueeze(2).to_broadcast([m, n, 64]), scalar=1 / 8e-8,
                                    in1=heads, op0=ALU.min, op1=ALU.mult)


def transpose_tokens(pe, turned_psum, src, ident, ready, filled, drained=None, n=NT):
    pe.wait_ge(*ready)
    for t in range(n):
        if drained is not None and t >= 2:
            pe.wait_ge(drained, t - 1)
        for k in range(KD):
            last = pe.transpose(turned_psum[t % 2][:, k, :], src[:, t, k * P:(k + 1) * P], ident)
        last.then_inc(filled, 1)


def xattn0_queries(g, q_T, kl_T):
    nc, d = g.nc, g.dram
    with Stage(nc, "a1") as s:
        wq = s.sb("wq", [P, KD, D])
        wk = s.sb("wk", [P, KD, D])
        gain = s.sb("gain", [P, KD])
        bias = s.sb("bias", [P, KD])
        qg = s.sb("qg", [P, SEQ])
        kg = s.sb("kg", [P, SEQ])
        qk = s.sb("qk", [P, SEQ])
        norm = Norm(s)
        sq = s.sb("sq", [P, 2, D])
        ss = s.sb("ss", [P, 2, 8])
        length = s.sb("length", [P, 2, 8])
        heads = s.sb("heads", [P, 2, D])
        turned = [s.ps(f"turned{i}", [P, KD, P]) for i in range(2)]
        proj = [s.ps(f"proj{i}", [P, D]) for i in range(2)]
        back = [s.ps(f"back{i}", [P, KD, P]) for i in range(2)]
        w_in = s.sem("w_in")
        dve_own, gains_made = s.sem("dve_own"), s.sem("gains_made")
        summed, rooted = s.sem("summed"), s.sem("rooted")
        turned_full, turned_out = s.sem("turned_full"), s.sem("turned_out")
        proj_full, squared, heads_made = s.sem("proj_full"), s.sem("squared"), s.sem("heads_made")
        back_full, back_out = s.sem("back_full"), s.sem("back_out")
        block = s.block()

        @block.sync
        def _(sp):
            for ap, name in ((wq, "L0_xattn_Wq"), (wk, "L0_xattn_Wlk")):
                sp.dma_start(ap[:], d[name]).then_inc(w_in, 16)
            sp.dma_start(gain[:], d["L0_xattn_ln_l_g"]).then_inc(w_in, 16)
            sp.dma_start(bias[:], d["L0_xattn_ln_l_b"]).then_inc(w_in, 16)
            sp.dma_start(qg[:], rows(d["L0_xattn_qn_g"])).then_inc(w_in, 16)
            sp.dma_start(kg[:], rows(d["L0_xattn_kn_g"])).then_inc(w_in, 16)

        @block.vector
        def _(dve):
            own = Steps(dve, dve_own)
            norm.on_vector(dve, g.x, g.hn)
            norm.on_vector(dve, g.hn, g.hn, 1)
            dve.wait_ge(w_in, 96)
            dve.scalar_tensor_tensor(out=qk[:], in0=qg[:], scalar=8.0, in1=kg[:], op0=ALU.mult,
                                     op1=ALU.mult).then_inc(gains_made, 1)
            dve.wait_ge(gains_made, 1)
            for t in range(NT):
                dve.wait_ge(turned_full, t + 1)
                for k in range(KD):
                    last = dve.tensor_scalar(g.hT[:, k, t * P:(t + 1) * P], turned[t % 2][:, k, :],
                                             gain[:, k:k + 1], bias[:, k:k + 1], ALU.mult, ALU.add)
                last.then_inc(turned_out, 1)
            for n in range(2 * NT):
                dve.wait_ge(squared, n + 1)
                if n >= 2:
                    dve.wait_ge(back_full, n - 1)
                dve.tensor_reduce(ss[:, n % 2, :], sq[:, n % 2, :].rearrange("p (h c) -> p h c", h=8),
                                  AXX, ALU.add).then_inc(summed, 1)
                dve.wait_ge(rooted, n + 1)
                h = heads[:, n % 2, :].rearrange("p (h c) -> p h c", h=8)
                ins = scale_by_length(dve, own, h, proj[n % 2][:].rearrange("p (h c) -> p h c", h=8),
                                      length[:, n % 2, :])
                if n < NT:
                    own.did(ins)
                    own.wait()
                    ins = dve.tensor_tensor(h, h, qk[:].unsqueeze(1).to_broadcast([P, 8, 64]), ALU.mult)
                ins.then_inc(heads_made, 1)

        def put_back(act, n):
            act.wait_ge(back_full, n + 1)
            dst = q_T if n < NT else kl_T
            t = n % NT
            act.activation(dst[:, :, t * P:(t + 1) * P], back[n % 2][:], ACT.Copy).then_inc(back_out, 1)

        @block.scalar
        def _(act):
            norm.on_scalar(act, g.eps[:])
            norm.on_scalar(act, g.eps[:], 1)
            for n in range(2 * NT):
                act.wait_ge(proj_full, n + 1)
                if n >= 2:
                    act.wait_ge(heads_made, n - 1)
                act.activation(sq[:, n % 2, :], proj[n % 2][:], ACT.Square).then_inc(squared, 1)
                act.wait_ge(summed, n + 1)
                act.activation(length[:, n % 2, :], ss[:, n % 2, :], ACT.Sqrt).then_inc(rooted, 1)
                if n >= 1:
                    put_back(act, n - 1)
            put_back(act, 2 * NT - 1)

        @block.tensor
        def _(pe):
            transpose_tokens(pe, turned, g.hn, g.ident[:], (norm.normed, 2 * NT), turned_full, turned_out)
            pe.wait_ge(turned_out, NT)
            for n in range(2 * NT + 1):
                if n < 2 * NT:
                    w, t = (wq, n) if n < NT else (wk, n - NT)
                    if n >= 2:
                        pe.wait_ge(heads_made, n - 1)
                    for k in range(KD):
                        last = pe.matmul(proj[n % 2][:], g.hT[:, k, t * P:(t + 1) * P], w[:, k, :],
                                         start=(k == 0), stop=(k == KD - 1))
                    last.then_inc(proj_full, 1)
                if n >= 1:
                    m = n - 1
                    pe.wait_ge(heads_made, m + 1)
                    if m >= 2:
                        pe.wait_ge(back_out, m - 1)
                    for k in range(KD):
                        last = pe.transpose(back[m % 2][:, k, :], heads[:, m % 2, k * P:(k + 1) * P], g.ident[:])
                    last.then_inc(back_full, 1)


def xattn0_context(g, q_T, kl_T, latent_probs):
    nc, d = g.nc, g.dram
    PAIRS = 4
    PER_RING = CT * 2 + PAIRS * 4
    PER_KS = CT + PAIRS * 4
    GROUPS = [(0, 4), (4, 8), (8, 12), (12, 13)]
    CHUNKS = [(0, 512), (512, 1024), (1024, 1536), (1536, KEYS)]

    def size(t):
        return P if t < CFULL else CLAST

    with Stage(nc, "a2") as s:
        xn = s.sb("xn", [P, 2, CT, DC])
        gain = s.sb("gain", [P, DC])
        bias = s.sb("bias", [P, DC])
        mask8 = s.sb("mask8", [P, 2, CTX], U8)
        mask = s.sb("mask", [P, KEYS], BF16)
        stats = s.sb("stats", [P, CT, 6])
        mv = s.sb("mv", [P, CT, 2])
        rstd = s.sb("rstd", [P, CT])
        xn_T = s.sb("xn_T", [P, 2, KC, P])
        xn_high = s.sb("xn_high", [P, 2, KC, P], F32R)
        xn_low = s.sb("xn_low", [P, 2, KC, P], F32R)
        wk_high = s.sb("wk_high", [P, KC, D], F32R)
        wk_low = s.sb("wk_low", [P, KC, D], F32R)
        ss = s.sb("ss", [P, 2, 8])
        length = s.sb("length", [P, 2, 8])
        keys = s.sb("keys", [P, 2, D])
        k_T = s.sb("k_T", [P, PAIRS, KEYS])
        q_diag = s.sb("q_diag", [P, PAIRS, P])
        probs = s.sb("probs", [P, 2, KEYS])
        top4 = s.sb("top4", [P, 2, 4])
        neg_top = s.sb("neg_top", [P, 2])
        total = s.sb("total", [P, 2])
        inv = s.sb("inv", [P, 2])
        probs_T = s.sb("probs_T", [P, CT, D])
        mixed = s.sb("mixed", [P, KC, D])
        wk = mixed
        ring = [s.ps(f"ring{i}", [P, 4, P]) for i in range(3)]
        ks = [s.ps(f"ks{i}", [P, D]) for i in range(2)]
        mix = [s.ps(f"mix{i}", [P, D]) for i in range(KC)]

        w_in = s.sem("w_in")
        ctx_in = [s.sem(f"ctx_in{i}") for i in range(2)]
        dve_own = s.sem("dve_own")
        pool_own = s.sem("pool_own")
        scaled = s.sem("scaled")
        context_ready = s.sem("context_ready")
        ring_full, ring_out = s.sem("ring_full"), s.sem("ring_out")
        ks_full, ks_out = s.sem("ks_full"), s.sem("ks_out")
        measured, rooted = s.sem("measured"), s.sem("rooted")
        squared, summed, lengths = s.sem("squared"), s.sem("summed"), s.sem("lengths")
        side_ready = s.sem("side_ready")
        wk_high_ready, wk_split = s.sem("wk_high_ready"), s.sem("wk_split")
        high_ready, low_ready = s.sem("high_ready"), s.sem("low_ready")
        row_top, exped, probs_ready = s.sem("row_top"), s.sem("exped"), s.sem("probs_ready")
        mix_full, mix_out, mix_stored = s.sem("mix_full"), s.sem("mix_out"), s.sem("mix_stored")
        block = s.block()

        def turn(t, what):
            n = 0
            for step in range(CT + 2):
                if step < CT:
                    if (step, 0) == (t, what):
                        return n
                    n += 1
                if step >= 2:
                    if (step - 2, 1) == (t, what):
                        return n
                    n += 1

        CTX_DMAS = 5

        def load(sp, b, par):
            src = d["ctx"][bass.ds(b, 1)].rearrange("a s d -> (a s) d")
            for lo, hi in GROUPS[:3]:
                sp.dma_start(xn[:, par, lo:hi, :],
                             src[lo * P:hi * P, :].rearrange("(t p) d -> p t d", p=P)).then_inc(ctx_in[par], 16)
            sp.dma_start(xn[0:CLAST, par, CFULL, :], src[CFULL * P:CTX, :]).then_inc(ctx_in[par], 16)
            sp.dma_start(mask8[:, par, :], d["mask_ctx0"][bass.ds(b, 1), :].rearrange("a s -> (a s)")
                         .partition_broadcast(P)).then_inc(ctx_in[par], 16)

        def store(sp, b):
            sp.wait_ge(mix_out, KC * b + KC + FIRST)
            for f in range(KC):
                sp.dma_start(g.mixed_dram[:, f, :, bass.ds(b * SEQ, SEQ)],
                             mixed[:, f, :].rearrange("p (h q) -> p h q", h=8)).then_inc(mix_stored, 16)

        @block.sync
        def _(sp):
            for signal in (mix_stored,):
                sp.sem_inc(signal, FIRST)
            sp.dma_start(wk[:], d["L0_xattn_Wk"]).then_inc(w_in, 16)
            sp.dma_start(gain[:], rows(d["L0_xattn_ln_x_g"])).then_inc(w_in, 16)
            sp.dma_start(bias[:], rows(d["L0_xattn_ln_x_b"])).then_inc(w_in, 16)
            for par in range(2):
                load(sp, par, par)
            with sp.Fori(0, NB // 2 - 1) as i:
                for par in range(2):
                    b = i * 2 + par
                    store(sp, b)
                    sp.wait_ge(mix_full, KC * b + KC)
                    load(sp, b + 2, par)
            for par in range(2):
                store(sp, NB - 2 + par)
            sp.wait_ge(mix_stored, 16 * KC * NB + FIRST)

        @block.gpsimd
        def _(pool):
            for signal in (side_ready,):
                pool.sem_inc(signal, FIRST)
            pool.memset(mask[:, CTX:KEYS], 0.0).then_inc(pool_own, 1)
            pool.wait_ge(pool_own, 1)
            pool.memset(q_diag[:], 0.0).then_inc(pool_own, 1)
            pool.wait_ge(pool_own, 2)
            pool.wait_ge(w_in, 48)
            PER = len(GROUPS)
            with pool.Fori(0, NB // 2) as i:
                for par in range(2):
                    b = i * 2 + par
                    for n, (lo, hi) in enumerate(GROUPS):
                        m = size(hi - 1)
                        if n == 0:
                            pool.wait_ge(side_ready, b * 4 + FIRST)
                        else:
                            pool.wait_ge(context_ready, b * PER + n)
                        pool.wait_ge(scaled, b * PER + (n + 1))
                        part = xn[0:m, par, lo:hi, :]
                        pool.tensor_tensor(part, part, gain[0:m].unsqueeze(1).to_broadcast([m, hi - lo, DC]),
                                           ALU.mult).then_inc(pool_own, 1)
                        pool.wait_ge(pool_own, b * PER + (n + 3))
                        pool.tensor_tensor(part, part, bias[0:m].unsqueeze(1).to_broadcast([m, hi - lo, DC]),
                                           ALU.add).then_inc(context_ready, 1)
                    pool.wait_ge(ks_out, b * PER_KS + 2)
                    pool.wait_ge(context_ready, b * PER + PER)
                    pool.nop(nofuse=True)
                    pool.tensor_scalar(mask[:, 0:CTX], mask8[:, par, :], -MASKED, MASKED, ALU.mult,
                                       ALU.add).then_inc(side_ready, 1)
                    for h in range(2):
                        pool.wait_ge(side_ready, b * 4 + (1 + h) + FIRST)
                        pool.tensor_copy(q_diag[h * 64:(h + 1) * 64, :, h * 64:(h + 1) * 64],
                                         q_T[h * 64:(h + 1) * 64, :, bass.ds(b * SEQ, SEQ)]).then_inc(side_ready, 1)
                    pool.wait_ge(side_ready, b * 4 + 3 + FIRST)
                    pool.tensor_copy(k_T[:, :, CTX:KEYS], kl_T[:, :, bass.ds(b * SEQ, SEQ)]).then_inc(side_ready, 1)

        @block.vector
        def _(dve):
            dve.sem_inc(ks_out, 2)
            dve.wait_ge(wk_high_ready, 1)
            dve.tensor_tensor(wk_low[:], wk[:], wk_high[:], ALU.subtract).then_inc(wk_split, 1)

            def split(own, b, par, t):
                m, i = size(t), (par * CT + t) % 2
                if t % 2 == 0:
                    dve.wait_ge(high_ready, b * (CT // 2 + 1) + (t // 2 + 1))
                else:
                    dve.wait_ge(ring_out, b * PER_RING + (turn(t, 0) + 1 + 3))
                    own.did(dve.tensor_copy(xn_high[:, i, :, 0:m], xn_T[:, i, :, 0:m]))
                    own.wait()
                dve.tensor_tensor(xn_low[:, i, :, 0:m], xn_T[:, i, :, 0:m], xn_high[:, i, :, 0:m],
                                  ALU.subtract).then_inc(low_ready, 1)

            def measure_group(own, par, n):
                lo, hi = GROUPS[n]
                m = size(hi - 1)
                for t in range(lo, hi):
                    own.did(dve.bn_stats(stats[0:m, t, :], xn[0:m, par, t, :]))
                own.wait()
                for t in range(lo, hi):
                    last = dve.bn_aggr(mv[0:m, t, :], stats[0:m, t, :])
                last.then_inc(measured, 1)

            def normalise_group(own, b, par, n):
                lo, hi = GROUPS[n]
                m = size(hi - 1)
                dve.wait_ge(rooted, b * len(GROUPS) + (n + 1))
                own.did(dve.reciprocal(rstd[0:m, lo:hi], rstd[0:m, lo:hi]))
                own.wait()
                for t in range(lo, hi):
                    last = dve.tensor_scalar(xn[0:m, par, t, :], xn[0:m, par, t, :], mv[0:m, t, 0:1],
                                             rstd[0:m, t:t + 1], ALU.subtract, ALU.mult)
                last.then_inc(scaled, 1)

            def sum_squares(b, par, t):
                m, i = size(t), (par * CT + t) % 2
                dve.wait_ge(squared, b * CT + (t + 1))
                dve.tensor_reduce(ss[0:m, i, :], keys[0:m, i, :].rearrange("p (h c) -> p h c", h=8),
                                  AXX, ALU.add).then_inc(summed, 1)

            def normalise_keys(own, b, par, t):
                m, i = size(t), (par * CT + t) % 2
                use = (par * PER_KS + t) % 2
                dve.wait_ge(ring_full, b * PER_RING + (turn(t - 2, 1) + 1 if t >= 2 else 0) + FIRST)
                dve.wait_ge(lengths, b * CT + (t + 1))
                scale_by_length(dve, own, keys[0:m, i, :].rearrange("p (h c) -> p h c", h=8),
                                ks[use][0:m, :].rearrange("p (h c) -> p h c", h=8),
                                length[0:m, i, :]).then_inc(ks_out, 1)

            def take_scores(own, b, par, pair, c):
                lo, hi = CHUNKS[c]
                n = CT + pair * 4 + c
                dve.wait_ge(ks_full, b * PER_KS + (n + 1) + FIRST)
                dve.nop(nofuse=True)
                dve.tensor_tensor_reduce(out=probs[:, pair % 2, lo:hi], in0=ks[(par * PER_KS + n) % 2][:, 0:hi - lo],
                                         in1=mask[:, lo:hi], scale=1.0, scalar=-3e38, op0=ALU.add, op1=ALU.max,
                                         accum_out=top4[:, pair % 2, c:c + 1]).then_inc(ks_out, 1)

            def scale_probs(own, b, pair):
                dve.wait_ge(exped, b * PAIRS + (pair + 1))
                own.did(dve.reciprocal(inv[:, pair % 2:pair % 2 + 1], total[:, pair % 2:pair % 2 + 1]))
                own.wait()
                dve.tensor_scalar(probs[:, pair % 2, :], probs[:, pair % 2, :], inv[:, pair % 2:pair % 2 + 1], None,
                                  ALU.mult).then_inc(probs_ready, 1)

            with dve.Fori(0, NB // 2) as i:
                for par in range(2):
                    b = i * 2 + par
                    restart(dve, dve_own)
                    own = Steps(dve, dve_own)
                    dve.wait_ge(ctx_in[par], (i + 1) * (16 * CTX_DMAS))
                    measure_group(own, par, 0)
                    for n in range(len(GROUPS)):
                        if n + 1 < len(GROUPS):
                            measure_group(own, par, n + 1)
                        normalise_group(own, b, par, n)
                    split(own, b, par, 0)
                    for t in range(CT):
                        if t + 1 < CT:
                            split(own, b, par, t + 1)
                        sum_squares(b, par, t)
                        normalise_keys(own, b, par, t)
                    dve.wait_ge(side_ready, b * 4 + 4 + FIRST)
                    for pair in range(PAIRS):
                        for c in range(4):
                            take_scores(own, b, par, pair, c)
                            if c == 2 and pair >= 1:
                                scale_probs(own, b, pair - 1)
                        dve.wait_ge(ks_out, b * PER_KS + (CT + pair * 4 + 4 + 2))
                        dve.tensor_reduce(neg_top[:, pair % 2:pair % 2 + 1], top4[:, pair % 2, :], AXX, ALU.max,
                                          negate=True).then_inc(row_top, 1)
                    scale_probs(own, b, PAIRS - 1)
                    own.wait()

        @block.scalar
        def _(act):
            for signal in (mix_out,):
                act.sem_inc(signal, FIRST)
            act.sem_inc(ring_out, 3)
            act.wait_ge(w_in, 48)
            act.activation(wk_high[:], wk[:], ACT.Copy).then_inc(wk_high_ready, 1)

            def put_context(b, par, t):
                m, n = size(t), turn(t, 0)
                act.wait_ge(ring_full, b * PER_RING + (n + 1) + FIRST)
                if t < 2:
                    act.wait_ge(ks_full, b * PER_KS + FIRST)
                else:
                    act.wait_ge(ks_full, b * PER_KS + (t - 1) + FIRST)
                act.activation(xn_T[:, (par * CT + t) % 2, :, 0:m], ring[(par * PER_RING + n) % 3][:, 0:KC, 0:m],
                               ACT.Copy).then_inc(ring_out, 1)
                if t % 2 == 0:
                    act.wait_ge(ring_out, b * PER_RING + (n + 1 + 3))
                    act.activation(xn_high[:, (par * CT + t) % 2, :, 0:m], xn_T[:, (par * CT + t) % 2, :, 0:m],
                                   ACT.Copy).then_inc(high_ready, 1)

            def square_keys(b, par, t):
                m, i = size(t), (par * CT + t) % 2
                act.wait_ge(ks_full, b * PER_KS + (t + 1) + FIRST)
                if t < 2:
                    act.wait_ge(ks_out, b * PER_KS + 2)
                else:
                    act.wait_ge(ks_out, b * PER_KS + (t - 2 + 1 + 2))
                act.activation(keys[0:m, i, :], ks[(par * PER_KS + t) % 2][0:m, :], ACT.Square).then_inc(squared, 1)

            def root_group(b, n):
                lo, hi = GROUPS[n]
                m = size(hi - 1)
                act.wait_ge(measured, b * len(GROUPS) + (n + 1))
                act.activation(rstd[0:m, lo:hi], mv[0:m, lo:hi, 1], ACT.Sqrt, bias=g.eps[0:m]).then_inc(rooted, 1)

            def root_lengths(b, par, t):
                m, i = size(t), (par * CT + t) % 2
                act.wait_ge(summed, b * CT + (t + 1))
                act.activation(length[0:m, i, :], ss[0:m, i, :], ACT.Sqrt).then_inc(lengths, 1)

            def put_keys(b, par, t):
                m, n = size(t), turn(t, 1)
                act.wait_ge(ring_full, b * PER_RING + (n + 1) + FIRST)
                act.activation(k_T[:, :, t * P:t * P + m], ring[(par * PER_RING + n) % 3][:, :, 0:m],
                               ACT.Copy).then_inc(ring_out, 1)

            def exponentials(b, pair):
                act.wait_ge(row_top, b * PAIRS + (pair + 1))
                act.activation(probs[:, pair % 2, :], probs[:, pair % 2, :], ACT.Exp,
                               bias=neg_top[:, pair % 2:pair % 2 + 1],
                               accum_out=total[:, pair % 2:pair % 2 + 1]).then_inc(exped, 1)

            def put_probs(b, par, pair):
                for q in range(4):
                    n = 2 * CT + pair * 4 + q
                    bank = ring[(par * PER_RING + n) % 3]
                    act.wait_ge(ring_full, b * PER_RING + (n + 1) + FIRST)
                    cols = slice(pair * P, (pair + 1) * P)
                    if q < 3:
                        act.activation(probs_T[:, 4 * q:4 * q + 4, cols], bank[:], ACT.Copy).then_inc(ring_out, 1)
                    else:
                        act.activation(probs_T[0:CLAST, CFULL, cols], bank[0:CLAST, 0, :], ACT.Copy)
                        act.activation(latent_probs[:, bass.ds(b, 1), cols], bank[0:SEQ, 1, :].unsqueeze(1),
                                       ACT.Copy).then_inc(ring_out, 1)

            def put_mixed(b):
                act.wait_ge(mix_stored, b * (16 * KC) + FIRST)
                for f in range(KC):
                    act.wait_ge(mix_full, b * KC + (f + 1))
                    act.activation(mixed[:, f, :], mix[f][:], ACT.Copy).then_inc(mix_out, 1)

            def batch(b, par):
                for n in range(len(GROUPS)):
                    root_group(b, n)
                if not (isinstance(b, int) and b == 0):
                    put_mixed(b - 1)
                for t in range(CT + 2):
                    if t < CT:
                        put_context(b, par, t)
                    if 1 <= t <= CT:
                        square_keys(b, par, t - 1)
                    if t >= 2:
                        put_keys(b, par, t - 2)
                    if 1 <= t <= CT:
                        root_lengths(b, par, t - 1)
                for pair in range(PAIRS):
                    exponentials(b, pair)
                    put_probs(b, par, pair)

            for par in range(2):
                batch(par, par)
            with act.Fori(1, NB // 2) as i:
                for par in range(2):
                    batch(i * 2 + par, par)
            put_mixed(NB - 1)

        @block.tensor
        def _(pe):
            for signal in (ring_full, ks_full,):
                pe.sem_inc(signal, FIRST)
            pe.wait_ge(wk_split, 1)

            def turn_context(b, par, t):
                m, n = size(t), turn(t, 0)
                if t % 4 == 0:
                    pe.wait_ge(context_ready, b * len(GROUPS) + (t // 4 + 1))
                pe.wait_ge(ring_out, b * PER_RING + (n + 1))
                for k in range(KC):
                    last = pe.transpose(ring[(par * PER_RING + n) % 3][:, k, 0:m], xn[0:m, par, t, k * P:(k + 1) * P],
                                        g.ident[0:m, 0:m])
                last.then_inc(ring_full, 1)

            def project(b, par, t):
                i = (par * CT + t) % 2
                pe.wait_ge(low_ready, b * CT + (t + 1))
                pe.wait_ge(ks_out, b * PER_KS + (t + 1))
                for k in range(KC):
                    last = product(pe, ks[(par * PER_KS + t) % 2][:], (xn_high[:, i, k, :], xn_low[:, i, k, :]),
                                   (wk_high[:, k, :], wk_low[:, k, :]), k, KC - 1)
                last.then_inc(ks_full, 1)

            def turn_keys(b, par, t):
                m, n = size(t), turn(t, 1)
                pe.wait_ge(ks_out, b * PER_KS + (t + 1 + 2))
                pe.wait_ge(ring_out, b * PER_RING + (n + 1))
                for k in range(4):
                    last = pe.transpose(ring[(par * PER_RING + n) % 3][:, k, 0:m],
                                        keys[0:m, (par * CT + t) % 2, k * P:(k + 1) * P], g.ident[0:m, 0:m])
                last.then_inc(ring_full, 1)

            def scores(b, par, pair):
                for c, (lo, hi) in enumerate(CHUNKS):
                    n = CT + pair * 4 + c
                    pe.wait_ge(ks_out, b * PER_KS + (n + 1))
                    pe.matmul(ks[(par * PER_KS + n) % 2][:, 0:hi - lo], q_diag[:, pair, :], k_T[:, pair, lo:hi],
                              start=True, stop=True).then_inc(ks_full, 1)

            def turn_probs(b, par, pair):
                pe.wait_ge(probs_ready, b * PAIRS + (pair + 1))
                for q in range(4):
                    n = 2 * CT + pair * 4 + q
                    bank = ring[(par * PER_RING + n) % 3]
                    pe.wait_ge(ring_out, b * PER_RING + (n + 1))
                    if q < 3:
                        for j in range(4):
                            t = 4 * q + j
                            last = pe.transpose(bank[:, j, :], probs[:, pair % 2, t * P:(t + 1) * P], g.ident[:])
                    else:
                        pe.transpose(bank[0:CLAST, 0, :], probs[:, pair % 2, CFULL * P:CTX], g.ident[:])
                        last = pe.transpose(bank[0:SEQ, 1, :], probs[:, pair % 2, CTX:KEYS], g.ident[:])
                    last.then_inc(ring_full, 1)

            with pe.Fori(0, NB // 2) as i:
                for par in range(2):
                    b = i * 2 + par
                    for t in range(CT + 2):
                        if t < CT:
                            turn_context(b, par, t)
                        if 1 <= t <= CT:
                            project(b, par, t - 1)
                        if t >= 2:
                            turn_keys(b, par, t - 2)
                    pe.wait_ge(ring_out, b * PER_RING + (2 * CT + 3))
                    pe.wait_ge(side_ready, b * 4 + 4 + FIRST)
                    scores(b, par, 0)
                    for pair in range(PAIRS):
                        if pair + 1 < PAIRS:
                            scores(b, par, pair + 1)
                        turn_probs(b, par, pair)
                    pe.wait_ge(ring_out, b * PER_RING + (PER_RING + 3))
                    for f in range(KC):
                        pe.wait_ge(mix_out, b * KC + FIRST)
                        for t in range(CT):
                            m = size(t)
                            last = pe.matmul(mix[f][:], xn[0:m, par, t, f * P:(f + 1) * P], probs_T[0:m, t, :],
                                             start=(t == 0), stop=(t == CT - 1))
                        last.then_inc(mix_full, 1)


def xattn0_output(g, latent_probs):
    nc, d = g.nc, g.dram
    with Stage(nc, "a3") as s:
        mixed = s.sb("mixed", [P, KC, 8, TOK])
        wv = s.sb("wv", [P, KC, D])
        wlv = s.sb("wlv", [P, KD, D])
        wo = s.sb("wo", [P, KD, D])
        bo = s.sb("bo", [P, D])
        lat_v = s.sb("lat_v", [SEQ, NB, D])
        o_T = s.sb("o_T", [P, 4, TOK])
        proj = [s.ps(f"proj{i}", [P, D]) for i in range(2)]
        heads = [s.ps(f"heads{i}", [P, TOK]) for i in range(2)]
        w_in, mixed_in = s.sem("w_in"), s.sem("mixed_in")
        v_full, v_out = s.sem("v_full"), s.sem("v_out")
        heads_full, heads_out = s.sem("heads_full"), s.sem("heads_out")
        y_full, biased, y_out = s.sem("y_full"), s.sem("biased"), s.sem("y_out")
        block = s.block()

        @block.sync
        def _(sp):
            sp.dma_start(wlv[:], d["L0_xattn_Wlv"]).then_inc(w_in, 16)
            sp.dma_start(wv[:], d["L0_xattn_Wv"]).then_inc(w_in, 16)
            sp.dma_start(wo[:], d["L0_xattn_Wo"]).then_inc(w_in, 16)
            sp.dma_start(bo[:], rows(d["L0_xattn_bo"])).then_inc(w_in, 16)
            sp.dma_start(mixed[:], g.mixed_dram).then_inc(mixed_in, 16)

        @block.gpsimd
        def _(pool):
            pool.wait_ge(w_in, 64)
            pool.tensor_tensor(g.x[:], g.x[:], bo[:].unsqueeze(1).to_broadcast([P, NT, D]),
                               ALU.add).then_inc(biased, 1)

        @block.tensor
        def _(pe):
            pe.wait_ge(w_in, 64)
            for b in range(NB):
                if b >= 2:
                    pe.wait_ge(v_out, b - 1)
                for k in range(KD):
                    last = pe.matmul(proj[b % 2][0:SEQ, :], g.hT[:, k, b * SEQ:(b + 1) * SEQ], wlv[:, k, :],
                                     start=(k == 0), stop=(k == KD - 1))
                last.then_inc(v_full, 1)
            pe.wait_ge(mixed_in, 16)
            pe.wait_ge(v_out, NB)
            for pair in range(4):
                if pair >= 2:
                    pe.wait_ge(heads_out, pair - 1)
                for half in range(2):
                    h = pair * 2 + half
                    out = heads[pair % 2][half * 64:(half + 1) * 64, :]
                    for k in range(KC):
                        pe.matmul(out, wv[:, k, h * 64:(h + 1) * 64], mixed[:, k, h, :], start=(k == 0), stop=False,
                                  skip_group_check=True)
                    for b in range(NB):
                        last = pe.matmul(out[:, b * SEQ:(b + 1) * SEQ], lat_v[:, b, h * 64:(h + 1) * 64],
                                         latent_probs[:, b, h * SEQ:(h + 1) * SEQ], start=False,
                                         stop=(b == NB - 1), skip_group_check=True)
                last.then_inc(heads_full, 1)
            pe.wait_ge(heads_out, 4)
            for t in range(NT):
                if t >= 2:
                    pe.wait_ge(y_out, t - 1)
                for k in range(KD):
                    last = pe.matmul(proj[t % 2][:], o_T[:, k, t * P:(t + 1) * P], wo[:, k, :],
                                     start=(k == 0), stop=(k == KD - 1))
                last.then_inc(y_full, 1)

        @block.scalar
        def _(act):
            for b in range(NB):
                act.wait_ge(v_full, b + 1)
                act.activation(lat_v[:, b, :], proj[b % 2][0:SEQ, :], ACT.Copy).then_inc(v_out, 1)
            for pair in range(4):
                act.wait_ge(heads_full, pair + 1)
                act.activation(o_T[:, pair, :], heads[pair % 2][:], ACT.Copy).then_inc(heads_out, 1)

        @block.vector
        def _(dve):
            dve.wait_ge(biased, 1)
            for t in range(NT):
                dve.wait_ge(y_full, t + 1)
                dve.tensor_tensor(g.x[:, t, :], proj[t % 2][:], g.x[:, t, :], ALU.add).then_inc(y_out, 1)


def causal_attention(g, name, w_dram, n_k, rope, v_dram, v_cols, wo_dram, bias_dram, scale):
    nc, d = g.nc, g.dram
    H, HD = 16, 32
    NQK = 4 + n_k
    NPROJ = NQK * (2 if rope else 1)
    with Stage(nc, name) as s:
        w = s.sb("w", [P, KD, NPROJ * P])
        wv = s.sb("wv", [P, KD, v_cols])
        wo = s.sb("wo", [P, KD, D])
        norm = Norm(s)
        causal = s.sb("causal", [P, P])
        qk_T = s.sb("qk_T", [P, NQK, TOK])
        v = s.sb("v", [P, NT, v_cols])
        scores = s.sb("scores", [P, 4, 4, P])
        top = s.sb("top", [P, H])
        total = s.sb("total", [P, H])
        probs_T = s.sb("probs_T", [P, H, P])
        o_T = s.sb("o_T", [P, 4, TOK])
        if rope:
            half = s.sb("half", [P, TOK])
            cos = s.sb("cos", [P, TOK])
            sin = s.sb("sin", [P, TOK])
        else:
            bias = s.sb("bias", [P, NQK])
            bias_v = s.sb("bias_v", [P, v_cols])
            bias_o = s.sb("bias_o", [P, D])
        bank = [s.ps(f"bank{i}", [P, 4, P]) for i in range(4)]
        ring = [s.ps(f"ring{i}", [P, 4, P]) for i in range(4)]
        w_in = s.sem("w_in")
        mask_made = s.sem("mask_made")
        ring_full, ring_out = s.sem("ring_full"), s.sem("ring_out")
        heads_ready = s.sem("heads_ready")
        v_ready = s.sem("v_ready")
        scores_full, masked, centred = s.sem("scores_full"), s.sem("masked"), s.sem("centred")
        exped, probs_ready, probs_turned = s.sem("exped"), s.sem("probs_ready"), s.sem("probs_turned")
        o_full, o_out, biased, x_out = s.sem("o_full"), s.sem("o_out"), s.sem("biased"), s.sem("x_out")
        dve_own = s.sem("dve_own")
        block = s.block()
        R_PROJ = NT
        R_V = R_PROJ + NPROJ
        R_TILE = R_V + NT
        R_Y = R_TILE + 5 * NT
        W_IN = 16 * (5 if rope else 6)

        @block.sync
        def _(sp):
            sp.dma_start(w[:], d[w_dram]).then_inc(w_in, 16)
            sp.dma_start(wv[:], d[v_dram]).then_inc(w_in, 16)
            sp.dma_start(wo[:], d[wo_dram]).then_inc(w_in, 16)
            if rope:
                sp.dma_start(cos[:], d["rope_cos"]).then_inc(w_in, 16)
                sp.dma_start(sin[:], d["rope_sin"]).then_inc(w_in, 16)
            else:
                sp.dma_start(bias[:], d[bias_dram + "_qk"]).then_inc(w_in, 16)
                sp.dma_start(bias_v[:], rows(d[bias_dram + "_v"])).then_inc(w_in, 16)
                sp.dma_start(bias_o[:], rows(d[bias_dram + "_o"])).then_inc(w_in, 16)

        @block.gpsimd
        def _(pool):
            pool.memset(causal[:], 0.0).then_inc(mask_made, 1)
            pool.wait_ge(mask_made, 1)
            pool.affine_select(out=causal[:], in_=causal[:], compare_op=ALU.is_ge, fill=MASKED, base=0,
                               pattern=[[-1, P]], channel_multiplier=1).then_inc(mask_made, 1)
            pool.wait_ge(mask_made, 2)
            pool.memset(causal[SEQ:P, 0:SEQ], MASKED).then_inc(mask_made, 1)
            if not rope:
                pool.wait_ge(mask_made, 3)
                pool.wait_ge(norm.normed, NT)
                pool.wait_ge(w_in, W_IN)
                pool.tensor_tensor(g.x[:], g.x[:], bias_o[:].unsqueeze(1).to_broadcast([P, NT, D]),
                                   ALU.add).then_inc(biased, 1)

        @block.vector
        def _(dve):
            own = Steps(dve, dve_own)
            norm.on_vector(dve, g.x, g.hn)
            dve.wait_ge(w_in, W_IN)
            if rope:
                for n in range(NQK):
                    u = R_PROJ + 2 * n
                    dve.wait_ge(ring_full, u + 1)
                    own.did(dve.tensor_tensor(qk_T[:, n, :], flat(ring[u % 4]), cos[:], ALU.mult))
                    own.wait()
                    dve.sem_inc(ring_out, 1)
                    dve.wait_ge(ring_full, u + 2)
                    own.did(dve.tensor_tensor(half[:], flat(ring[(u + 1) % 4]), sin[:], ALU.mult))
                    own.wait()
                    dve.sem_inc(ring_out, 1)
                    dve.tensor_tensor(qk_T[:, n, :], qk_T[:, n, :], half[:], ALU.add).then_inc(heads_ready, 1)
                    dve.wait_ge(heads_ready, n + 1)
            else:
                for n in range(NQK):
                    u = R_PROJ + n
                    dve.wait_ge(ring_full, u + 1)
                    own.did(dve.tensor_scalar(qk_T[:, n, :], flat(ring[u % 4]), bias[:, n:n + 1], None, ALU.add))
                    own.wait()
                    dve.sem_inc(ring_out, 1)
            for t in range(NT):
                u = R_V + t
                dve.wait_ge(ring_full, u + 1)
                part = flat(ring[u % 4])[:, 0:v_cols]
                if rope:
                    own.did(dve.tensor_copy(v[:, t, :], part))
                else:
                    own.did(dve.tensor_tensor(v[:, t, :], part, bias_v[:], ALU.add))
                own.wait()
                dve.sem_inc(ring_out, 1)
            dve.sem_inc(v_ready, 1)
            dve.wait_ge(mask_made, 3)
            for t in range(NT):
                if t >= 1:
                    dve.wait_ge(ring_full, R_TILE + 5 * (t - 1) + 4)
                for i in range(4):
                    dve.wait_ge(scores_full, 4 * t + i + 1)
                    dve.tensor_tensor(scores[:, i, :, :], bank[i][:], causal[:].unsqueeze(1).to_broadcast([P, 4, P]),
                                      ALU.add).then_inc(masked, 1)
                dve.wait_ge(masked, 4 * t + 4)
                by_head = scores[:].rearrange("p i c k -> p (i c) k")
                own.did(dve.tensor_reduce(top[:], by_head, AXX, ALU.max))
                own.wait()
                dve.tensor_tensor(by_head, by_head, top[:].unsqueeze(2).to_broadcast([P, H, P]),
                                  ALU.subtract).then_inc(centred, 1)
                dve.wait_ge(exped, t + 1)
                own.did(dve.tensor_reduce(total[:], by_head, AXX, ALU.add))
                own.wait()
                own.did(dve.reciprocal(total[:], total[:]))
                own.wait()
                dve.tensor_tensor(by_head, by_head, total[:].unsqueeze(2).to_broadcast([P, H, P]),
                                  ALU.mult).then_inc(probs_ready, 1)
            if not rope:
                dve.wait_ge(biased, 1)
            for t in range(NT):
                dve.wait_ge(ring_full, R_Y + t + 1)
                dve.tensor_tensor(g.x[:, t, :], flat(ring[(R_Y + t) % 4]), g.x[:, t, :], ALU.add).then_inc(x_out, 1)

        @block.scalar
        def _(act):
            norm.on_scalar(act, g.eps[:])
            for t in range(NT):
                act.wait_ge(ring_full, t + 1)
                act.activation(g.hT[:, :, t * P:(t + 1) * P], ring[t % 4][:], ACT.Copy).then_inc(ring_out, 1)
            for t in range(NT):
                act.wait_ge(centred, t + 1)
                act.activation(scores[:], scores[:], ACT.Exp, scale=scale).then_inc(exped, 1)
                if t >= 1:
                    act.wait_ge(ring_full, R_TILE + 5 * t)
                for i in range(4):
                    u = R_TILE + 5 * t + i
                    act.wait_ge(ring_full, u + 1)
                    act.activation(probs_T[:, 4 * i:4 * i + 4, :], ring[u % 4][:], ACT.Copy).then_inc(ring_out, 1)
                u = R_TILE + 5 * t + 4
                act.wait_ge(ring_full, u + 1)
                act.activation(o_T[:, :, t * P:(t + 1) * P], ring[u % 4][:], ACT.Copy).then_inc(ring_out, 1)

        @block.tensor
        def _(pe):
            pe.wait_ge(norm.normed, NT)
            for t in range(NT):
                for k in range(KD):
                    last = pe.transpose(ring[t][:, k, :], g.hn[:, t, k * P:(k + 1) * P], g.ident[:])
                last.then_inc(ring_full, 1)
            pe.wait_ge(w_in, W_IN)
            for n in range(NPROJ):
                u = R_PROJ + n
                pe.wait_ge(ring_out, max(u - 3, NT))
                col = (n // 2 + n % 2 * NQK) if rope else n
                for k in range(KD):
                    last = pe.matmul(flat(ring[u % 4]), w[:, k, col * P:(col + 1) * P], g.hT[:, k, :],
                                     start=(k == 0), stop=(k == KD - 1))
                last.then_inc(ring_full, 1)
            for t in range(NT):
                u = R_V + t
                pe.wait_ge(ring_out, u - 3)
                for k in range(KD):
                    last = pe.matmul(flat(ring[u % 4])[:, 0:v_cols], g.hT[:, k, t * P:(t + 1) * P], wv[:, k, :],
                                     start=(k == 0), stop=(k == KD - 1))
                last.then_inc(ring_full, 1)
            pe.wait_ge(ring_out, R_TILE)
            if rope:
                pe.wait_ge(heads_ready, NQK)

            def tile_scores(t):
                tok = slice(t * P, (t + 1) * P)
                for i in range(4):
                    if t >= 1:
                        pe.wait_ge(masked, 4 * (t - 1) + i + 1)
                    r = slice(HD * i, HD * i + HD)
                    for c in range(4):
                        key = 4 + (c if n_k == 4 else 0)
                        last = pe.matmul(bank[i][:, c, :], qk_T[r, c, tok], qk_T[r, key, tok], start=True, stop=True)
                    last.then_inc(scores_full, 1)

            tile_scores(0)
            for t in range(NT):
                if t + 1 < NT:
                    tile_scores(t + 1)
                pe.wait_ge(probs_ready, t + 1)
                for i in range(4):
                    u = R_TILE + 5 * t + i
                    pe.wait_ge(ring_out, u - 3)
                    for c in range(4):
                        last = pe.transpose(ring[u % 4][:, c, :], scores[:, i, c, :], g.ident[:])
                    last.then_inc(ring_full, 1)
                u = R_TILE + 5 * t + 4
                pe.wait_ge(ring_out, u)
                for c in range(4):
                    for i in range(4):
                        h = c * 4 + i
                        vh = v[:, t, h * HD:(h + 1) * HD] if v_cols > HD else v[:, t, :]
                        last = pe.matmul(ring[u % 4][i * HD:(i + 1) * HD, c, :], vh, probs_T[:, i * 4 + c, :],
                                         start=True, stop=True)
                last.then_inc(ring_full, 1)
            pe.wait_ge(ring_out, R_Y)
            for t in range(NT):
                u = R_Y + t
                for k in range(KD):
                    last = pe.matmul(flat(ring[u % 4]), o_T[:, k, t * P:(t + 1) * P], wo[:, k, :],
                                     start=(k == 0), stop=(k == KD - 1))
                last.then_inc(ring_full, 1)


def flat(bank):
    return bank[:].rearrange("p k n -> p (k n)")


E_N = 8
TOP = 2


def choose(dve, own, probs, above, equal, before, rank, chosen):
    mine = probs[:].unsqueeze(3).to_broadcast([P, NT, E_N, E_N])
    other = probs[:].unsqueeze(2).to_broadcast([P, NT, E_N, E_N])
    own.did(dve.tensor_tensor(above[:], other, mine, ALU.is_gt))
    own.did(dve.tensor_tensor(equal[:], other, mine, ALU.is_equal))
    own.wait()
    flat_equal = equal[:].rearrange("p t e f -> p t (e f)")
    own.did(dve.tensor_tensor(flat_equal, flat_equal, before[:].unsqueeze(1).to_broadcast([P, NT, E_N * E_N]),
                              ALU.mult))
    own.wait()
    own.did(dve.tensor_tensor(above[:], above[:], equal[:], ALU.add))
    own.wait()
    own.did(dve.tensor_reduce(rank[:], above[:], AXX, ALU.add))
    own.wait()
    own.did(dve.tensor_scalar(rank[:], rank[:], TOP - 0.5, None, ALU.is_lt))
    own.wait()
    own.did(dve.tensor_tensor(chosen, probs[:], rank[:], ALU.mult))
    own.wait()


def shared_and_routed_experts(g):
    nc, d = g.nc, g.dram
    F = 1024
    FC = F // P
    NE = E_N + 1
    LANDING, SPLIT = 2, 4
    AHEAD = 2
    BEGIN = 2
    GATE, UP, DOWN = 0, 1, 2
    with Stage(nc, "c") as s:
        arrived = s.sb("arrived", [P, LANDING, 3, D])
        w_high = s.sb("w_high", [P, SPLIT, 3, D], F32R)
        w_low = s.sb("w_low", [P, SPLIT, 3, D], F32R)
        w_route = s.sb("w_route", [P, KD, E_N])
        bias = s.sb("bias", [P, E_N])
        before = s.sb("before", [P, E_N * E_N])
        norm = Norm(s)
        probs = s.sb("probs", [P, NT, E_N])
        above = s.sb("above", [P, NT, E_N, E_N])
        equal = s.sb("equal", [P, NT, E_N, E_N])
        rank = s.sb("rank", [P, NT, E_N])
        weight = s.sb("weight", [P, NT, NE])
        silu = s.sb("silu", [P, 2, TOK])
        hidden = s.sb("hidden", [P, 2, TOK])
        hidden_high = s.sb("hidden_high", [P, 2, TOK], F32R)
        hidden_low = s.sb("hidden_low", [P, 2, TOK], F32R)
        h_high = s.sb("h_high", [P, KD, TOK], F32R)
        h_low = s.sb("h_low", [P, KD, TOK], F32R)
        up = [s.ps(f"up{i}", [P, TOK]) for i in range(4)]
        y = [s.ps(f"y{i}", [P, D]) for i in range(NT)]
        r_in = s.sem("r_in")
        w_in = [s.sem(f"w_in{i}") for i in range(LANDING)]
        high_ready, low_ready = s.sem("high_ready"), s.sem("low_ready")
        h_high_ready, h_low_ready = s.sem("h_high_ready"), s.sem("h_low_ready")
        turned_full, turned_out = s.sem("turned_full"), s.sem("turned_out")
        routed, biased, probs_ready, weights_ready = (s.sem("routed"), s.sem("biased"), s.sem("probs_ready"),
                                                      s.sem("weights_ready"))
        gate_full, up_full, silu_ready, hidden_ready = (s.sem("gate_full"), s.sem("up_full"), s.sem("silu_ready"),
                                                        s.sem("hidden_ready"))
        hidden_high_ready, hidden_low_ready = s.sem("hidden_high_ready"), s.sem("hidden_low_ready")
        down_done, y_out = s.sem("down_done"), s.sem("y_out")
        dve_own = s.sem("dve_own")
        ss = StateSpace(s, g)
        block = s.block()

        @block.gpsimd
        def _(pool):
            ss.on_gpsimd(pool)

        def in_chunks(eng, chunk, finish, aside=lambda: None):
            chunk(0, 0, True)
            aside()
            with eng.Fori(0, NE - 1) as e:
                for m in range(1, FC):
                    chunk(e, m, True)
                chunk(e + 1, 0, True)
                finish(e)
            for m in range(1, FC):
                chunk(NE - 1, m, m + AHEAD < FC)
            finish(NE - 1)

        def nth(e, m, start=0):
            return e * FC + (m + 1 + start)

        @block.sync
        def _(sp):
            sp.dma_start(w_route[:], d["L0_ffn_Wr"]).then_inc(r_in, 16)
            sp.dma_start(bias[:], rows(d["L0_ffn_rb"])).then_inc(r_in, 16)
            sp.dma_start(before[:], rows(d["before"])).then_inc(r_in, 16)
            def load(e, m):
                sp.dma_start(arrived[:, m % LANDING], d["L0_ffn_W"][bass.ds(e, 1), m].rearrange("a p k n -> (a p) k n")
                             ).then_inc(w_in[m % LANDING], 16)

            for m in range(LANDING):
                load(0, m)
            ss.on_sync(sp)

            def reload(e, m, more):
                sp.wait_ge(low_ready, nth(e, m))
                if more:
                    load(e + (m + LANDING) // FC, (m + LANDING) % FC)

            in_chunks(sp, reload, lambda e: None)

        @block.vector
        def _(dve):
            dve.sem_inc(y_out, FIRST)
            dve.sem_inc(hidden_ready, BEGIN)
            own = Steps(dve, dve_own)
            norm.on_vector(dve, g.x, g.hn)
            dve.wait_ge(r_in, 48)
            own.did(dve.memset(weight[:], 1.0))

            def split(e, m):
                dve.wait_ge(high_ready, nth(e, m))
                dve.tensor_tensor(w_low[:, m % SPLIT], arrived[:, m % LANDING], w_high[:, m % SPLIT],
                                  ALU.subtract).then_inc(low_ready, 1)

            for t in range(NT):
                dve.wait_ge(h_high_ready, t + 1)
                r = slice(t * P, (t + 1) * P)
                dve.tensor_tensor(h_low[:, :, r], g.hT[:, :, r], h_high[:, :, r], ALU.subtract
                                  ).then_inc(h_low_ready, 1)
            dve.wait_ge(routed, 1)
            dve.tensor_tensor(probs[:], up[3][:, 0:NT * E_N].rearrange("p (t e) -> p t e", t=NT),
                              bias[:].unsqueeze(1).to_broadcast([P, NT, E_N]), ALU.add).then_inc(biased, 1)
            for m in range(AHEAD):
                split(0, m)

            def aside():
                dve.wait_ge(probs_ready, 1)
                choose(dve, own, probs, above, equal, before, rank, weight[:, :, 1:NE])
                ss.on_vector(dve)

            def multiply(e, m, more):
                i = m % 2
                if more:
                    split(e + (m + AHEAD) // FC, (m + AHEAD) % FC)
                dve.wait_ge(silu_ready, nth(e, m))
                dve.wait_ge(up_full, nth(e, m))
                dve.tensor_tensor(hidden[:, i, :], silu[:, i, :], up[2 + i][:], ALU.mult).then_inc(hidden_ready, 1)
                dve.wait_ge(hidden_high_ready, nth(e, m))
                dve.tensor_tensor(hidden_low[:, i, :], hidden[:, i, :], hidden_high[:, i, :],
                                  ALU.subtract).then_inc(hidden_low_ready, 1)

            def add(e):
                dve.wait_ge(down_done, nth(e, FC - 1, BEGIN))
                dve.wait_ge(y_out, e * NT + FIRST)
                for t in range(NT):
                    dve.scalar_tensor_tensor(out=g.x[:, t, :], in0=y[t][:], scalar=weight[:, t, bass.ds(e, 1)],
                                             in1=g.x[:, t, :], op0=ALU.mult, op1=ALU.add).then_inc(y_out, 1)

            in_chunks(dve, multiply, add, aside)

        @block.scalar
        def _(act):
            norm.on_scalar(act, g.eps[:])
            for t in range(NT):
                act.wait_ge(turned_full, t + 1)
                act.activation(g.hT[:, :, t * P:(t + 1) * P], y[t][:].rearrange("p (k n) -> p k n", k=KD),
                               ACT.Copy).then_inc(turned_out, 1)
            for t in range(NT):
                act.wait_ge(turned_out, t + 1)
                act.activation(h_high[:, :, t * P:(t + 1) * P], g.hT[:, :, t * P:(t + 1) * P],
                               ACT.Copy).then_inc(h_high_ready, 1)

            def split(e, m):
                act.wait_ge(w_in[m % LANDING], e * (16 * FC // LANDING) + (m // LANDING + 1) * 16)
                act.wait_ge(down_done, nth(e, m, BEGIN - SPLIT)) if not (isinstance(e, int) and e == 0) else None
                act.activation(w_high[:, m % SPLIT], arrived[:, m % LANDING], ACT.Copy).then_inc(high_ready, 1)

            for m in range(AHEAD):
                split(0, m)
            act.wait_ge(biased, 1)
            act.activation(probs[:], probs[:], ACT.Sigmoid).then_inc(probs_ready, 1)
            ss.steps_on_scalar(act)

            def gate(e, m, more):
                i = m % 2
                if more:
                    split(e + (m + AHEAD) // FC, (m + AHEAD) % FC)
                act.wait_ge(gate_full, nth(e, m))
                act.wait_ge(hidden_ready, nth(e, m, BEGIN - 2))
                act.activation(silu[:, i, :], up[i][:], ACT.Silu).then_inc(silu_ready, 1)
                act.wait_ge(hidden_ready, nth(e, m, BEGIN))
                act.wait_ge(down_done, nth(e, m, BEGIN - 2))
                act.activation(hidden_high[:, i, :], hidden[:, i, :], ACT.Copy).then_inc(hidden_high_ready, 1)

            in_chunks(act, gate, lambda e: None, lambda: ss.waves_on_scalar(act))

        @block.tensor
        def _(pe):
            pe.sem_inc(down_done, BEGIN)
            pe.wait_ge(norm.normed, NT)
            for t in range(NT):
                for k in range(KD):
                    last = pe.transpose(y[t][:, k * P:(k + 1) * P], g.hn[:, t, k * P:(k + 1) * P], g.ident[:])
                last.then_inc(turned_full, 1)
            pe.wait_ge(turned_out, NT)
            pe.wait_ge(r_in, 48)
            for t in range(NT):
                for k in range(KD):
                    last = pe.matmul(up[3][:, t * E_N:(t + 1) * E_N], g.hT[:, k, t * P:(t + 1) * P], w_route[:, k, :],
                                     start=(k == 0), stop=(k == KD - 1))
            last.then_inc(routed, 1)
            pe.wait_ge(biased, 1)

            def wide(e, m):
                i = m % 2
                pe.wait_ge(hidden_ready, nth(e, m, BEGIN - 2))
                pe.wait_ge(low_ready, nth(e, m))
                for part, bank, signal in ((GATE, up[i], gate_full), (UP, up[2 + i], up_full)):
                    for k in range(KD):
                        r = slice(k * P, (k + 1) * P)
                        last = product(pe, bank[:], (w_high[:, m % SPLIT, part, r], w_low[:, m % SPLIT, part, r]),
                                       (h_high[:, k, :], h_low[:, k, :]), k, KD - 1)
                    last.then_inc(signal, 1)

            def down(e, m):
                i = m % 2
                pe.wait_ge(hidden_low_ready, nth(e, m))
                if m == 0:
                    pe.wait_ge(y_out, e * NT + FIRST)
                for t in range(NT):
                    r = slice(t * P, (t + 1) * P)
                    last = product(pe, y[t][:], (hidden_high[:, i, r], hidden_low[:, i, r]),
                                   (w_high[:, m % SPLIT, DOWN, :], w_low[:, m % SPLIT, DOWN, :]), m, FC - 1)
                last.then_inc(down_done, 1)

            def chunk(e, m, more):
                wide(e, m)
                if m:
                    down(e, m - 1)

            pe.wait_ge(h_low_ready, NT)
            in_chunks(pe, chunk, lambda e: down(e, FC - 1))


def capacity_experts(g):
    nc, d = g.nc, g.dram
    F = 2048
    FC = F // P
    CAP = -(-TOK * TOP * 5 // (4 * E_N))
    REST = CAP - P
    TRIPLES = [(m, min(m + 3, FC)) for m in range(0, FC, 3)]
    assert 0 < REST <= 32 and 3 * CAP <= 512 < 4 * CAP
    with Stage(nc, "f") as s:
        w1 = s.sb("w1", [P, KD, F])
        w2 = s.sb("w2", [P, FC, D])
        w_route = s.sb("w_route", [P, KD, E_N])
        before = s.sb("before", [P, E_N * E_N])
        slots = s.sb("slots", [P, CAP])
        earlier = s.sb("earlier", [P, NT, TOK])
        norm = Norm(s)
        probs = s.sb("probs", [P, NT, E_N])
        above = s.sb("above", [P, NT, E_N, E_N])
        equal = s.sb("equal", [P, NT, E_N, E_N])
        rank8 = s.sb("rank8", [P, NT, E_N])
        stat = s.sb("stat", [P, NT])
        gate = s.sb("gate", [P, NT, E_N + 1])
        gate_rows = s.sb("gate_rows", [P, E_N + 1, TOK])
        compared = s.sb("compared", [P, TOK])
        better = s.sb("better", [P, NT])
        level = s.sb("level", [P, NT])
        place = s.sb("place", [P, NT])
        pick = s.sb("pick", [P, NT, CAP])
        pick_gate = s.sb("pick_gate", [P, NT, CAP])
        picked_T = s.sb("picked_T", [P, KD, CAP])
        put_back = s.sb("put_back", [P, 2, NT, P])
        hidden = s.sb("hidden", [P, FC, CAP])
        y_T = s.sb("y_T", [P, KD, CAP])
        y = s.sb("y", [P, 2, D])
        zero = s.sb("zero", [1, D])
        acc = [s.ps(f"acc{t}", [P, D]) for t in range(NT)]
        ring = [s.ps(f"ring{i}", [P, 512]) for i in range(2)]
        side = [s.ps(f"side{i}", [P, 512]) for i in range(2)]
        r_in, w1_in, w2_in = s.sem("r_in"), s.sem("w1_in"), s.sem("w2_in")
        pool_own, dve_own = s.sem("pool_own"), s.sem("dve_own")
        turned_full, turned_out, routed, centred = (s.sem("turned_full"), s.sem("turned_out"), s.sem("routed"),
                                                    s.sem("centred"))
        exped, gates_ready, rows_full, rows_out = (s.sem("exped"), s.sem("gates_ready"), s.sem("rows_full"),
                                                   s.sem("rows_out"))
        picks_ready = s.sem("picks_ready")
        side_full, side_out = s.sem("side_full"), s.sem("side_out")
        ring_full, ring_out = s.sem("ring_full"), s.sem("ring_out")
        acc_full = s.sem("acc_full")
        N_SIDE = 6
        N_RING = len(TRIPLES) + 2
        block = s.block()

        def load(sp, w, name, e, sem):
            sp.dma_start(w[:], d[name][bass.ds(e, 1)].rearrange("a p k n -> p (a k) n")).then_inc(sem, 16)

        @block.sync
        def _(sp):
            sp.dma_start(w_route[:], d["L1_ffn_Wr"]).then_inc(r_in, 16)
            sp.dma_start(before[:], rows(d["before"])).then_inc(r_in, 16)
            sp.dma_start(slots[:], rows(d["slots"])).then_inc(r_in, 16)
            load(sp, w1, "L1_ffn_W1", 0, w1_in)
            load(sp, w2, "L1_ffn_W2", 0, w2_in)
            with sp.Fori(0, E_N - 1) as e:
                sp.wait_ge(ring_full, e * N_RING + len(TRIPLES))
                load(sp, w1, "L1_ffn_W1", e + 1, w1_in)
                sp.wait_ge(ring_full, e * N_RING + N_RING)
                load(sp, w2, "L1_ffn_W2", e + 1, w2_in)

        @block.gpsimd
        def _(pool):
            pool.memset(zero[:], 0.0).then_inc(pool_own, 1)
            pool.wait_ge(pool_own, 1)
            pool.memset(gate[:], 0.0).then_inc(pool_own, 1)
            pool.wait_ge(pool_own, 2)
            pool.memset(gate_rows[:, E_N, :], 0.0).then_inc(pool_own, 1)
            pool.wait_ge(pool_own, 3)
            pool.memset(earlier[:], 1.0).then_inc(pool_own, 1)
            pool.wait_ge(pool_own, 4)
            pool.affine_select(out=earlier[:], in_=earlier[:], compare_op=ALU.is_gt, fill=0.0, base=0,
                               pattern=[[P, NT], [-1, TOK]], channel_multiplier=1).then_inc(pool_own, 1)

        @block.vector
        def _(dve):
            for signal in (side_out,):
                dve.sem_inc(signal, FIRST)
            own = Steps(dve, dve_own)
            norm.on_vector(dve, g.x, g.hn)
            dve.wait_ge(r_in, 48)
            dve.wait_ge(pool_own, 5)
            dve.wait_ge(routed, 1)
            logits = side[0][:, 0:NT * E_N].rearrange("p (t e) -> p t e", t=NT)
            own.did(dve.tensor_reduce(stat[:], logits, AXX, ALU.max))
            own.wait()
            dve.tensor_tensor(probs[:], logits, stat[:].unsqueeze(2).to_broadcast([P, NT, E_N]),
                              ALU.subtract).then_inc(centred, 1)
            dve.wait_ge(exped, 1)
            own.did(dve.tensor_reduce(stat[:], probs[:], AXX, ALU.add))
            own.wait()
            own.did(dve.reciprocal(stat[:], stat[:]))
            own.wait()
            own.did(dve.tensor_tensor(probs[:], probs[:], stat[:].unsqueeze(2).to_broadcast([P, NT, E_N]), ALU.mult))
            own.wait()
            choose(dve, own, probs, above, equal, before, rank8, gate[:, :, 0:E_N])
            dve.sem_inc(gates_ready, 1)

            def place_tokens(e, own, turned=None):
                row = gate_rows[:, bass.ds(e, 1), :].rearrange("p a n -> p (a n)")
                for t in range(NT):
                    mine = gate[:, t, bass.ds(e, 1)]
                    own.did(dve.tensor_scalar(compared[:], row, mine, 0.0, ALU.is_gt, ALU.add,
                                              accum_out=better[:, t:t + 1]))
                    own.wait()
                    own.did(dve.scalar_tensor_tensor(out=compared[:], in0=row, scalar=mine, in1=earlier[:, t, :],
                                                     op0=ALU.is_equal, op1=ALU.mult,
                                                     accum_out=level[:, t:t + 1]))
                    own.wait()
                own.did(dve.tensor_tensor(place[:], better[:], level[:], ALU.add))
                own.wait()
                if turned:
                    dve.wait_ge(*turned)
                for t in range(NT):
                    dve.tensor_scalar(pick[:, t, :], slots[:], place[:, t:t + 1], None,
                                      ALU.is_equal).then_inc(picks_ready, 1)
                    dve.tensor_scalar(pick_gate[:, t, :], slots[:], place[:, t:t + 1], gate[:, t, bass.ds(e, 1)],
                                      ALU.is_equal, ALU.mult).then_inc(picks_ready, 1)

            dve.wait_ge(rows_out, E_N)
            place_tokens(0, own)
            with dve.Fori(0, E_N) as e:
                restart(dve, dve_own)
                own = Steps(dve, dve_own)
                dve.wait_ge(side_full, e * N_SIDE + 1)
                dve.tensor_copy(picked_T[:, 0:3, :], side[0][:, 0:3 * CAP].rearrange("p (k n) -> p k n", k=3)
                                ).then_inc(side_out, 1)
                dve.wait_ge(side_full, e * N_SIDE + 2)
                dve.tensor_copy(picked_T[:, 3, :], side[1][:, 0:CAP]).then_inc(side_out, 1)
                dve.wait_ge(acc_full, e + FIRST)
                for j in range(2):
                    m = P if j == 0 else REST
                    dve.wait_ge(side_full, e * N_SIDE + (3 + j))
                    dve.tensor_copy(put_back[0:m, j, :, :], side[j][0:m, :].rearrange("p (t n) -> p t n", t=NT)
                                    ).then_inc(side_out, 1)
                place_tokens(e + 1, own, (side_full, e * N_SIDE + 4))
                for j in range(2):
                    m = P if j == 0 else REST
                    dve.wait_ge(side_full, e * N_SIDE + (5 + j))
                    dve.tensor_copy(y[0:m, j, :], side[j][0:m, :]).then_inc(side_out, 1)
                own.wait()
            for t in range(NT):
                dve.wait_ge(acc_full, E_N + FIRST)
                dve.tensor_tensor(g.x[:, t, :], acc[t][:], g.x[:, t, :], ALU.add).then_inc(side_out, 1)

        @block.scalar
        def _(act):
            for signal in (ring_out,):
                act.sem_inc(signal, FIRST)
            norm.on_scalar(act, g.eps[:])
            for t in range(NT):
                act.wait_ge(turned_full, t + 1)
                act.activation(g.hT[:, :, t * P:(t + 1) * P], acc[t][:].rearrange("p (k n) -> p k n", k=KD),
                               ACT.Copy).then_inc(turned_out, 1)
            act.wait_ge(centred, 1)
            act.activation(probs[:], probs[:], ACT.Exp).then_inc(exped, 1)
            act.wait_ge(pool_own, 5)
            for e in range(E_N):
                act.wait_ge(rows_full, e + 1)
                act.activation(gate_rows[:, e, :], acc[e % NT][:], ACT.Copy).then_inc(rows_out, 1)
            with act.Fori(0, E_N) as e:
                for n, (lo, hi) in enumerate(TRIPLES):
                    act.wait_ge(ring_full, e * N_RING + (n + 1))
                    act.activation(hidden[:, lo:hi, :], ring[n % 2][:, 0:(hi - lo) * CAP]
                                   .rearrange("p (m n) -> p m n", m=hi - lo), ACT.Relu).then_inc(ring_out, 1)
                for j, (lo, hi) in enumerate(((0, 3), (3, 4))):
                    n = len(TRIPLES) + j
                    act.wait_ge(ring_full, e * N_RING + (n + 1))
                    act.activation(y_T[:, lo:hi, :], ring[n % 2][:, 0:(hi - lo) * CAP]
                                   .rearrange("p (m n) -> p m n", m=hi - lo), ACT.Copy).then_inc(ring_out, 1)

        @block.tensor
        def _(pe):
            for signal in (acc_full,):
                pe.sem_inc(signal, FIRST)
            pe.wait_ge(norm.normed, NT)
            for t in range(NT):
                for k in range(KD):
                    last = pe.transpose(acc[t][:, k * P:(k + 1) * P], g.hn[:, t, k * P:(k + 1) * P], g.ident[:])
                last.then_inc(turned_full, 1)
            pe.wait_ge(turned_out, NT)
            pe.wait_ge(r_in, 48)
            for t in range(NT):
                for k in range(KD):
                    last = pe.matmul(side[0][:, t * E_N:(t + 1) * E_N], g.hT[:, k, t * P:(t + 1) * P],
                                     w_route[:, k, :], start=(k == 0), stop=(k == KD - 1))
            last.then_inc(routed, 1)
            pe.wait_ge(gates_ready, 1)
            for e in range(E_N):
                if e >= NT:
                    pe.wait_ge(rows_out, e - NT + 1)
                for t in range(NT):
                    last = pe.transpose(acc[e % NT][:, t * P:(t + 1) * P], gate[:, t, e:e + 1].to_broadcast([P, P]),
                                        g.ident[:])
                last.then_inc(rows_full, 1)
            pe.wait_ge(rows_out, E_N)
            for t in range(NT):
                pe.matmul(acc[t][:], zero[:, 0:P], zero[:], start=True, stop=False, skip_group_check=True)
            assert N_RING % 2 == 0 and N_SIDE % 2 == 0
            with pe.Fori(0, E_N) as e:
                pe.wait_ge(picks_ready, e * 2 * NT + 2 * NT)
                for k in range(KD):
                    if k == 0:
                        pe.wait_ge(side_out, e * N_SIDE + FIRST)
                    out = side[0][:, k * CAP:(k + 1) * CAP] if k < 3 else side[1][:, 0:CAP]
                    for t in range(NT):
                        last = pe.matmul(out, g.hn[:, t, k * P:(k + 1) * P], pick[:, t, :], start=(t == 0),
                                         stop=(t == NT - 1))
                    if k >= 2:
                        last.then_inc(side_full, 1)
                for j in range(2):
                    m = P if j == 0 else REST
                    pe.wait_ge(side_out, e * N_SIDE + (1 + j) + FIRST)
                    for t in range(NT):
                        last = pe.transpose(side[j][0:m, t * P:(t + 1) * P], pick_gate[:, t, j * P:j * P + m],
                                            g.ident[:])
                    last.then_inc(side_full, 1)
                pe.wait_ge(side_out, e * N_SIDE + 2 + FIRST)
                pe.wait_ge(w1_in, e * 16 + 16)
                for n, (lo, hi) in enumerate(TRIPLES):
                    pe.wait_ge(ring_out, e * N_RING + (n - 1 if n >= 2 else 0) + FIRST)
                    for m in range(lo, hi):
                        for k in range(KD):
                            last = pe.matmul(ring[n % 2][:, (m - lo) * CAP:(m - lo + 1) * CAP],
                                             w1[:, k, m * P:(m + 1) * P], picked_T[:, k, :], start=(k == 0),
                                             stop=(k == KD - 1))
                    last.then_inc(ring_full, 1)
                pe.wait_ge(w2_in, e * 16 + 16)
                for j, (lo, hi) in enumerate(((0, 3), (3, 4))):
                    n = len(TRIPLES) + j
                    pe.wait_ge(ring_out, e * N_RING + len(TRIPLES) + FIRST)
                    for m in range(lo, hi):
                        for k in range(FC):
                            last = pe.matmul(ring[n % 2][:, (m - lo) * CAP:(m - lo + 1) * CAP],
                                             w2[:, k, m * P:(m + 1) * P], hidden[:, k, :], start=(k == 0),
                                             stop=(k == FC - 1))
                    last.then_inc(ring_full, 1)
                pe.wait_ge(ring_out, e * N_RING + N_RING + FIRST)
                for j in range(2):
                    m = P if j == 0 else REST
                    pe.wait_ge(side_out, e * N_SIDE + (3 + j) + FIRST)
                    for k in range(KD):
                        last = pe.transpose(side[j][0:m, k * P:(k + 1) * P], y_T[:, k, j * P:j * P + m], g.ident[:])
                    last.then_inc(side_full, 1)
                pe.wait_ge(side_out, e * N_SIDE + 6 + FIRST)
                for t in range(NT):
                    for j in range(2):
                        m = P if j == 0 else REST
                        last = pe.matmul(acc[t][:], put_back[0:m, j, t, :], y[0:m, j, :], start=False,
                                         stop=(j == 1), skip_group_check=True)
                last.then_inc(acc_full, 1)


S4 = 64
MAGIC = 1.5 * 2.0 ** 23
TWO_PI = (6.28125, 0.0019350051879882812, 3.019916e-07)
PI_BELOW = 3.1415925


class StateSpace:

    SMALL = ("ar", "ai", "er", "rs", "rc", "wr", "wi", "nr", "ni", "t0", "t1", "t2")

    def __init__(self, s, g):
        self.g, self.s = g, s
        n = [P, KD, S4]
        self.inp = {k: s.sb(f"ss_{k}", n) for k in ("A_re", "A_im", "C_re", "C_im")}
        self.dt = s.sb("ss_dt", [P, KD])
        self.skip = s.sb("ss_skip", [P, KD])
        self.v = {k: s.sb(f"ss_{k}", n) for k in self.SMALL}
        self.re = s.sb("ss_re", [P, SEQ, S4])
        self.im = s.sb("ss_im", [P, SEQ // 2, S4])
        self.tmp = s.sb("ss_tmp", [P, SEQ // 2, S4])
        self.loaded, self.own = s.sem("ss_loaded"), s.sem("ss_own")
        self.dt_ready, self.phased, self.waved, self.dt_used = (s.sem("ss_dt_ready"), s.sem("ss_phased"),
                                                                s.sem("ss_waved"), s.sem("ss_dt_used"))
        self.inverse_in, self.inverse_out = s.sem("ss_inverse_in"), s.sem("ss_inverse_out")

    def on_sync(self, sp):
        d = self.g.dram
        for k, t in self.inp.items():
            sp.dma_start(t[:], d[f"L1_xattn_{k}"]).then_inc(self.loaded, 16)
        sp.dma_start(self.dt[:], d["L1_xattn_log_dt"]).then_inc(self.loaded, 16)
        sp.dma_start(self.skip[:], d["L1_xattn_D_skip"]).then_inc(self.loaded, 16)

    def steps_on_scalar(self, act):
        act.wait_ge(self.loaded, 96)
        act.activation(self.dt[:], self.dt[:], ACT.Exp).then_inc(self.dt_ready, 1)

    def waves_on_scalar(self, act):
        v = self.v
        act.wait_ge(self.phased, 1)
        act.activation(v["er"][:], v["ar"][:], ACT.Exp).then_inc(self.waved, 1)
        act.activation(v["rs"][:], v["rs"][:], ACT.Sin).then_inc(self.waved, 1)
        act.activation(v["rc"][:], v["rc"][:], ACT.Sin).then_inc(self.waved, 1)

    def on_vector(self, dve):
        dve.wait_ge(self.inverse_in, 1)
        dve.reciprocal(self.v["t2"][:], self.v["t2"][:]).then_inc(self.inverse_out, 1)

    def on_gpsimd(self, pool):
        v, inp, own = self.v, self.inp, Steps(pool, self.own)

        def tt(out, a, b, op):
            own.did(pool.tensor_tensor(out, a, b, op))
            own.wait()

        def ts(out, a, s1, s2, op0, op1):
            own.did(pool.tensor_scalar(out, a, s1, s2, op0, op1))
            own.wait()

        a = {k: t[:] for k, t in v.items()}
        a.update({k: t[:] for k, t in inp.items()})
        pool.wait_ge(self.dt_ready, 1)
        dt = self.dt[:].unsqueeze(2).to_broadcast([P, KD, S4])
        tt(a["ar"], a["A_re"], dt, ALU.mult)
        tt(a["ai"], a["A_im"], dt, ALU.mult)
        for out, shift in (("rs", 0.0), ("rc", 0.25)):
            ts(a["t0"], a["ai"], 1 / (2 * np.pi), shift, ALU.mult, ALU.add)
            ts(a["t0"], a["t0"], MAGIC, -MAGIC, ALU.add, ALU.add)
            src = a["ai"]
            for part in TWO_PI:
                ts(a["t1"], a["t0"], -part, 0.0, ALU.mult, ALU.add)
                tt(a[out], src, a["t1"], ALU.add)
                src = a[out]
            if shift:
                ts(a[out], a[out], np.pi / 2, 0.0, ALU.add, ALU.add)
            ts(a[out], a[out], PI_BELOW, -PI_BELOW, ALU.min, ALU.max)
        pool.sem_inc(self.phased, 1)
        tt(a["t0"], a["A_re"], a["A_re"], ALU.mult)
        tt(a["t1"], a["A_im"], a["A_im"], ALU.mult)
        tt(a["t2"], a["t0"], a["t1"], ALU.add)
        pool.sem_inc(self.inverse_in, 1)
        pool.wait_ge(self.waved, 3)
        tt(a["wr"], a["er"], a["rc"], ALU.mult)
        tt(a["wi"], a["er"], a["rs"], ALU.mult)
        ts(a["er"], a["wr"], -1.0, 0.0, ALU.add, ALU.add)
        tt(a["t0"], a["er"], a["A_re"], ALU.mult)
        tt(a["t1"], a["wi"], a["A_im"], ALU.mult)
        tt(a["nr"], a["t0"], a["t1"], ALU.add)
        tt(a["t0"], a["wi"], a["A_re"], ALU.mult)
        tt(a["t1"], a["er"], a["A_im"], ALU.mult)
        tt(a["ni"], a["t0"], a["t1"], ALU.subtract)
        pool.wait_ge(self.inverse_out, 1)
        ts(a["t2"], a["t2"], 2.0, 0.0, ALU.mult, ALU.add)
        tt(a["nr"], a["nr"], a["t2"], ALU.mult)
        tt(a["ni"], a["ni"], a["t2"], ALU.mult)
        tt(a["t0"], a["nr"], a["C_re"], ALU.mult)
        tt(a["t1"], a["ni"], a["C_im"], ALU.mult)
        tt(a["rs"], a["t0"], a["t1"], ALU.subtract)
        tt(a["t0"], a["nr"], a["C_im"], ALU.mult)
        tt(a["t1"], a["ni"], a["C_re"], ALU.mult)
        tt(a["rc"], a["t0"], a["t1"], ALU.add)
        re, im, tmp = self.re, self.im, self.tmp
        for c in range(KD):
            one = [P, 1, S4]
            wr, wi = v["wr"][:, c:c + 1, :], v["wi"][:, c:c + 1, :]
            tt(re[:, 0:1, :], v["rs"][:, c:c + 1, :], self.g.zero[:].to_broadcast(one), ALU.add)
            tt(im[:, 0:1, :], v["rc"][:, c:c + 1, :], self.g.zero[:].to_broadcast(one), ALU.add)
            h = 1
            while h < SEQ:
                br, bi = wr.to_broadcast([P, h, S4]), wi.to_broadcast([P, h, S4])
                tt(re[:, h:2 * h, :], re[:, 0:h, :], br, ALU.mult)
                tt(tmp[:, 0:h, :], im[:, 0:h, :], bi, ALU.mult)
                tt(re[:, h:2 * h, :], re[:, h:2 * h, :], tmp[:, 0:h, :], ALU.subtract)
                if 2 * h < SEQ:
                    tt(im[:, h:2 * h, :], im[:, 0:h, :], br, ALU.mult)
                    tt(tmp[:, 0:h, :], re[:, 0:h, :], bi, ALU.mult)
                    tt(im[:, h:2 * h, :], im[:, h:2 * h, :], tmp[:, 0:h, :], ALU.add)
                    t0, t1 = v["t0"][:, c:c + 1, :], v["t1"][:, c:c + 1, :]
                    tt(t0, wr, wr, ALU.mult)
                    tt(t1, wi, wi, ALU.mult)
                    tt(wi, wr, wi, ALU.mult)
                    ts(wi, wi, 2.0, 0.0, ALU.mult, ALU.add)
                    tt(wr, t0, t1, ALU.subtract)
                h *= 2
            n = S4 // 2
            while n:
                out = re[:, :, 0:n] if n > 1 else self.g.kern[:, c, :].unsqueeze(2)
                tt(out, re[:, :, 0:n], re[:, :, n:2 * n], ALU.add)
                n //= 2
        tt(self.g.kern[:, :, 0], self.g.kern[:, :, 0], self.skip[:], ALU.add)


def xattn1_context(g, c_T):
    nc, d = g.nc, g.dram
    HD, HEADS, ROUNDS = 32, 4, 4
    SCALE = 1.0 / float(np.sqrt(32.0))
    CHUNKS = [(0, 512), (512, 1024), (1024, 1536), (1536, CTX)]
    PER_KS = 4 + 2 * 4
    BUFS = 3
    LOADED = 16 * 5

    def size(t):
        return P if t < CFULL else CLAST

    with Stage(nc, "d2") as s:
        wq = s.sb("wq", [P, KD, P])
        wk = s.sb("wk", [P, KC, P])
        norm = Norm(s)
        q_T = s.sb("q_T", [P, TOK])
        q_diag = s.sb("q_diag", [P, 2, P])
        ones = s.sb("ones", [1, P], BF16)
        stack = s.sb("stack", [P, SEQ])
        context = s.sb("context", [P, BUFS, CT, DC])
        mask8 = s.sb("mask8", [1, BUFS, CTX], U8)
        mask = s.sb("mask", [1, CTX], BF16)
        context_T = s.sb("context_T", [P, 2, KC, 4 * P])
        k_T = s.sb("k_T", [P, CTX])
        scores = s.sb("scores", [P, 2 * BUFS, CTX])
        left = s.sb("left", [P, 2, CTX])
        best = s.sb("best", [P, 2 * BUFS, ROUNDS * 8])
        neg_top = s.sb("neg_top", [P, 2 * BUFS])
        best_exp = s.sb("best_exp", [P, ROUNDS * 8])
        total = s.sb("total", [P, 2 * BUFS])
        share = s.sb("share", [P, 2, SEQ])
        mean_T = s.sb("mean_T", [P, CT, SEQ])
        ring = [s.ps(f"ring{i}", [P, 4, P]) for i in range(2)]
        ks = [s.ps(f"ks{i}", [P, 512]) for i in range(3)]
        mean = [s.ps(f"mean{i}", [P, 8, SEQ]) for i in range(2)]
        mix = s.ps("mix", [P, KC, SEQ])
        w_in = s.sem("w_in")
        ctx_in = [s.sem(f"ctx_in{i}") for i in range(BUFS)]
        pool_own, dve_own, act_own = s.sem("pool_own"), s.sem("dve_own"), s.sem("act_own")
        q_full, q_out = s.sem("q_full"), s.sem("q_out")
        side_ready = s.sem("side_ready")
        ring_full, ring_out = s.sem("ring_full"), s.sem("ring_out")
        ks_full, ks_out = s.sem("ks_full"), s.sem("ks_out")
        picked, exped, probs_ready, share_ready = (s.sem("picked"), s.sem("exped"), s.sem("probs_ready"),
                                                   s.sem("share_ready"))
        mean_full, mean_out, mix_full, mix_out = (s.sem("mean_full"), s.sem("mean_out"), s.sem("mix_full"),
                                                  s.sem("mix_out"))
        block = s.block()

        def in_turn(eng, step):
            with eng.Fori(0, NB // BUFS) as i:
                for buf in range(BUFS):
                    step(i * BUFS + buf, buf, i, False)
            for b in range(NB - NB % BUFS, NB):
                step(b, b % BUFS, b // BUFS, True)

        @block.sync
        def _(sp):
            sp.dma_start(wq[:], d["L1_xattn_Wq"]).then_inc(w_in, 16)
            sp.dma_start(wk[:], d["L1_xattn_Wk"]).then_inc(w_in, 16)

            def load(b, par):
                src = d["ctx"][b]
                for lo in range(0, CFULL, 4):
                    sp.dma_start(context[:, par, lo:lo + 4, :],
                                 src[lo * P:(lo + 4) * P, :].rearrange("(t p) d -> p t d", p=P)
                                 ).then_inc(ctx_in[par], 16)
                sp.dma_start(context[0:CLAST, par, CFULL, :], src[CFULL * P:CTX, :]).then_inc(ctx_in[par], 16)
                sp.dma_start(mask8[:, par, :], d["mask_ctx1"][b:b + 1, :]).then_inc(ctx_in[par], 16)

            for b in range(NB):
                if b >= BUFS:
                    sp.wait_ge(mix_full, b - BUFS + 1)
                load(b, b % BUFS)

        @block.gpsimd
        def _(pool):
            pool.memset(q_diag[:], 0.0).then_inc(pool_own, 1)
            pool.wait_ge(pool_own, 1)
            pool.memset(ones[:], 1.0).then_inc(pool_own, 1)
            pool.wait_ge(pool_own, 2)
            pool.tensor_tensor(stack[:], g.ident[:, 0:SEQ], g.ident[:, SEQ:P], ALU.add).then_inc(pool_own, 1)
            pool.wait_ge(pool_own, 3)
            pool.wait_ge(q_out, 1)
            SIDE = 1 + HEADS

            def prepare(b, par, turn):
                pool.wait_ge(ctx_in[par], turn * LOADED + LOADED)
                if not (isinstance(b, int) and b == 0):
                    pool.wait_ge(ks_full, b * PER_KS)
                    pool.nop(nofuse=True)
                pool.tensor_scalar(mask[:], mask8[:, par, :], -MASKED, MASKED, ALU.mult,
                                   ALU.add).then_inc(side_ready, 1)
                for h in range(HEADS):
                    pool.wait_ge(side_ready, b * SIDE + (1 + h))
                    r = slice(h * HD, (h + 1) * HD)
                    pool.tensor_copy(q_diag[r, h // 2, (h % 2) * SEQ:(h % 2 + 1) * SEQ],
                                     q_T[r, bass.ds(b * SEQ, SEQ)]).then_inc(side_ready, 1)
                pool.wait_ge(side_ready, b * SIDE + SIDE)

            def step(b, par, turn, last):
                for r in range(2):
                    if r == 1 and not last:
                        prepare(b + 2, (par + 2) % BUFS, turn + (par + 2) // BUFS)
                    pool.wait_ge(exped, b * 2 + (r + 1))
                    sc = scores[:, 2 * par + r, :]
                    pool.tensor_tensor(sc, sc, left[:, r, :], ALU.subtract).then_inc(probs_ready, 1)
                    pool.wait_ge(probs_ready, b * 2 + (r + 1))

            prepare(0, 0, 0)
            prepare(1, 1, 0)
            in_turn(pool, step)

        @block.vector
        def _(dve):
            norm.on_vector(dve, g.x, g.hn)

            def pick(par, r, rounds, after=None):
                own = Steps(dve, dve_own, rounds[0] * 2)
                sc = scores[:, 2 * par + r, :]
                for n in rounds:
                    src = sc if n == 0 else left[:, r, :]
                    eight = best[:, 2 * par + r, 8 * n:8 * n + 8]
                    own.did(dve.max(eight, src))
                    own.wait()
                    if n == 0:
                        if after is not None:
                            dve.wait_ge(probs_ready, after)
                            dve.nop(nofuse=True)
                    ins = dve.match_replace(left[:, r, :], eight, src, MASKED)
                    if n < ROUNDS - 1:
                        own.did(ins)
                        own.wait()
                    else:
                        ins.then_inc(picked, 1)

            def shares(b, par):
                own = Steps(dve, dve_own, 2)
                dve.wait_ge(exped, b * 2 + 2)
                own.did(dve.reciprocal(total[:, 2 * par:2 * par + 2], total[:, 2 * par:2 * par + 2]))
                own.wait()
                dve.wait_ge(mean_full, b * 2 + FIRST)
                for r in range(2):
                    dve.tensor_scalar(share[:, r, :], stack[:], total[:, 2 * par + r:2 * par + r + 1], 1.0 / HEADS,
                                      ALU.mult, ALU.mult).then_inc(share_ready, 1)

            def first(b, par):
                dve.wait_ge(ks_out, b * PER_KS + (8 + 3))
                restart(dve, dve_own)
                pick(par, 0, range(ROUNDS))
                dve.wait_ge(ks_out, b * PER_KS + (12 + 3))
                restart(dve, dve_own)
                pick(par, 1, range(ROUNDS))

            def step(b, par, turn, last):
                if isinstance(b, int) and b == NB - 1:
                    restart(dve, dve_own)
                    dve.sem_inc(dve_own, 2)
                    shares(b, par)
                    return
                q = (par + 1) % BUFS
                dve.wait_ge(ks_out, (b + 1) * PER_KS + (8 + 3))
                restart(dve, dve_own)
                pick(q, 0, range(0, 1), b * 2 + 1)
                shares(b, par)
                pick_rest(q)
                dve.wait_ge(picked, (b + 1) * 2 + 1)
                dve.wait_ge(ks_out, (b + 1) * PER_KS + (12 + 3))
                restart(dve, dve_own)
                pick(q, 1, range(ROUNDS), b * 2 + 2)
                dve.wait_ge(picked, (b + 1) * 2 + 2)

            def pick_rest(par):
                own = Steps(dve, dve_own, 3)
                for n in range(1, ROUNDS):
                    eight = best[:, 2 * par, 8 * n:8 * n + 8]
                    own.did(dve.max(eight, left[:, 0, :]))
                    own.wait()
                    ins = dve.match_replace(left[:, 0, :], eight, left[:, 0, :], MASKED)
                    if n < ROUNDS - 1:
                        own.did(ins)
                        own.wait()
                    else:
                        ins.then_inc(picked, 1)

            first(0, 0)
            dve.wait_ge(picked, 2)
            in_turn(dve, step)

        @block.scalar
        def _(act):
            for signal in (mean_out, mix_out,):
                act.sem_inc(signal, FIRST)
            norm.on_scalar(act, g.eps[:])
            for t in range(NT):
                act.wait_ge(ring_full, t + 1)
                act.activation(g.hT[:, :, t * P:(t + 1) * P], ring[t % 2][:], ACT.Copy).then_inc(ring_out, 1)
            act.wait_ge(q_full, 1)
            act.activation(q_T[:], ks[0][:], ACT.Copy).then_inc(q_out, 1)
            act.wait_ge(ring_out, NT)
            act.wait_ge(q_out, 1)
            act.sem_inc(ks_out, 3)

            def put_context(b, tiles):
                for t in tiles:
                    m = size(t)
                    act.wait_ge(ring_full, b * CT + (t + 1 + NT))
                    if t >= 8 and t % 4 == 0:
                        act.wait_ge(ks_full, b * PER_KS + (t // 4 - 1))
                    act.activation(context_T[:, t // 4 % 2, :, t % 4 * P:t % 4 * P + m], ring[t % 2][:, 0:KC, 0:m],
                                   ACT.Copy).then_inc(ring_out, 1)
                    if t % 4 == 3:
                        put_keys(b, t // 4)
                    elif t == CFULL:
                        put_keys(b, 3)

            def put_keys(b, c):
                lo, hi = CHUNKS[c]
                act.wait_ge(ks_full, b * PER_KS + (c + 1))
                act.activation(k_T[:, lo:hi], ks[c % 3][:, 0:hi - lo], ACT.Copy).then_inc(ks_out, 1)

            def put_scores(b, par):
                for n in range(8):
                    r, c = n // 4, n % 4
                    lo, hi = CHUNKS[c]
                    act.wait_ge(ks_full, b * PER_KS + (4 + n + 1))
                    act.activation(scores[:, 2 * par + r, lo:hi], ks[(4 + n) % 3][:, 0:hi - lo],
                                   ACT.Copy).then_inc(ks_out, 1)

            def exponentials(b, par, r):
                i = 2 * par + r
                act.wait_ge(picked, b * 2 + (r + 1))
                restart(act, act_own)
                act.activation(neg_top[:, i:i + 1], best[:, i, 0:1], ACT.Copy, scale=-SCALE).then_inc(act_own, 1)
                act.wait_ge(act_own, 1)
                top = neg_top[:, i:i + 1]
                act.activation(best_exp[:], best[:, i, :], ACT.Exp, bias=top, scale=SCALE,
                               accum_out=total[:, i:i + 1]).then_inc(act_own, 1)
                act.activation(scores[:, i, :], scores[:, i, :], ACT.Exp, bias=top, scale=SCALE).then_inc(act_own, 1)
                act.activation(left[:, r, :], left[:, r, :], ACT.Exp, bias=top, scale=SCALE).then_inc(act_own, 1)
                act.wait_ge(act_own, 4)
                act.sem_inc(exped, 1)

            def step(b, par, turn, last):
                if not last:
                    put_context(b + 2, range(0, 3))
                exponentials(b, par, 1)
                if not last:
                    put_context(b + 2, range(3, CT))
                for j in range(2):
                    act.wait_ge(mean_full, b * 2 + (j + 1) + FIRST)
                    if j == 0:
                        act.activation(mean_T[:, 0:8, :], mean[0][:], ACT.Copy).then_inc(mean_out, 1)
                    else:
                        act.activation(mean_T[:, 8:CFULL, :], mean[1][:, 0:CFULL - 8, :],
                                       ACT.Copy).then_inc(mean_out, 1)
                        act.activation(mean_T[0:CLAST, CFULL, :], mean[1][0:CLAST, CFULL - 8, :],
                                       ACT.Copy).then_inc(mean_out, 1)
                if not (isinstance(b, int) and b == NB - 1):
                    exponentials(b + 1, (par + 1) % BUFS, 0)
                act.wait_ge(mix_full, b + 1)
                act.activation(c_T[:, :, bass.ds(b * SEQ, SEQ)], mix[:], ACT.Copy).then_inc(mix_out, 1)
                if not last:
                    put_scores(b + 2, (par + 2) % BUFS)

            for b in range(2):
                put_context(b, range(CT))
                put_scores(b, b)
            exponentials(0, 0, 0)
            in_turn(act, step)

        @block.tensor
        def _(pe):
            for signal in (mean_full,):
                pe.sem_inc(signal, FIRST)
            pe.wait_ge(norm.normed, NT)
            for t in range(NT):
                if t >= 2:
                    pe.wait_ge(ring_out, t - 1)
                for k in range(KD):
                    last = pe.transpose(ring[t % 2][:, k, :], g.hn[:, t, k * P:(k + 1) * P], g.ident[:])
                last.then_inc(ring_full, 1)
            pe.wait_ge(ring_out, NT)
            pe.wait_ge(w_in, 32)
            for k in range(KD):
                last = pe.matmul(ks[0][:], wq[:, k, :], g.hT[:, k, :], start=(k == 0), stop=(k == KD - 1))
            last.then_inc(q_full, 1)
            pe.wait_ge(q_out, 1)
            pe.wait_ge(pool_own, 3)

            def turn_context(b, par, turn):
                pe.wait_ge(ctx_in[par], turn * LOADED + LOADED)
                for t in range(CT):
                    m = size(t)
                    pe.wait_ge(ring_out, b * CT + (max(t - 1, 0) + NT))
                    for k in range(KC):
                        last = pe.transpose(ring[t % 2][:, k, 0:m],
                                            context[0:m, par, t, k * P:(k + 1) * P], g.ident[0:m, 0:m])
                    last.then_inc(ring_full, 1)
                    if t % 4 == 0 and t:
                        keys(b, t // 4 - 1)
                keys(b, 3)

            def score(b):
                pe.wait_ge(side_ready, b * 5 + 5)
                for n in range(8):
                    r, c = n // 4, n % 4
                    lo, hi = CHUNKS[c]
                    if n == 0:
                        pe.wait_ge(ks_out, b * PER_KS + (4 + 3))
                    pe.wait_ge(ks_out, b * PER_KS + (4 + n + 1))
                    out = ks[(4 + n) % 3][:, 0:hi - lo]
                    pe.matmul(out, q_diag[:, r, :], k_T[:, lo:hi], start=True, stop=False)
                    pe.matmul(out, ones[:], mask[:, lo:hi], start=False, stop=True).then_inc(ks_full, 1)

            def keys(b, c):
                lo, hi = CHUNKS[c]
                pe.wait_ge(ring_out, b * CT + (min(4 * c + 4, CT) + NT))
                pe.wait_ge(ks_out, b * PER_KS + (c + 1))
                for k in range(KC):
                    last = pe.matmul(ks[c % 3][:, 0:hi - lo], wk[:, k, :], context_T[:, c % 2, k, 0:hi - lo], start=(k == 0),
                                     stop=(k == KC - 1))
                last.then_inc(ks_full, 1)

            def step(b, par, turn, last):
                if not last:
                    turn_context(b + 2, (par + 2) % BUFS, turn + (par + 2) // BUFS)
                pe.wait_ge(share_ready, b * 2 + 2)
                pe.wait_ge(probs_ready, b * 2 + 2)
                pe.wait_ge(mean_out, b * 3 + FIRST)
                for t in range(CT):
                    m = size(t)
                    for r in range(2):
                        ins = pe.matmul(mean[t // 8][0:m, t % 8, :], scores[:, 2 * par + r, t * P:t * P + m],
                                        share[:, r, :], start=(r == 0), stop=(r == 1))
                    if t in (7, CFULL):
                        ins.then_inc(mean_full, 1)
                pe.wait_ge(mean_out, b * 3 + 3 + FIRST)
                pe.wait_ge(mix_out, b + FIRST)
                for f in range(KC):
                    for t in range(CT):
                        m = size(t)
                        ins = pe.matmul(mix[:, f, :], context[0:m, par, t, f * P:(f + 1) * P], mean_T[0:m, t, :],
                                        start=(t == 0), stop=(t == CT - 1))
                ins.then_inc(mix_full, 1)
                if not last:
                    score(b + 2)

            for b in range(2):
                turn_context(b, b, 0)
                score(b)
            in_turn(pe, step)


def film_and_mlp(g, c_T):
    nc, d = g.nc, g.dram
    F = 2048
    FC = F // P
    with Stage(nc, "d3") as s:
        w_v = s.sb("w_v", [P, KC, D])
        w_in_film = s.sb("w_in_film", [P, KD, 2 * D])
        w_out_film = s.sb("w_out_film", [P, KD, 2 * D])
        w_wide = s.sb("w_wide", [P, KD, F])
        w_down0 = s.sb("w_down0", [P, KD, D])
        halves = [w[:, 2 * i:2 * i + 2, :].rearrange("p a (c n) -> p (a c) n", c=2)
                  for w in (w_in_film, w_out_film) for i in range(2)]
        w_down = [w_down0[:]] + halves[0:3]
        vecs = {n: s.sb(f"v_{n}", [P, k]) for n, k in (("g_norm_in", KD), ("b_norm_in", KD), ("g_ffn", KD),
                                                       ("b_ffn", KD), ("b_film_in", 2 * KD), ("b_film_out", 2 * KD),
                                                       ("b1", FC), ("mod_gate", 1))}
        long = {n: s.sb(f"r_{n}", [P, D]) for n in ("b2", "g_norm_out", "b_norm_out")}
        mask8 = s.sb("mask8", [P, TOK], U8)
        value_T = s.sb("value_T", [P, KD, TOK])
        film = s.sb("film", [P, 2, 2, TOK])
        xin = s.sb("xin", [P, KD, TOK])
        conv = s.sb("conv", [P, KD, TOK])
        hidden = s.sb("hidden", [P, FC, TOK])
        xt = s.sb("xt", [P, NT, D])
        diag = s.sb("diag", [P, 4, P])
        norm = Norm(s)
        ring = [s.ps(f"ring{i}", [P, TOK]) for i in range(4)]
        y = [s.ps(f"y{i}", [P, D]) for i in range(NT)]
        v_in, long_in = s.sem("v_in"), s.sem("long_in")
        down_in = [s.sem(f"down_in{q}") for q in range(4)]
        w_v_in, w_film_in, w_in = s.sem("w_v_in"), s.sem("w_film_in"), s.sem("w_in")
        own_dve = s.sem("own_dve")
        masked, gates_ready = s.sem("masked"), s.sem("gates_ready")
        ring_full, ring_out = s.sem("ring_full"), s.sem("ring_out")
        film_used, turned_full, turned_out = s.sem("film_used"), s.sem("turned_full"), s.sem("turned_out")
        diag_ready, diag_used = s.sem("diag_ready"), s.sem("diag_used")
        conv_done, y_full, normed_T = s.sem("conv_done"), s.sem("y_full"), s.sem("normed_T")
        block = s.block()
        BY_TENSOR = KD // 2
        R_IN = KD
        R_OUT = R_IN + 2 * KD
        R_WIDE = R_OUT + 2 * KD
        V_IN = 16 * (len(vecs) + 1)

        @block.sync
        def _(sp):
            sp.dma_start(mask8[:], rows(d["mask_text"])).then_inc(v_in, 16)
            for n, t in vecs.items():
                src = rows(d[f"L1_xattn_{n}"]) if n == "mod_gate" else d[f"L1_xattn_{n}"]
                sp.dma_start(t[:], src).then_inc(v_in, 16)
            sp.dma_start(w_v[:], d["L1_xattn_Wv"]).then_inc(w_v_in, 16)
            sp.dma_start(w_in_film[:], d["L1_xattn_W_film_in"]).then_inc(w_film_in, 16)
            sp.dma_start(w_out_film[:], d["L1_xattn_W_film_out"]).then_inc(w_film_in, 16)
            sp.dma_start(w_wide[:], d["L1_xattn_W1"]).then_inc(w_in, 16)
            for n, t in long.items():
                sp.dma_start(t[:], rows(d[f"L1_xattn_{n}"])).then_inc(long_in, 16)
            for q in range(4):
                if q in (1, 3):
                    sp.wait_ge(ring_full, R_IN + 2 * KD if q == 1 else R_WIDE)
                sp.dma_start(w_down[q], d["L1_xattn_W2"][:, q * KD:(q + 1) * KD, :]).then_inc(down_in[q], 16)

        @block.vector
        def _(dve):
            own = Steps(dve, own_dve)
            dve.wait_ge(v_in, V_IN)
            for k in range(KC):
                dve.tensor_tensor(c_T[:, k, :], c_T[:, k, :], mask8[:], ALU.mult).then_inc(masked, 1)
            for n in ("b_film_in", "b_film_out"):
                t = vecs[n]
                own.did(dve.tensor_scalar(t[:], t[:], vecs["mod_gate"][:, 0:1], None, ALU.mult))
                own.wait()
                dve.tensor_scalar(t[:, 0:KD], t[:, 0:KD], 1.0, None, ALU.add).then_inc(gates_ready, 1)
            norm.on_vector(dve, g.hn, xt)
            for t in range(NT):
                dve.wait_ge(turned_full, t + 1)
                for k in range(KD):
                    last = dve.tensor_scalar(xin[:, k, t * P:(t + 1) * P], y[t][:, k * P:(k + 1) * P],
                                             vecs["g_norm_in"][:, k:k + 1], vecs["b_norm_in"][:, k:k + 1],
                                             ALU.mult, ALU.add)
                last.then_inc(turned_out, 1)
            dve.wait_ge(turned_out, NT)

            def modulate(t, n):
                dve.wait_ge(ring_out, R_IN + 2 * n + 2)
                own.did(dve.tensor_tensor(t, t, film[:, n % 2, 0, :], ALU.mult))
                own.wait()
                dve.tensor_tensor(t, t, film[:, n % 2, 1, :], ALU.add).then_inc(film_used, 1)
                dve.wait_ge(film_used, n + 1)

            def convolve(k):
                out = conv[:, k, :].rearrange("p (b s) -> p b s", b=NB)
                src = xin[:, k, :].rearrange("p (b s) -> p b s", b=NB)
                own.did(dve.tensor_scalar(conv[:, k, :], xin[:, k, :], g.kern[:, k, 0:1], None, ALU.mult))
                for l in range(1, SEQ):
                    own.wait()
                    own.did(dve.scalar_tensor_tensor(out=out[:, :, l:SEQ], in0=src[:, :, 0:SEQ - l],
                                                     scalar=g.kern[:, k, l:l + 1], in1=out[:, :, l:SEQ],
                                                     op0=ALU.mult, op1=ALU.add))
                own.wait()

            for k in range(KD):
                modulate(xin[:, k, :], k)
            for k in range(KD):
                if k >= BY_TENSOR:
                    dve.wait_ge(diag_used, SEQ * (k - BY_TENSOR + 1))
                    own.did(dve.tensor_copy(conv[:, k, :], y[k][:]))
                    own.wait()
                else:
                    convolve(k)
                modulate(conv[:, k, :], KD + k)
                dve.tensor_tensor(conv[:, k, :], conv[:, k, :], g.hT[:, k, :], ALU.add).then_inc(conv_done, 1)
            for t in range(NT):
                dve.wait_ge(turned_full, NT + t + 1)
                own.did(dve.tensor_copy(xt[:, t, :], y[t][:]))
            own.wait()
            norm.on_vector(dve, xt, g.hn, 1)
            for t in range(NT):
                dve.wait_ge(turned_full, 2 * NT + t + 1)
                for k in range(KD):
                    last = dve.tensor_scalar(xin[:, k, t * P:(t + 1) * P], y[t][:, k * P:(k + 1) * P],
                                             vecs["g_ffn"][:, k:k + 1], vecs["b_ffn"][:, k:k + 1],
                                             ALU.mult, ALU.add)
                last.then_inc(normed_T, 1)
            dve.wait_ge(long_in, 16 * len(long))
            for t in range(NT):
                own.did(dve.tensor_tensor(xt[:, t, :], xt[:, t, :], long["b2"][:], ALU.add))
            own.wait()
            dve.wait_ge(y_full, 4)
            for t in range(NT):
                own.did(dve.tensor_tensor(xt[:, t, :], xt[:, t, :], y[t][:], ALU.add))
            own.wait()
            norm.on_vector(dve, xt, g.hn, 2)
            for t in range(NT):
                own.did(dve.tensor_tensor(g.hn[:, t, :], g.hn[:, t, :], long["g_norm_out"][:], ALU.mult))
                own.did(dve.tensor_tensor(g.x[:, t, :], g.x[:, t, :], long["b_norm_out"][:], ALU.add))
            own.wait()
            for t in range(NT):
                own.did(dve.tensor_tensor(g.x[:, t, :], g.x[:, t, :], g.hn[:, t, :], ALU.add))

        @block.scalar
        def _(act):
            norm.on_scalar(act, g.eps[:])
            for m in range(KD):
                act.wait_ge(ring_full, m + 1)
                act.activation(value_T[:, m, :], ring[m % 4][:], ACT.Copy).then_inc(ring_out, 1)
            act.wait_ge(gates_ready, 2)
            for n in range(2 * KD):
                bias = vecs["b_film_in" if n < KD else "b_film_out"]
                if n == KD + BY_TENSOR:
                    for i in range((KD - BY_TENSOR) * SEQ):
                        k, l = BY_TENSOR + i // SEQ, i % SEQ
                        if i >= 4:
                            act.wait_ge(diag_used, i - 3)
                        act.activation(diag[:, i % 4, :], g.ident[:], ACT.Copy,
                                       scale=g.kern[:, k, l:l + 1]).then_inc(diag_ready, 1)
                if n >= 2:
                    act.wait_ge(film_used, n - 1)
                for j in range(2):
                    u = R_IN + 2 * n + j
                    act.wait_ge(ring_full, u + 1)
                    act.activation(film[:, n % 2, j, :], ring[u % 4][:], ACT.Identity,
                                   bias=bias[:, j * KD + n % KD:j * KD + n % KD + 1],
                                   scale=vecs["mod_gate"][:, 0:1]).then_inc(ring_out, 1)
            norm.on_scalar(act, g.eps[:], 1)
            for m in range(FC):
                u = R_WIDE + m
                act.wait_ge(ring_full, u + 1)
                act.activation(hidden[:, m, :], ring[u % 4][:], ACT.Gelu,
                               bias=vecs["b1"][:, m:m + 1]).then_inc(ring_out, 1)
            norm.on_scalar(act, g.eps[:], 2)

        @block.tensor
        def _(pe):
            pe.wait_ge(w_v_in, 16)
            pe.wait_ge(masked, KC)
            for m in range(KD):
                for k in range(KC):
                    last = pe.matmul(ring[m % 4][:], w_v[:, k, m * P:(m + 1) * P], c_T[:, k, :], start=(k == 0),
                                     stop=(k == KC - 1))
                last.then_inc(ring_full, 1)
            pe.wait_ge(norm.normed, NT)
            for t in range(NT):
                for k in range(KD):
                    last = pe.transpose(y[t][:, k * P:(k + 1) * P], xt[:, t, k * P:(k + 1) * P], g.ident[:])
                last.then_inc(turned_full, 1)
            pe.wait_ge(ring_out, KD)
            pe.wait_ge(w_film_in, 32)
            for n in range(2 * KD):
                w = w_in_film if n < KD else w_out_film
                if n == KD + BY_TENSOR:
                    pe.wait_ge(film_used, KD)
                    pe.wait_ge(turned_out, NT)
                    for i in range((KD - BY_TENSOR) * SEQ):
                        k, l = BY_TENSOR + i // SEQ, i % SEQ
                        out = y[k][:].rearrange("p (b s) -> p b s", b=NB)
                        src = xin[:, k, :].rearrange("p (b s) -> p b s", b=NB)
                        pe.wait_ge(diag_ready, i + 1)
                        pe.matmul(out[:, :, l:SEQ], diag[:, i % 4, :], src[:, :, 0:SEQ - l], start=(l == 0),
                                  stop=(l == SEQ - 1), skip_group_check=True).then_inc(diag_used, 1)
                for j in range(2):
                    u = R_IN + 2 * n + j
                    pe.wait_ge(ring_out, max(u - 3, KD))
                    m = j * KD + n % KD
                    for k in range(KD):
                        last = pe.matmul(ring[u % 4][:], w[:, k, m * P:(m + 1) * P], value_T[:, k, :],
                                         start=(k == 0), stop=(k == KD - 1))
                    last.then_inc(ring_full, 1)
            pe.wait_ge(conv_done, KD)
            for t in range(NT):
                for k in range(KD):
                    last = pe.transpose(y[t][:, k * P:(k + 1) * P], conv[:, k, t * P:(t + 1) * P], g.ident[:])
                last.then_inc(turned_full, 1)
            pe.wait_ge(norm.normed, 2 * NT)
            for t in range(NT):
                for k in range(KD):
                    last = pe.transpose(y[t][:, k * P:(k + 1) * P], g.hn[:, t, k * P:(k + 1) * P], g.ident[:])
                last.then_inc(turned_full, 1)
            pe.wait_ge(normed_T, NT)
            pe.wait_ge(w_in, 16)
            for m in range(FC):
                u = R_WIDE + m
                pe.wait_ge(ring_out, u - 3)
                for k in range(KD):
                    last = pe.matmul(ring[u % 4][:], w_wide[:, k, m * P:(m + 1) * P], xin[:, k, :],
                                     start=(k == 0), stop=(k == KD - 1))
                last.then_inc(ring_full, 1)
            for q in range(4):
                pe.wait_ge(down_in[q], 16)
                pe.wait_ge(ring_out, R_WIDE + (q + 1) * KD)
                for t in range(NT):
                    for k in range(KD):
                        m = q * KD + k
                        last = pe.matmul(y[t][:], hidden[:, m, t * P:(t + 1) * P], w_down[q][:, k, :],
                                         start=(m == 0), stop=(m == FC - 1))
                last.then_inc(y_full, 1)


def state_space_alone(g):
    with Stage(g.nc, "y") as s:
        ss = StateSpace(s, g)
        block = s.block()

        @block.sync
        def _(sp):
            ss.on_sync(sp)

        @block.scalar
        def _(act):
            ss.steps_on_scalar(act)
            ss.waves_on_scalar(act)

        @block.vector
        def _(dve):
            ss.on_vector(dve)

        @block.gpsimd
        def _(pool):
            ss.on_gpsimd(pool)


def write_out(g):
    nc = g.nc
    with Stage(nc, "z") as s:
        stored = s.sem("stored")
        block = s.block()

        @block.sync
        def _(sp):
            sp.dma_start(tokens(g.out), g.x[:]).then_inc(stored, 16)
            sp.wait_ge(stored, 16)


def load_x(g):
    nc = g.nc
    with Stage(nc, "i") as s:
        loaded, cleared, made = s.sem("loaded"), s.sem("cleared"), s.sem("made")
        block = s.block()

        @block.sync
        def _(sp):
            sp.dma_start(g.x[:], tokens(g.dram["x"])).then_inc(loaded, 16)
            sp.wait_ge(loaded, 16)

        @block.gpsimd
        def _(pool):
            pool.memset(g.eps[:], EPS).then_inc(cleared, 1)
            pool.wait_ge(cleared, 1)
            pool.memset(g.zero[:], 0.0).then_inc(cleared, 1)
            pool.wait_ge(cleared, 2)
            pool.memset(g.ident[:], 0.0).then_inc(cleared, 1)
            pool.wait_ge(cleared, 3)
            pool.affine_select(out=g.ident[:], in_=g.ident[:], compare_op=ALU.not_equal, fill=1.0, base=0,
                               pattern=[[-1, P]], channel_multiplier=1).then_inc(made, 1)
            pool.wait_ge(made, 1)


def build(nc, dram, out, stages=range(6)):
    with ExitStack() as ctx:
        g = Core(nc, ctx, dram, out, None)
        load_x(g)
        if 0 in stages:
            g.mixed_dram = nc.dram_tensor("mixed_context", [P, KC, 8, TOK], F32, kind="Internal").ap()
            with Stage(nc, "a") as s:
                q_T = s.sb("q_T", [P, 4, TOK])
                kl_T = s.sb("kl_T", [P, 4, TOK])
                latent_probs = s.sb("latent_probs", [SEQ, NB, D])
                xattn0_queries(g, q_T, kl_T)
                xattn0_context(g, q_T, kl_T, latent_probs)
                xattn0_output(g, latent_probs)
        if 1 in stages:
            causal_attention(g, "b", "L0_attn_qk", 4, False, "L0_attn_v", D, "L0_attn_out_w", "L0_attn_b",
                             1.0 / float(np.sqrt(32.0)))
        if 2 in stages:
            shared_and_routed_experts(g)
        if 3 in stages:
            if 2 not in stages:
                state_space_alone(g)
            with Stage(nc, "d") as s:
                c_T = s.sb("c_T", [P, KC, TOK])
                xattn1_context(g, c_T)
                film_and_mlp(g, c_T)
        if 4 in stages:
            causal_attention(g, "e", "L1_attn_qk", 1, True, "L1_attn_wv", 32, "L1_attn_wo", None,
                             1.0 / float(np.sqrt(32.0)))
        if 5 in stages:
            capacity_experts(g)
        write_out(g)


def lay(w):
    k, n = w.shape
    return np.ascontiguousarray(w.reshape(k // P, P, n).transpose(1, 0, 2))


def layout(inputs):
    a = {k: np.asarray(v) for k, v in inputs.items()}
    o = {}
    o["x"] = a["x"]
    o["ctx"] = a["ctx_768"]
    o["mask_ctx0"] = a["mask_BxS2_bk0"]
    o["L0_xattn_Wq"] = lay(a["L0_xattn_Wq"].T)
    o["L0_xattn_Wk"] = lay(a["L0_xattn_Wkv"][:D].T)
    o["L0_xattn_Wv"] = lay(a["L0_xattn_Wkv"][D:].T)
    o["L0_xattn_Wlk"] = lay(a["L0_xattn_Wlkv"][:D].T)
    o["L0_xattn_Wlv"] = lay(a["L0_xattn_Wlkv"][D:].T)
    o["L0_xattn_Wo"] = lay(a["L0_xattn_Wo"].T)
    for n in ("L0_xattn_ln_l_g", "L0_xattn_ln_l_b"):
        o[n] = np.ascontiguousarray(a[n].reshape(KD, P).T)
    for n in ("L0_xattn_qn_g", "L0_xattn_kn_g", "L0_xattn_ln_x_g", "L0_xattn_ln_x_b", "L0_xattn_bo"):
        o[n] = a[n]
    qkv = a["L0_attn_qkv_w"]
    o["L0_attn_qk"] = lay(qkv[:, :2 * D])
    o["L0_attn_v"] = lay(qkv[:, 2 * D:])
    o["L0_attn_out_w"] = lay(a["L0_attn_out_w"])
    o["L0_attn_b_qk"] = np.ascontiguousarray(a["L0_attn_qkv_b"][:2 * D].reshape(8, P).T)
    o["L0_attn_b_v"] = a["L0_attn_qkv_b"][2 * D:]
    o["L0_attn_b_o"] = a["L0_attn_out_b"]
    gate, up, down = (np.concatenate([a[f"L0_ffn_{n}_s"][None], a[f"L0_ffn_{n}"]]) for n in ("Wg", "Wu", "Wd"))
    o["L0_ffn_W"] = np.ascontiguousarray(np.stack(
        [w.reshape(E_N + 1, 8, P, KD, P).transpose(0, 1, 4, 3, 2).reshape(E_N + 1, 8, P, D) for w in (gate, up)]
        + [down.transpose(0, 2, 1).reshape(E_N + 1, 8, P, D)], axis=3))
    o["L0_ffn_Wr"] = lay(a["L0_ffn_Wr"].T)
    o["L0_ffn_rb"] = a["L0_ffn_rb"]
    o["mask_ctx1"] = a["mask_BxS2_bf1"]
    o["mask_text"] = a["mask_BxS_bf1"].reshape(-1)
    for n in ("Wq", "Wk", "Wv", "W_film_in", "W_film_out", "W1", "W2"):
        o[f"L1_xattn_{n}"] = lay(a[f"L1_xattn_{n}"])
    for n in ("g_norm_in", "b_norm_in", "g_ffn", "b_ffn", "b_film_in", "b_film_out", "b1", "log_dt", "D_skip"):
        o[f"L1_xattn_{n}"] = np.ascontiguousarray(a[f"L1_xattn_{n}"].reshape(-1, P).T)
    for n in ("A_re", "A_im", "C_re", "C_im"):
        o[f"L1_xattn_{n}"] = lay(a[f"L1_xattn_{n}"])
    for n in ("b2", "g_norm_out", "b_norm_out"):
        o[f"L1_xattn_{n}"] = a[f"L1_xattn_{n}"]
    o["L1_xattn_mod_gate"] = a["L1_xattn_mod_gate"].reshape(1)
    o["L1_ffn_Wr"] = lay(a["L1_ffn_Wr"])
    o["L1_ffn_W1"] = np.stack([lay(m) for m in a["L1_ffn_W1"]])
    o["L1_ffn_W2"] = np.stack([lay(m) for m in a["L1_ffn_W2"]])
    o["slots"] = np.arange(160, dtype=np.float32)
    o["before"] = (np.arange(E_N)[None, :] < np.arange(E_N)[:, None]).astype(np.float32).reshape(-1)
    even_odd = np.concatenate([np.arange(0, 32, 2), np.arange(1, 32, 2)])
    odd_even = np.concatenate([np.arange(1, 32, 2), np.arange(0, 32, 2)])
    wq, wk = a["L1_attn_wq"].T.reshape(D, 16, 32), a["L1_attn_wk"]
    cols = []
    for order in (even_odd, odd_even):
        cols += [wq[:, :, order].reshape(D, D)] + [wk[:, order]] * 4
    o["L1_attn_qk"] = lay(np.concatenate(cols, axis=1))
    o["L1_attn_wv"] = lay(a["L1_attn_wv"])
    o["L1_attn_wo"] = lay(a["L1_attn_wo"].T)
    freqs = (np.float32(1.0) / np.float32(1000.0) ** (np.arange(0, 32, 2, dtype=np.float32) / np.float32(32)))
    ang = np.arange(SEQ, dtype=np.float32)[:, None] * freqs[None, :].astype(np.float32)
    cos, sin = np.cos(ang).T, np.sin(ang).T
    o["rope_cos"] = np.ascontiguousarray(np.tile(np.concatenate([cos, cos]), (4, NB)))
    o["rope_sin"] = np.ascontiguousarray(np.tile(np.concatenate([-sin, sin]), (4, NB)))
    return o


def kernel(**inputs):
    import concourse.bacc as bacc
    from concourse.bass_utils import run_bass_kernel_spmd

    nc = bacc.Bacc("TRN2", target_bir_lowering=False, num_devices=1)
    arrays = layout(inputs)
    dram = {n: nc.dram_tensor(f"in_{n}", v.shape, mybir.dt.from_np(v.dtype), kind="ExternalInput").ap()
            for n, v in arrays.items()}
    out = nc.dram_tensor("out", [NB, SEQ, D], F32, kind="ExternalOutput").ap()
    build(nc, dram, out)
    r = run_bass_kernel_spmd(nc, [{f"in_{n}": v for n, v in arrays.items()}], core_ids=[0])
    return r.results[0]["out"]
```
